# Optimizing a Trainium2 kernel written in Bass

```python
import numpy as np
import jax
import jax.numpy as jnp

def _softmax(x, axis=-1):
    return jax.nn.softmax(x, axis=axis)

def _gelu(x):
    return jax.nn.gelu(x, approximate=True)

def _silu(x):
    return jax.nn.silu(x)

def _sigmoid(x):
    return jax.nn.sigmoid(x)

def _layernorm(x, axis=-1, eps=1e-05):
    m = jnp.mean(x, axis=axis, keepdims=True)
    v = jnp.var(x, axis=axis, keepdims=True)
    return (x - m) / jnp.sqrt(v + eps)

def _scatter_add(tgt, idx, src, axis=0):
    return tgt.at[idx].add(src)

def _segment_sum(src, seg, n):
    return jax.ops.segment_sum(src, seg, n)
kernel_name = 'mk_adj_resnorm_d4_adj_r2_a67864'

def setup_inputs(seed: int=0):
    np.random.seed(seed)
    _w = jnp.asarray

    def _rec_inputs():
        import jax
        import jax.numpy as jnp
        _gk = jax.random.key(seed)
        x = 7.22e-05 + 1 * jax.random.normal(jax.random.fold_in(_gk, 1), (8, 1024, 256), jnp.float32)
        _a = jax.random.bernoulli(jax.random.fold_in(_gk, 2), 0.00195312, (8, 1024, 1024))
        adj = _a.astype(jnp.int32)
        return (x, adj)
    x, adj = _rec_inputs()

    def _L0_gnn_setup():
        import jax, jax.numpy as jnp
        import numpy as np
        ALPHA = 0.2
        MASK_VAL = -1000000000.0
        key = jax.random.key(seed)
        k1, k2, k3, k4 = jax.random.split(key, 4)
        B, N, F_in, F_out = (8, 1024, 256, 256)
        h = jax.random.normal(k1, (B, N, F_in), dtype=jnp.float32)
        adj = jax.random.randint(k2, (B, N, N), 0, 2, dtype=jnp.int32)

        def xavier(k, shape, gain=1.414):
            fan_in, fan_out = (shape[0], shape[1])
            bound = gain * np.sqrt(6.0 / (fan_in + fan_out))
            return jax.random.uniform(k, shape, jnp.float32, -bound, bound)
        W = xavier(k3, (F_in, F_out))
        a = xavier(k4, (2 * F_out, 1))
        return {'h': h, 'adj': adj, 'W': W, 'a': a}
    _L0_gnn_all = _L0_gnn_setup()
    _L0_gnn_in = {k: v for k, v in _L0_gnn_all.items() if k in ('W', 'a')}
    del _L0_gnn_all

    def _L1_gnn_setup():
        import jax, jax.numpy as jnp
        import numpy as np
        L = 3
        D = 256
        B, N = (8, 512)
        EPS = 1e-05

        def layernorm(x, gamma, beta):
            mu = jnp.mean(x, axis=-1, keepdims=True)
            var = jnp.var(x, axis=-1, keepdims=True)
            return (x - mu) * jax.lax.rsqrt(var + EPS) * gamma + beta
        key = jax.random.key(seed)
        ks = jax.random.split(key, 12)
        s = 1.0 / np.sqrt(D)
        node_features = jax.random.normal(ks[0], (B, N, D), dtype=jnp.float32)
        adjacency_matrix = jax.random.randint(ks[1], (B, N, N), 0, 2, dtype=jnp.int32)
        return {'node_features': node_features, 'adjacency_matrix': adjacency_matrix, 'attn_w': jax.random.normal(ks[2], (L, 2 * D), dtype=jnp.float32) * (1.0 / np.sqrt(2 * D)), 'attn_b': jax.random.normal(ks[3], (L,), dtype=jnp.float32) * 0.01, 'W1': jax.random.normal(ks[4], (L, D, 4 * D), dtype=jnp.float32) * s, 'b1': jnp.zeros((L, 4 * D), dtype=jnp.float32), 'W2': jax.random.normal(ks[5], (L, 4 * D, D), dtype=jnp.float32) * (1.0 / np.sqrt(4 * D)), 'b2': jnp.zeros((L, D), dtype=jnp.float32), 'g1': jnp.ones((L, D), dtype=jnp.float32), 'beta1': jnp.zeros((L, D), dtype=jnp.float32), 'g2': jnp.ones((L, D), dtype=jnp.float32), 'beta2': jnp.zeros((L, D), dtype=jnp.float32)}
    _L1_gnn_all = _L1_gnn_setup()
    _L1_gnn_in = {k: v for k, v in _L1_gnn_all.items() if k in ('attn_w', 'attn_b', 'W1', 'b1', 'W2', 'b2', 'g1', 'beta1', 'g2', 'beta2')}
    del _L1_gnn_all

    def _L2_gnn_setup():
        import jax, jax.numpy as jnp
        import numpy as np
        ALPHA = 0.2
        NEG_INF = -1000000000.0
        key = jax.random.key(seed)
        k1, k2, k3, k4 = jax.random.split(key, 4)
        B, N, IN, OUT = (8, 1024, 256, 32)
        graph_input = jax.random.normal(k1, (B, N, IN), dtype=jnp.float32)
        adj = jax.random.randint(k2, (B, N, N), 0, 2, dtype=jnp.int32)
        W_fc = jax.random.normal(k3, (OUT, IN), dtype=jnp.float32) * (1.0 / np.sqrt(IN))
        W_attn = jax.random.normal(k4, (1, 2 * OUT), dtype=jnp.float32) * (1.0 / np.sqrt(2 * OUT))
        return {'graph_input': graph_input, 'adj': adj, 'W_fc': W_fc, 'W_attn': W_attn}
    _L2_gnn_all = _L2_gnn_setup()
    _L2_gnn_in = {k: v for k, v in _L2_gnn_all.items() if k in ('W_fc', 'W_attn')}
    del _L2_gnn_all

    def _L3_gnn_setup():
        import jax, jax.numpy as jnp
        import numpy as np
        ALPHA = 0.2

        def _leaky(x):
            return jnp.where(x >= 0, x, ALPHA * x)
        key = jax.random.key(seed)
        k1, k2, k3, k4 = jax.random.split(key, 4)
        B, N, F_in, F_out = (4, 1024, 256, 256)
        h = jax.random.normal(k1, (B, N, F_in), dtype=jnp.float32)
        W = jax.random.normal(k2, (F_in, F_out), dtype=jnp.float32) * 0.05
        a = jax.random.normal(k3, (2 * F_out, 1), dtype=jnp.float32) * 0.05
        adj = jax.random.randint(k4, (B, N, N), 0, 2, dtype=jnp.int32)
        return {'h': h, 'W': W, 'a': a, 'adj': adj}
    _L3_gnn_all = _L3_gnn_setup()
    _L3_gnn_in = {k: v for k, v in _L3_gnn_all.items() if k in ('W', 'a')}
    del _L3_gnn_all
    return {'x': x, 'adj': adj, 'L0_gnn_W': _L0_gnn_in['W'], 'L0_gnn_a': _L0_gnn_in['a'], 'L1_gnn_attn_w': _L1_gnn_in['attn_w'], 'L1_gnn_attn_b': _L1_gnn_in['attn_b'], 'L1_gnn_W1': _L1_gnn_in['W1'], 'L1_gnn_b1': _L1_gnn_in['b1'], 'L1_gnn_W2': _L1_gnn_in['W2'], 'L1_gnn_b2': _L1_gnn_in['b2'], 'L1_gnn_g1': _L1_gnn_in['g1'], 'L1_gnn_beta1': _L1_gnn_in['beta1'], 'L1_gnn_g2': _L1_gnn_in['g2'], 'L1_gnn_beta2': _L1_gnn_in['beta2'], 'L2_gnn_W_fc': _L2_gnn_in['W_fc'], 'L2_gnn_W_attn': _L2_gnn_in['W_attn'], 'L3_gnn_W': _L3_gnn_in['W'], 'L3_gnn_a': _L3_gnn_in['a']}

def reference(x, adj, L0_gnn_W, L0_gnn_a, L1_gnn_attn_w, L1_gnn_attn_b, L1_gnn_W1, L1_gnn_b1, L1_gnn_W2, L1_gnn_b2, L1_gnn_g1, L1_gnn_beta1, L1_gnn_g2, L1_gnn_beta2, L2_gnn_W_fc, L2_gnn_W_attn, L3_gnn_W, L3_gnn_a):
    import jax
    import jax.numpy as jnp

    def _L0_gnn_ref(h, adj, W, a):
        import jax, jax.numpy as jnp
        import numpy as np
        ALPHA = 0.2
        MASK_VAL = -1000000000.0
        Fout = W.shape[1]
        Wh = jnp.matmul(h, W)
        a1 = a[:Fout, 0]
        a2 = a[Fout:, 0]
        e_i = jnp.einsum('bnf,f->bn', Wh, a1)
        e_j = jnp.einsum('bnf,f->bn', Wh, a2)
        e = e_i[:, :, None] + e_j[:, None, :]
        e = jax.nn.leaky_relu(e, negative_slope=ALPHA)
        e = jnp.where(adj == 0, MASK_VAL, e)
        attention = jax.nn.softmax(e, axis=2)
        h_prime = jnp.matmul(attention, Wh)
        return jax.nn.elu(h_prime)

    def _L1_gnn_ref(node_features, adjacency_matrix, attn_w, attn_b, W1, b1, W2, b2, g1, beta1, g2, beta2):
        import jax, jax.numpy as jnp
        import numpy as np
        L = 3
        D = 256
        B, N = (8, 512)
        EPS = 1e-05

        def layernorm(x, gamma, beta):
            mu = jnp.mean(x, axis=-1, keepdims=True)
            var = jnp.var(x, axis=-1, keepdims=True)
            return (x - mu) * jax.lax.rsqrt(var + EPS) * gamma + beta
        n = adjacency_matrix.shape[-1]
        mask = adjacency_matrix.astype(jnp.float32) + jnp.eye(n, dtype=jnp.float32) > 0
        x = node_features
        d = x.shape[-1]
        for l in range(attn_w.shape[0]):
            si = x @ attn_w[l, :d]
            sj = x @ attn_w[l, d:]
            scores = si[:, :, None] + sj[:, None, :] + attn_b[l]
            scores = jnp.where(scores >= 0, scores, 0.2 * scores)
            scores = jnp.where(mask, scores, -jnp.inf)
            attn = jax.nn.softmax(scores, axis=-1)
            agg = jnp.einsum('bij,bjd->bid', attn, x)
            h = layernorm(x + agg, g1[l], beta1[l])
            ff = jax.nn.gelu(h @ W1[l] + b1[l], approximate=False) @ W2[l] + b2[l]
            x = layernorm(h + ff, g2[l], beta2[l])
        return x

    def _L2_gnn_ref(graph_input, adj, W_fc, W_attn):
        import jax, jax.numpy as jnp
        import numpy as np
        ALPHA = 0.2
        NEG_INF = -1000000000.0
        h = jnp.einsum('bni,oi->bno', graph_input, W_fc)
        out_dim = W_fc.shape[0]
        a1 = W_attn[0, :out_dim]
        a2 = W_attn[0, out_dim:]
        f1 = jnp.einsum('bno,o->bn', h, a1)
        f2 = jnp.einsum('bno,o->bn', h, a2)
        scores = jax.nn.leaky_relu(f1[:, :, None] + f2[:, None, :], negative_slope=ALPHA)
        scores = jnp.where(adj == 0, NEG_INF, scores)
        attn = jax.nn.softmax(scores, axis=2)
        h_prime = jnp.einsum('bnm,bmi->bni', attn, graph_input)
        return jax.nn.elu(h_prime)

    def _L3_gnn_ref(h, W, a, adj):
        import jax, jax.numpy as jnp
        import numpy as np
        ALPHA = 0.2

        def _leaky(x):
            return jnp.where(x >= 0, x, ALPHA * x)
        F_out = W.shape[1]
        Wh = jnp.matmul(h, W)
        Wh_sg = jax.lax.stop_gradient(Wh)
        a1 = a[:F_out, 0]
        a2 = a[F_out:, 0]
        s_i = Wh_sg @ a1
        s_j = Wh_sg @ a2
        e = _leaky(s_i[:, :, None] + s_j[:, None, :])
        e = jnp.where(adj > 0, e, jnp.float32(-9000000000000000.0))
        attention = jax.nn.softmax(e, axis=1)
        h_prime = jnp.einsum('bij,bjf->bif', attention, Wh)
        return _leaky(h_prime)
    x = _layernorm(x + _L0_gnn_ref(x, adj, L0_gnn_W, L0_gnn_a), axis=-1)
    x = _layernorm(x + _L1_gnn_ref(x, adj, L1_gnn_attn_w, L1_gnn_attn_b, L1_gnn_W1, L1_gnn_b1, L1_gnn_W2, L1_gnn_b2, L1_gnn_g1, L1_gnn_beta1, L1_gnn_g2, L1_gnn_beta2), axis=-1)
    x = _layernorm(x + _L2_gnn_ref(x, adj, L2_gnn_W_fc, L2_gnn_W_attn), axis=-1)
    x = _layernorm(x + _L3_gnn_ref(x, L3_gnn_W, L3_gnn_a, adj), axis=-1)
    return x

_drawn_inputs = setup_inputs


def setup_inputs(seed=0):
    import zlib

    import numpy as np

    out = dict(_drawn_inputs(seed))
    spreads = {'L1_gnn_b1': (0.0, 0.1),
     'L1_gnn_b2': (0.0, 0.1),
     'L1_gnn_g1': (1.0, 0.2),
     'L1_gnn_beta1': (0.0, 0.1),
     'L1_gnn_g2': (1.0, 0.2),
     'L1_gnn_beta2': (0.0, 0.1)}
    factors = {'L1_gnn_attn_b': 64.0}
    for name, (base, spread) in spreads.items():
        noise = np.random.default_rng([zlib.crc32(name.encode()), seed]).standard_normal(out[name].shape)
        drawn = base * np.exp(spread * noise) if base else spread * noise
        out[name] = jnp.asarray(drawn.astype(out[name].dtype))
    for name, factor in factors.items():
        out[name] = (out[name] * factor).astype(out[name].dtype)
    return out
```

```python
from contextlib import ExitStack

import concourse.bass as bass
from concourse import mybir

ALU = mybir.AluOpType
ACT = mybir.ActivationFunctionType
F32 = mybir.dt.float32
F16 = mybir.dt.float16
BF16 = mybir.dt.bfloat16
I32 = mybir.dt.int32

P = 128
BIG = float(2.0 ** 100)
WSCALE = 64.0
EPS = 1e-5
SLOPE = 0.2
TILES = 16
RING = 4

PASSES = [("att", 0), ("att", 1), ("ffn", 0), ("att", 2), ("ffn", 1), ("att", 3), ("ffn", 2), ("att", 4), ("att", 5)]
ATT_PASS = [q for q, (k, _) in enumerate(PASSES) if k == "att"]
FFN_PASS = [q for q, (k, _) in enumerate(PASSES) if k == "ffn"]
LN_ORDER = [("g0", 0), ("g0", 1)]
for _l in range(3):
    LN_ORDER += [(f"a{_l}", 0), (f"a{_l}", 1)]
    LN_ORDER += [(f"f{_l}", 0)] + ([("g1", 0)] if _l == 2 else []) + [(f"f{_l}", 1)] + ([("g1", 1)] if _l == 2 else [])
LN_ORDER += [("g2", 0), ("g2", 1), ("g3", 0), ("g3", 1)]


def ln_count(name, half):
    return LN_ORDER.index((name, half)) + 1


def build(nc, x, adj, W0, a0, attn_w, attn_b, W1, b1, W2, b2, g1, beta1, g2, beta2, W_fc, W_attn, W3, a3, out):
    B, N, D = x.shape
    NC, DC, HALF = N // P, D // P, N // 2
    HC = NC // 2
    L, H = b1.shape
    KC = H // P
    OUT = W_fc.shape[0]
    R = D + 2
    DG = N + P
    assert (NC, HC * P, KC, TILES) == (8, HALF, 8, 16)

    ctx = ExitStack()
    with ctx:
        def sb(name, shape, dt):
            return ctx.enter_context(nc.sbuf_tensor(name, shape, dt))

        ident_f = sb("ident_f", [P, P], F32)
        ident_b = sb("ident_b", [P, P], BF16)
        diag_neg = sb("diag_neg", [P, P], BF16)
        ones_f = sb("ones_f", [P, P], F32)
        pick_s = sb("pick_s", [6, P], BF16)
        pick_t = sb("pick_t", [6, P], BF16)
        pick_r = sb("pick_r", [4, P], BF16)
        mean_w = sb("mean_w", [P, 4], F16)
        neg_half = sb("neg_half", [P, NC], F32)
        w1h, w1l = sb("w1h", [P, L, DC, H], F16), sb("w1l", [P, L, DC, H], F16)
        w2h, w2l = sb("w2h", [P, L, KC, D], F16), sb("w2l", [P, L, KC, D], F16)
        wgh, wgl = sb("wgh", [P, 2, DC, R], F16), sb("wgl", [P, 2, DC, R], F16)
        b1c = sb("b1c", [P, L, KC], F32)
        sb_v = sb("score_v", [P, L + 1, 2, D], F32)
        ab = sb("attn_bias", [P, L], F32)
        lnc = sb("ln_const", [P, L, 5, D], F32)

        x_cur = sb("x_cur", [P, NC, D], F32)
        x_in = sb("x_in", [P, NC, D], F32)
        h = sb("h", [P, NC, D], F32)
        yTh, yTl = sb("yTh", [P, DC, N], F16), sb("yTl", [P, DC, N], F16)
        rh, rl = sb("rh", [P, NC, R], F16), sb("rl", [P, NC, R], F16)
        mask = sb("mask", [P, NC * DG], BF16)
        maskT = sb("maskT", [P, NC * DG], BF16)
        diag_keep = sb("diag_keep", [P, 2, NC, P], BF16)
        adj_sb = sb("adj_sb", [P, 2, N], I32)
        s8_row = sb("s8_row", [P, N], F32)
        t_row = sb("t_row", [P, N], F32)
        junk = sb("junk", [P, 2, N], BF16)
        xt = sb("xt", [P, 2, HALF], F32)
        p32 = sb("p32", [P, RING, HALF], F32)
        ph, pl = sb("ph", [P, RING, HALF], F16), sb("pl", [P, RING, HALF], F16)
        st = sb("st", [P, 2, NC], F32)
        c2 = sb("c2", [P, 2, NC], F32)
        res = sb("res", [P, 2, NC], F32)
        n8t = sb("n8t", [P, NC], F32)
        sp = sb("sp", [P, NC, 6], BF16)
        spr = sb("spr", [P, NC, 4], BF16)
        rows = sb("rows", [6, N], BF16)
        rowr = sb("rowr", [4, N], BF16)
        col = sb("col", [P, 8, NC], F32)
        resr = sb("resr", [P, NC], F32)
        rinv = sb("rinv", [P, NC], F32)
        csum = sb("csum", [P, NC, 2], F32)
        mnh, mnl = sb("mnh", [4, R], F16), sb("mnl", [4, R], F16)
        bst = sb("bst", [P, HC, 6], F32)
        mv = sb("mv", [P, NC, 2], F32)
        vare = sb("vare", [P, NC], F32)
        rstd = sb("rstd", [P, NC], F32)
        a_col = sb("a_col", [OUT, 2], F32)
        a_mat = sb("a_mat", [OUT, 2, P], F32)
        wfc_sb = sb("wfc_sb", [OUT, D], F32)

        acc = ctx.enter_context(nc.psum_tensor("acc", [P, 4, 512], F32))
        vu = ctx.enter_context(nc.psum_tensor("vu", [P, 2, 512], F32))
        misc = ctx.enter_context(nc.psum_tensor("misc", [P, 2, 512], F32))
        misc_flat = misc[:, :, :].rearrange("p a b -> p (a b)")
        vu_flat = vu[:, :, :].rearrange("p a b -> p (a b)")

        def mrow(m, c, j0, n):
            return m[:, c * N + j0:c * N + j0 + n]

        def diag(m):
            return m[:, :].rearrange("p (c k) -> p c k", k=DG)[:, :, 0:P]

        mask_n = mask[:, 0:NC * N].rearrange("p (c n) -> p c n", c=NC)
        maskT_n = maskT[:, 0:NC * N].rearrange("p (c n) -> p c n", c=NC)
        feat = h[:, :, :].rearrange("p c d -> p (c d)")
        stage = x_in[:, :, :].rearrange("p c d -> p (c d)")

        su = [ctx.enter_context(nc.semaphore(f"setup_{n}")) for n in ("load", "dve", "pool", "pe", "wload", "wdone")]
        s_load, s_dve, s_pool, s_pe, s_wload, s_wdone = su
        NW = 2 * L + 2
        with nc.Block() as block:
            @block.sync
            def _(sp_):
                n = 0
                for l in range(L):
                    for k, a in enumerate((g1, beta1, b2, g2, beta2)):
                        sp_.dma_start(lnc[:, l, k, :], a[l].partition_broadcast(P)).then_inc(s_load, 16)
                        n += 1
                    sp_.dma_start(sb_v[:, l, :, :], attn_w[l].rearrange("(a d) -> a d", a=2).partition_broadcast(P)).then_inc(s_load, 16)
                    with nc.allow_non_contiguous_dma(reason="bias as columns"):
                        sp_.dma_start(b1c[:, l, :], b1[l].rearrange("(c p) -> p c", p=P)).then_inc(s_load, 16)
                    n += 2
                sp_.dma_start(ab[:, :], attn_b.partition_broadcast(P)).then_inc(s_load, 16)
                with nc.allow_non_contiguous_dma(reason="attention vector as columns"):
                    sp_.dma_start(a_col[:, :], W_attn[0].rearrange("(a o) -> o a", a=2)).then_inc(s_load, 16)
                sp_.dma_start(wfc_sb[:, :], W_fc).then_inc(s_load, 16)
                sp_.dma_start(s8_row[:, 0:2 * D], a0.rearrange("d o -> (d o)").partition_broadcast(P)).then_inc(s_load, 16)
                sp_.dma_start(s8_row[:, 2 * D:4 * D], a3.rearrange("d o -> (d o)").partition_broadcast(P)).then_inc(s_load, 16)
                for w in range(NW):
                    if w >= 1:
                        sp_.wait_ge(s_wdone, w)
                    if w < 2:
                        src = (W0, W3)[w].rearrange("(c p) d -> p c d", p=P)
                        dst = stage[:, 0:DC * D].rearrange("p (c d) -> p c d", c=DC)
                    elif w < 2 + L:
                        src = W1[w - 2].rearrange("(c p) d -> p c d", p=P)
                        dst = stage.rearrange("p (c d) -> p c d", c=DC)
                    else:
                        src = W2[w - 2 - L].rearrange("(c p) d -> p c d", p=P)
                        dst = x_in[:, :, :]
                    sp_.dma_start(dst, src).then_inc(s_wload, 16)

            @block.gpsimd
            def _(pool):
                pool.memset(ident_f[:, :], 0.0).then_inc(s_pool, 1)
                pool.wait_ge(s_pool, 1)
                pool.affine_select(out=ident_f[:, :], in_=ident_f[:, :], compare_op=ALU.not_equal, fill=1.0,
                                   base=0, pattern=[[-1, P]], channel_multiplier=1).then_inc(s_pool, 1)

            @block.vector
            def _(dve):
                n = [0]

                def link(ins):
                    n[0] += 1
                    ins.then_inc(s_dve, 1)
                    dve.wait_ge(s_dve, n[0])

                dve.wait_ge(s_pool, 2)
                dve.tensor_copy(ident_b[:, :], ident_f[:, :])
                dve.tensor_scalar(diag_neg[:, :], ident_f[:, :], 1.0, BIG, ALU.subtract, ALU.mult)
                dve.memset(ones_f[:, :], 1.0)
                dve.memset(pick_s[:, :], 0.0)
                dve.memset(pick_t[:, :], 1.0)
                dve.memset(pick_r[:, :], 1.0)
                dve.memset(mean_w[:, :], 0.0)
                dve.memset(neg_half[:, :], -0.5)
                dve.memset(mask[:, :], 0.0)
                dve.memset(maskT[:, :], 0.0)
                dve.memset(rh[:, :, :], 0.0)
                dve.memset(rl[:, :, :], 0.0)
                link(dve.memset(spr[:, :, :], 0.0))
                dve.memset(pick_s[0:3, :], 1.0)
                dve.memset(pick_t[0:3, :], 0.0)
                dve.memset(pick_r[0:1, :], 0.0)
                dve.memset(mean_w[:, 0:1], 1.0 / N)
                link(dve.memset(rh[:, :, D:D + 1], 1.0))
                dve.wait_ge(s_load, 16 * (7 * L + 5))
                for k in range(2):
                    dve.tensor_scalar(a_mat[:, k, :], ones_f[0:OUT, :], a_col[:, k:k + 1], None, ALU.mult)
                link(dve.memset(junk[:, :, :], 0.0))
                for w in range(NW):
                    dve.wait_ge(s_wload, 16 * (w + 1))
                    if w < 2:
                        src = stage[:, 0:DC * D].rearrange("p (c d) -> p c d", c=DC)
                        for c in range(DC):
                            for k in range(2):
                                a_row = s8_row[:, (2 * w + k) * D:(2 * w + k + 1) * D]
                                dve.tensor_tensor_reduce(feat[:, (4 * w + 2 * c + k) * D:(4 * w + 2 * c + k + 1) * D], src[:, c, :], a_row, 1.0, 0.0,
                                                         ALU.mult, ALU.add, col[:, 2 * w + k, c:c + 1])
                        link(dve.tensor_scalar(wgh[:, w, :, 0:D], src, WSCALE, None, ALU.mult))
                        dve.scalar_tensor_tensor(out=wgl[:, w, :, 0:D], in0=src, scalar=WSCALE,
                                                 in1=wgh[:, w, :, 0:D], op0=ALU.mult, op1=ALU.subtract)
                        for k in range(2):
                            c_ = col[:, 2 * w + k, 0:DC]
                            link(dve.tensor_scalar(wgh[:, w, :, D + k], c_, WSCALE, None, ALU.mult))
                            last = dve.scalar_tensor_tensor(out=wgl[:, w, :, D + k], in0=c_, scalar=WSCALE,
                                                            in1=wgh[:, w, :, D + k], op0=ALU.mult, op1=ALU.subtract)
                        last.then_inc(s_wdone, 1)
                    else:
                        l = (w - 2) % L
                        hi, lo = (w1h, w1l) if w < 2 + L else (w2h, w2l)
                        hi, lo = (m[:, l, :, :].rearrange("p c d -> p (c d)") for m in (hi, lo))
                        link(dve.tensor_scalar(hi, stage, WSCALE, None, ALU.mult))
                        dve.scalar_tensor_tensor(out=lo, in0=stage, scalar=WSCALE, in1=hi,
                                                 op0=ALU.mult, op1=ALU.subtract).then_inc(s_wdone, 1)
                dve.wait_ge(s_pe, 1)
                dve.tensor_copy(sb_v[:, L, :, :], acc[:, 0:2, 0:D])

            @block.tensor
            def _(pe):
                pe.wait_ge(s_dve, 3)
                for k in range(2):
                    last = pe.matmul(acc[:, k, 0:D], a_mat[:, k, :], wfc_sb[:, :], start=True, stop=True)
                last.then_inc(s_pe, 1)

        names = ("x_loaded adj_loaded_0 adj_loaded_1 mask_made maskT_ps maskT_made diag_set tr_ps tr_hi tr_lo wh_ps wh_hi wh_lo "
                 "mean_ps mean_hi mean_lo r_hi r_lo sp_made rows_ps rows_made bc_ps bc_made spr_made rr_ps rr_made "
                 "v_ps x_made p_made pl_made tile_done acc_free elu_min elu_exp var_made rstd_made ln_made hb_made "
                 "r3_made l3_copy dve_step stored").split()
        S = {n: ctx.enter_context(nc.semaphore(n)) for n in names}
        first, last_sem = S[names[0]], S[names[-1]]
        (x_loaded, adj_loaded_0, adj_loaded_1, mask_made, maskT_ps, maskT_made, diag_set, tr_ps, tr_hi, tr_lo, wh_ps, wh_hi, wh_lo,
         mean_ps, mean_hi, mean_lo, r_hi, r_lo, sp_made, rows_ps, rows_made, bc_ps, bc_made, spr_made, rr_ps, rr_made,
         v_ps, x_made, p_made, pl_made, tile_done, acc_free, elu_min, elu_exp, var_made, rstd_made, ln_made, hb_made,
         r3_made, l3_copy, dve_step, stored) = (S[n] for n in names)
        adj_loaded = (adj_loaded_0, adj_loaded_1)

        def nodes(m, half):
            return m[:, half * HC:(half + 1) * HC, :]

        def flat(m, half):
            return nodes(m, half).rearrange("p c d -> p (c d)")

        def ln_before(a):
            return [None, "g0", "f0", "f1", "g1", "g2"][a]

        with nc.Fori(0, B) as b:
            with nc.Block() as block:
                @block.sync
                def _(sp_):
                    sp_.dma_start(x_cur[:, :, :], x[b].rearrange("(c p) d -> p c d", p=P)).then_inc(x_loaded, 16)
                    for c in range(NC):
                        if c >= 2:
                            sp_.wait_ge(mask_made, c - 1)
                        sp_.dma_start(adj_sb[:, c % 2, :], adj[b, c * P:(c + 1) * P, :]).then_inc(adj_loaded[c % 2], 16)
                    for half in range(2):
                        sp_.wait_ge(ln_made, ln_count("g3", half))
                        sp_.dma_start(out[b, half * HALF:(half + 1) * HALF, :].rearrange("(c p) d -> p c d", p=P),
                                      nodes(h, half)).then_inc(stored, 16)
                    sp_.wait_ge(stored, 32)

                @block.tensor
                def _(pe):
                    def transpose_mask(c):
                        pe.wait_ge(mask_made, c + 1)
                        if c >= 2:
                            pe.wait_ge(maskT_made, c - 1)
                        dst = misc[:, c % 2, :].bitcast(BF16)
                        for j in range(NC):
                            last = pe.transpose(dst[:, j * P:(j + 1) * P], mrow(mask, c, j * P, P), ident_b[:, :])
                        last.then_inc(maskT_ps, 1)

                    def transpose_half(k, src, half):
                        for fc in range(DC):
                            g = 4 * k + 2 * half + fc
                            if g >= 2:
                                pe.wait_ge(tr_lo, g - 1)
                            for c in range(HC):
                                last = pe.transpose(misc[:, fc, c * P:(c + 1) * P],
                                                    src[:, half * HC + c, fc * P:(fc + 1) * P], ident_f[:, :])
                            last.then_inc(tr_ps, 1)

                    def project(w):
                        for c in range(NC):
                            if c % HC == 0:
                                pe.wait_ge(tr_lo, (4 if w == 0 else 20) - (2 if c == 0 else 0))
                            if c >= 4:
                                pe.wait_ge(wh_lo, 8 * w + c - 3)
                            parts = [(yTh, wgh), (yTh, wgl), (yTl, wgh)]
                            for fc in range(DC):
                                for i, (y, wt) in enumerate(parts):
                                    last = pe.matmul(acc[:, c % 4, 0:R], y[:, fc, c * P:(c + 1) * P], wt[:, w, fc, :],
                                                     start=(fc == 0 and i == 0), stop=(fc == DC - 1 and i == 2))
                            last.then_inc(wh_ps, 1)

                    def mean_of_r(k, a):
                        if a == 0:
                            pe.wait_ge(wh_lo, NC)
                        else:
                            pe.wait_ge(r_hi, 2 * a)
                            pe.wait_ge(r_lo, 2 * a)
                            pe.wait_ge(acc_free, 2 * ATT_PASS[a])
                        for c in range(NC):
                            for m in (rh, rl):
                                last = pe.matmul(acc[0:4, 0, 0:R], mean_w[:, :], m[:, c, :],
                                                 start=(c == 0 and m is rh), stop=(c == NC - 1 and m is rl))
                        last.then_inc(mean_ps, 1)

                    def spread_rows(a):
                        pe.wait_ge(sp_made, a + 1)
                        for c in range(NC):
                            last = pe.matmul(misc_flat[0:6, c * P:(c + 1) * P], sp[:, c, :], ident_b[:, :],
                                             start=True, stop=True)
                        last.then_inc(rows_ps, 1)
                        pe.wait_ge(rows_made, a + 1)
                        for i in range(2):
                            last = pe.matmul(misc[:, i, :], pick_s[:, :], rows[:, i * 512:(i + 1) * 512], start=True, stop=True)
                        last.then_inc(bc_ps, 1)
                        if a < 5:
                            for i in range(2):
                                last = pe.matmul(vu[:, i, :], pick_t[:, :], rows[:, i * 512:(i + 1) * 512], start=True, stop=True)
                            last.then_inc(bc_ps, 1)

                    def row_term(a, half):
                        pe.wait_ge(spr_made, 2 * a + half + 1)
                        pe.wait_ge(bc_made, 2 * a + 1)
                        for c in range(HC):
                            last = pe.matmul(misc[0:4, half, c * P:(c + 1) * P], spr[:, half * HC + c, :], ident_b[:, :],
                                             start=True, stop=True)
                        last.then_inc(rr_ps, 1)

                    def where(a, n):
                        return (n // 2, n % 2) if a == 5 else (n % NC, n // NC)

                    def score_base(a, n):
                        T = TILES * ATT_PASS[a] + n
                        j, half = where(a, n)
                        if n == 0:
                            pe.wait_ge(maskT_made, NC)
                            if a in (1, 4):
                                pe.wait_ge(diag_set, 1 if a == 1 else 2)
                            if a < 5:
                                pe.wait_ge(bc_made, 2 * a + 2)
                        if n < 2 or (a < 5 and n == NC):
                            pe.wait_ge(rr_made, 2 * a + half + 1)
                        if T >= 2:
                            pe.wait_ge(p_made, 2 * (T - 1))
                        pe.matmul(vu[:, T % 2, :], ident_b[:, :], mrow(maskT, j, half * HALF, HALF), start=True, stop=False)
                        pe.matmul(vu[:, T % 2, :], pick_r[:, :], rowr[:, half * HALF:(half + 1) * HALF],
                                  start=False, stop=True).then_inc(v_ps, 1)

                    def aggregate(a, n):
                        T = TILES * ATT_PASS[a] + n
                        j, half = where(a, n)
                        s = T % RING
                        if n == 0:
                            if a in (1, 2, 3):
                                pe.wait_ge(r_hi, 2 * a)
                                pe.wait_ge(r_lo, 2 * a)
                            if a in (0, 4):
                                k = 0 if a == 0 else 1
                                pe.wait_ge(mean_hi, k + 1)
                                pe.wait_ge(mean_lo, k + 1)
                            pe.wait_ge(acc_free, 2 * ATT_PASS[a])
                        if n == NC:
                            pe.wait_ge(acc_free, 2 * ATT_PASS[a] + 1)
                        pe.wait_ge(p_made, 2 * (T + 1))
                        hi = [(ph, rh), (ph, rl)]
                        for c in range(HC):
                            for i, (p, r) in enumerate(hi):
                                pe.matmul(acc[:, c, 0:R], p[:, s, c * P:(c + 1) * P], r[:, j, :],
                                          start=(j == 0 and i == 0), stop=False)
                        pe.wait_ge(pl_made, T + 1)
                        for c in range(HC):
                            last = pe.matmul(acc[:, c, 0:R], pl[:, s, c * P:(c + 1) * P], rh[:, j, :], start=False,
                                             stop=(j == NC - 1 and a not in (0, 4)))
                        if j == NC - 1 and a in (0, 4):
                            for c in range(HC):
                                e_row = rowr[:, half * HALF + c * P:half * HALF + (c + 1) * P]
                                pe.matmul(acc[:, c, 0:R], e_row, mnh[:, :], start=False, stop=False)
                                last = pe.matmul(acc[:, c, 0:R], e_row, mnl[:, :], start=False, stop=True)
                        last.then_inc(tile_done, 1)

                    def aggregate_columns(j):
                        T = TILES * ATT_PASS[5] + 2 * j
                        if j == 0:
                            pe.wait_ge(acc_free, 2 * ATT_PASS[5])
                            pe.wait_ge(wh_lo, 2 * NC)
                        pe.wait_ge(r3_made, j + 1)
                        for half in range(2):
                            s = (T + half) % RING
                            pe.wait_ge(pl_made, T + half + 1)
                            for c in range(HC):
                                ic = half * HC + c
                                dst = acc[:, ic // 2, (ic % 2) * D:(ic % 2 + 1) * D]
                                for i, (p, r) in enumerate([(ph, rh), (ph, rl), (pl, rh)]):
                                    last = pe.matmul(dst, p[:, s, c * P:(c + 1) * P], r[:, j, 0:D],
                                                     start=(j == 0 and i == 0 and ic % 2 == 0),
                                                     stop=(j == NC - 1 and i == 2), skip_group_check=True)
                            last.then_inc(tile_done, 1)

                    def hidden(l, n):
                        T = TILES * FFN_PASS[l] + n
                        k, half = n % KC, n // KC
                        if k == 0:
                            pe.wait_ge(tr_lo, 4 * (l + 1) + 2 * half + 2)
                        pe.wait_ge(p_made, 2 * (T - 1))
                        parts = [(w1h, yTh), (w1h, yTl), (w1l, yTh)]
                        for fc in range(DC):
                            for i, (wt, y) in enumerate(parts):
                                last = pe.matmul(vu[:, T % 2, :], wt[:, l, fc, k * P:(k + 1) * P],
                                                 y[:, fc, half * HALF:(half + 1) * HALF],
                                                 start=(fc == 0 and i == 0), stop=(fc == DC - 1 and i == 2))
                        last.then_inc(v_ps, 1)

                    def contract(l, n):
                        T = TILES * FFN_PASS[l] + n
                        k, half = n % KC, n // KC
                        s = T % RING
                        if k == 0:
                            pe.wait_ge(acc_free, 2 * FFN_PASS[l] + half)
                        pe.wait_ge(p_made, 2 * (T + 1))
                        for c in range(HC):
                            for i, wt in enumerate((w2h, w2l)):
                                pe.matmul(acc[:, c, 0:D], ph[:, s, c * P:(c + 1) * P], wt[:, l, k, :],
                                          start=(k == 0 and i == 0), stop=False)
                        pe.wait_ge(pl_made, T + 1)
                        for c in range(HC):
                            last = pe.matmul(acc[:, c, 0:D], pl[:, s, c * P:(c + 1) * P], w2h[:, l, k, :],
                                             start=False, stop=(k == KC - 1))
                        last.then_inc(tile_done, 1)

                    for c in range(NC):
                        transpose_mask(c)
                    pe.wait_ge(maskT_made, NC)
                    pe.wait_ge(x_loaded, 16)
                    for half in range(2):
                        transpose_half(0, x_cur, half)
                    project(0)
                    for q, (kind, a) in enumerate(PASSES):
                        if kind == "att":
                            if a == 5:
                                pe.wait_ge(ln_made, ln_count("g2", 1))
                                for half in range(2):
                                    transpose_half(4, x_cur, half)
                                pe.wait_ge(acc_free, 2 * q)
                                project(1)
                            spread_rows(a)
                            if a in (0, 4):
                                mean_of_r(0 if a == 0 else 1, a)
                            row_term(a, 0)
                            if a == 5:
                                row_term(a, 1)
                            score_base(a, 0)
                            score_base(a, 1)
                            if a == 5:
                                for j in range(NC):
                                    if j + 1 < NC:
                                        score_base(a, 2 * j + 2)
                                        score_base(a, 2 * j + 3)
                                    aggregate_columns(j)
                                continue
                            for n in range(TILES):
                                if n == 14 and a in (1, 2, 3):
                                    pe.wait_ge(ln_made, ln_count(f"a{a - 1}", 0))
                                    transpose_half(a, h, 0)
                                aggregate(a, n)
                                if n == 4:
                                    row_term(a, 1)
                                if n + 2 < TILES:
                                    score_base(a, n + 2)
                        else:
                            hidden(a, 0)
                            hidden(a, 1)
                            for n in range(TILES):
                                if n == 4:
                                    pe.wait_ge(ln_made, ln_count(f"a{a}", 1))
                                    transpose_half(a + 1, h, 1)
                                contract(a, n)
                                if n + 2 < TILES:
                                    hidden(a, n + 2)

                @block.scalar
                def _(act):
                    def copy_transposed(g0):
                        for fc in range(DC):
                            g = g0 + fc
                            act.wait_ge(tr_ps, g + 1)
                            half = g // 2 % 2
                            act.activation(yTh[:, fc, half * HALF:(half + 1) * HALF], misc[:, fc, :], ACT.Copy).then_inc(tr_hi, 1)

                    def r_high(a, half, src):
                        act.wait_ge(ln_made, ln_count(ln_before(a), half))
                        act.activation(rh[:, half * HC:(half + 1) * HC, 0:D], nodes(src, half), ACT.Copy).then_inc(r_hi, 1)

                    for c in range(NC):
                        act.wait_ge(maskT_ps, c + 1)
                        act.activation(maskT_n[:, :, c * P:(c + 1) * P],
                                       misc[:, c % 2, :].bitcast(BF16).rearrange("p (j i) -> p j i", j=NC),
                                       ACT.Copy).then_inc(maskT_made, 1)
                    copy_transposed(0)
                    copy_transposed(2)
                    for c in range(NC):
                        act.wait_ge(wh_ps, c + 1)
                        act.activation(rh[:, c, 0:D], acc[:, c % 4, 0:D], ACT.Copy, scale=1.0 / WSCALE).then_inc(wh_hi, 1)
                    for q, (kind, a) in enumerate(PASSES):
                        if kind == "att":
                            if a == 5:
                                copy_transposed(16)
                                copy_transposed(18)
                                for c in range(NC):
                                    act.wait_ge(wh_ps, NC + c + 1)
                                    act.activation(h[:, c, :], acc[:, c % 4, 0:D], ACT.Copy, scale=1.0 / WSCALE).then_inc(wh_hi, 1)
                            act.wait_ge(rows_ps, a + 1)
                            act.activation(rows[:, :], misc_flat[0:6, :], ACT.Copy).then_inc(rows_made, 1)
                            act.wait_ge(bc_ps, 2 * a + 1)
                            act.activation(s8_row[:, :], misc_flat, ACT.Copy).then_inc(bc_made, 1)
                            if a < 5:
                                act.wait_ge(bc_ps, 2 * a + 2)
                                act.activation(t_row[:, :], vu_flat, ACT.Copy).then_inc(bc_made, 1)
                            if a in (0, 4):
                                act.wait_ge(mean_ps, 1 if a == 0 else 2)
                                act.activation(mnh[:, :], acc[0:4, 0, 0:R], ACT.Copy).then_inc(mean_hi, 1)

                            def copy_row_term(half):
                                act.wait_ge(rr_ps, 2 * a + half + 1)
                                act.activation(rowr[:, half * HALF:(half + 1) * HALF], misc[0:4, half, :], ACT.Copy).then_inc(rr_made, 1)

                            copy_row_term(0)
                            if a == 5:
                                copy_row_term(1)
                            for n in range(TILES):
                                T = TILES * q + n
                                s = T % RING
                                A = TILES * a + n
                                act.wait_ge(x_made, A + 1)
                                if T >= RING:
                                    act.wait_ge(tile_done, T - RING + 1)
                                if a < 5:
                                    t_j = st[:, 1, n % NC:n % NC + 1]
                                    act.activation(p32[:, s, :], xt[:, A % 2, :], ACT.Exp, bias=t_j).then_inc(p_made, 1)
                                    act.activation(ph[:, s, :], xt[:, A % 2, :], ACT.Exp, bias=t_j).then_inc(p_made, 1)
                                else:
                                    j, half = n // 2, n % 2
                                    bias, scale = col[:, 6, j:j + 1], col[:, 0, j:j + 1]
                                    act.activation(p32[:, s, :], xt[:, A % 2, :], ACT.Exp, bias=bias, scale=scale,
                                                   accum_out=csum[:, j, half:half + 1]).then_inc(p_made, 1)
                                    act.activation(ph[:, s, :], xt[:, A % 2, :], ACT.Exp, bias=bias, scale=scale).then_inc(p_made, 1)
                                if n == 5 and a < 5:
                                    copy_row_term(1)
                                if n == 11 and a in (0, 4):
                                    act.wait_ge(elu_min, (0 if a == 0 else 2) + 1)
                                    act.activation(flat(x_in, 0), flat(x_in, 0), ACT.Exp).then_inc(elu_exp, 1)
                                if n == 14 and a in (1, 2, 3):
                                    copy_transposed(4 * a)
                            if a in (0, 4):
                                act.wait_ge(elu_min, (0 if a == 0 else 2) + 2)
                                act.activation(flat(x_in, 1), flat(x_in, 1), ACT.Exp).then_inc(elu_exp, 1)
                            if a == 0:
                                r_high(1, 0, x_in)
                                r_high(1, 1, x_in)
                            if a == 5:
                                for k in range(4):
                                    act.wait_ge(tile_done, TILES * (q + 1))
                                    act.activation(x_in[:, 2 * k:2 * k + 2, :].rearrange("p c d -> p (c d)"), acc[:, k, :],
                                                   ACT.Copy).then_inc(l3_copy, 1)
                        else:
                            for n in range(TILES):
                                T = TILES * q + n
                                s = T % RING
                                act.wait_ge(v_ps, T + 1)
                                act.wait_ge(tile_done, T - RING + 1)
                                bias = b1c[:, a, n % KC:n % KC + 1]
                                act.activation(p32[:, s, :], vu[:, T % 2, :], ACT.Gelu, bias=bias, scale=1.0 / WSCALE).then_inc(p_made, 1)
                                act.activation(ph[:, s, :], vu[:, T % 2, :], ACT.Gelu, bias=bias, scale=1.0 / WSCALE).then_inc(p_made, 1)
                                if n == 5:
                                    copy_transposed(4 * (a + 1) + 2)
                                if n == 14 and a < 2:
                                    r_high(a + 2, 0, x_cur)
                            if a == 2:
                                r_high(a + 2, 0, x_cur)
                            r_high(a + 2, 1, x_cur)

                @block.gpsimd
                def _(pool):
                    def inv_std(name, half):
                        pool.wait_ge(var_made, ln_count(name, half))
                        cs = slice(half * HC, (half + 1) * HC)
                        pool.tensor_tensor(rstd[:, cs], vare[:, cs], neg_half[:, cs], ALU.pow).then_inc(rstd_made, 1)

                    def r_low(a, half, src):
                        pool.wait_ge(ln_made, ln_count(ln_before(a), half))
                        pool.wait_ge(r_hi, 2 * (a - 1) + half + 1 + (0))
                        pool.tensor_tensor(rl[:, half * HC:(half + 1) * HC, 0:D], nodes(src, half),
                                           rh[:, half * HC:(half + 1) * HC, 0:D], ALU.subtract).then_inc(r_lo, 1)

                    def add_b2(l, half):
                        pool.wait_ge(ln_made, ln_count(f"a{l}", half))
                        pool.tensor_tensor(nodes(x_cur, half), nodes(h, half),
                                           lnc[:, l, 2:3, :].broadcast_to([P, HC, D]), ALU.add).then_inc(hb_made, 1)

                    for q, (kind, a) in enumerate(PASSES):
                        for n in range(TILES):
                            T = TILES * q + n
                            s = T % RING
                            pool.wait_ge(p_made, 2 * (T + 1))
                            pool.tensor_tensor(pl[:, s, :], p32[:, s, :], ph[:, s, :], ALU.subtract).then_inc(pl_made, 1)
                            if kind == "att":
                                if n == 11 and a in (1, 2, 3):
                                    inv_std(f"a{a - 1}", 0)
                                if n == 13 and a in (0, 4):
                                    inv_std("g0" if a == 0 else "g2", 0)
                                if n == 15 and a in (1, 2, 3):
                                    add_b2(a - 1, 0)
                            else:
                                if n == 1:
                                    inv_std(f"a{a}", 1)
                                if n == 5:
                                    add_b2(a, 1)
                                if n == 10:
                                    inv_std(f"f{a}", 0)
                                if n == 12 and a == 2:
                                    inv_std("g1", 0)
                                if n == 14 and a < 2:
                                    r_low(a + 2, 0, x_cur)
                        if kind == "att" and a in (0, 4):
                            inv_std("g0" if a == 0 else "g2", 1)
                            if a == 0:
                                r_low(1, 0, x_in)
                                r_low(1, 1, x_in)
                        if kind == "ffn":
                            if a == 2:
                                inv_std("f2", 1)
                                inv_std("g1", 1)
                                r_low(4, 0, x_cur)
                                r_low(4, 1, x_cur)
                            else:
                                inv_std(f"f{a}", 1)
                                r_low(a + 2, 1, x_cur)
                    inv_std("g3", 0)
                    inv_std("g3", 1)

                @block.vector
                def _(dve):
                    steps = [0]

                    def link(ins):
                        steps[0] += 1
                        ins.then_inc(dve_step, 1)
                        dve.wait_ge(dve_step, steps[0])

                    def lag(ins):
                        steps[0] += 1
                        ins.then_inc(dve_step, 1)
                        if steps[0] > 1:
                            dve.wait_ge(dve_step, steps[0] - 1)

                    def catch_up():
                        dve.wait_ge(dve_step, steps[0])

                    def copy_transposed_low(g0):
                        for fc in range(DC):
                            g = g0 + fc
                            half = g // 2 % 2
                            cs = slice(half * HALF, (half + 1) * HALF)
                            dve.wait_ge(tr_hi, g + 1)
                            dve.tensor_tensor(yTl[:, fc, cs], misc[:, fc, :], yTh[:, fc, cs], ALU.subtract).then_inc(tr_lo, 1)

                    def score_columns(a, half, src):
                        for c in range(half * HC, (half + 1) * HC):
                            for k in range(2):
                                lag(dve.tensor_tensor_reduce(junk[:, k, 0:D], src[:, c, :], sb_v[:, a - 1, k, :], 1.0, 0.0,
                                                             ALU.mult, ALU.add, st[:, k, c:c + 1]))
                        catch_up()

                    def split_scores(a):
                        if a in (1, 2, 3):
                            link(dve.tensor_scalar(st[:, 0, :], st[:, 0, :], ab[:, a - 1:a], None, ALU.add))
                        dve.tensor_scalar(c2[:, 0, :], st[:, 0, :], 1 - SLOPE, None, ALU.mult)
                        dve.tensor_scalar(n8t[:, :], st[:, 1, :], SLOPE - 1, None, ALU.mult)
                        link(dve.tensor_copy(c2[:, 1, :], st[:, 1, :]))
                        parts = sp[:, :, :].rearrange("p c (v k) -> p v c k", v=2)
                        link(dve.tensor_copy(parts[:, :, :, 0], c2[:, :, :]))
                        link(dve.tensor_tensor(res[:, :, :], c2[:, :, :], parts[:, :, :, 0], ALU.subtract))
                        link(dve.tensor_copy(parts[:, :, :, 1], res[:, :, :]))
                        dve.tensor_tensor(parts[:, :, :, 2], res[:, :, :], parts[:, :, :, 1], ALU.subtract).then_inc(sp_made, 1)

                    KEEP, MAX, LEAKY, TERM = 0, 1, 2, 3

                    def row_maximum(a, c):
                        lag(dve.tensor_tensor_reduce(junk[:, c % 2, :], mask_n[:, c, :], t_row[:, :], 1.0, -3e38,
                                                     ALU.add, ALU.max, col[:, MAX, c:c + 1]))

                    def split_row_term(cs, src):
                        link(dve.tensor_copy(spr[:, cs, 1], src))
                        link(dve.tensor_tensor(resr[:, cs], src, spr[:, cs, 1], ALU.subtract))
                        link(dve.tensor_copy(spr[:, cs, 2], resr[:, cs]))
                        return dve.tensor_tensor(spr[:, cs, 3], resr[:, cs], spr[:, cs, 2], ALU.subtract)

                    def make_row_term(half):
                        cs = slice(half * HC, (half + 1) * HC)
                        s = st[:, 0, cs]
                        dve.tensor_scalar(spr[:, cs, 0], col[:, MAX, cs], -BIG / 2, None, ALU.is_le)
                        link(dve.tensor_scalar(col[:, KEEP, cs], col[:, MAX, cs], -BIG / 2, None, ALU.is_gt))
                        link(dve.tensor_tensor(col[:, MAX, cs], col[:, MAX, cs], col[:, KEEP, cs], ALU.mult))
                        link(dve.tensor_tensor(col[:, MAX, cs], s, col[:, MAX, cs], ALU.add))
                        link(dve.scalar_tensor_tensor(out=col[:, LEAKY, cs], in0=col[:, MAX, cs], scalar=SLOPE,
                                                      in1=col[:, MAX, cs], op0=ALU.mult, op1=ALU.max))
                        link(dve.scalar_tensor_tensor(out=col[:, TERM, cs], in0=s, scalar=SLOPE,
                                                      in1=col[:, LEAKY, cs], op0=ALU.mult, op1=ALU.subtract))
                        split_row_term(cs, col[:, TERM, cs]).then_inc(spr_made, 1)

                    def score_tile(a, n):
                        T = TILES * ATT_PASS[a] + n
                        A = TILES * a + n
                        j, half = (n // 2, n % 2) if a == 5 else (n % NC, n // NC)
                        dve.wait_ge(v_ps, T + 1)
                        if n == 0:
                            dve.wait_ge(bc_made, 2 * a + 1)
                        if n >= 2:
                            dve.wait_ge(p_made, 2 * (T - 1))
                        dve.scalar_tensor_tensor(out=xt[:, A % 2, :], in0=s8_row[:, half * HALF:(half + 1) * HALF],
                                                 scalar=n8t[:, j:j + 1], in1=vu[:, T % 2, :],
                                                 op0=ALU.max, op1=ALU.add).then_inc(x_made, 1)

                    def norm_stats(src, half):
                        for c in range(HC):
                            last = dve.bn_stats(bst[:, c, :], src[:, half * HC + c, :])
                        link(last)
                        for c in range(HC):
                            last = dve.bn_aggr(mv[:, half * HC + c, :], bst[:, c, :])
                        link(last)
                        cs = slice(half * HC, (half + 1) * HC)
                        dve.tensor_scalar(vare[:, cs], mv[:, cs, 1], EPS, None, ALU.add).then_inc(var_made, 1)

                    def norm_apply(name, half, src, dst):
                        dve.wait_ge(rstd_made, ln_count(name, half))
                        for c in range(half * HC, (half + 1) * HC):
                            last = dve.tensor_scalar(dst[:, c, :], src[:, c, :], mv[:, c, 0:1], rstd[:, c:c + 1],
                                                     ALU.subtract, ALU.mult)
                        last.then_inc(ln_made, 1)

                    def norm_apply_affine(name, half, src, dst, l, k):
                        dve.wait_ge(rstd_made, ln_count(name, half))
                        for c in range(half * HC, (half + 1) * HC):
                            last = dve.scalar_tensor_tensor(out=dst[:, c, :], in0=src[:, c, :], scalar=mv[:, c, 0:1],
                                                            in1=lnc[:, l, k, :], op0=ALU.subtract, op1=ALU.mult)
                        link(last)
                        for c in range(half * HC, (half + 1) * HC):
                            last = dve.scalar_tensor_tensor(out=dst[:, c, :], in0=dst[:, c, :], scalar=rstd[:, c:c + 1],
                                                            in1=lnc[:, l, k + 1, :], op0=ALU.mult, op1=ALU.add)
                        last.then_inc(ln_made, 1)

                    def take_attention(a, q, half, src):
                        dve.wait_ge(tile_done, TILES * q + 8 * (half + 1))
                        cs = slice(half * HC, (half + 1) * HC)
                        link(dve.reciprocal(rinv[:, cs], acc[:, :, D]))
                        for c in range(HC):
                            k = half * HC + c
                            if a in (1, 2, 3):
                                last = dve.scalar_tensor_tensor(out=h[:, k, :], in0=acc[:, c, 0:D], scalar=rinv[:, k:k + 1],
                                                                in1=src[:, k, :], op0=ALU.mult, op1=ALU.add)
                            else:
                                last = dve.tensor_scalar(h[:, k, :], acc[:, c, 0:D], rinv[:, k:k + 1], None, ALU.mult)
                        last.then_inc(acc_free, 1)
                        dve.wait_ge(acc_free, 2 * q + half + 1)
                        if a in (0, 4):
                            dve.tensor_scalar(flat(x_in, half), flat(h, half), 0.0, None, ALU.min).then_inc(elu_min, 1)

                    def add_elu(a, half):
                        link(dve.scalar_tensor_tensor(out=flat(h, half), in0=flat(h, half), scalar=0.0,
                                                      in1=flat(x_cur, half), op0=ALU.max, op1=ALU.add))
                        dve.wait_ge(elu_exp, (0 if a == 0 else 2) + half + 1)
                        link(dve.scalar_tensor_tensor(out=flat(h, half), in0=flat(x_in, half), scalar=-1.0,
                                                      in1=flat(h, half), op0=ALU.add, op1=ALU.add))

                    for c in range(NC):
                        dve.wait_ge(adj_loaded[c % 2], 16 * (c // 2 + 1))
                        dve.tensor_scalar(mask_n[:, c, :], adj_sb[:, c % 2, :], 0, -BIG, ALU.is_le, ALU.mult).then_inc(mask_made, 1)
                    copy_transposed_low(0)
                    copy_transposed_low(2)
                    for c in range(NC):
                        dve.wait_ge(wh_hi, c + 1)
                        link(dve.tensor_scalar(st[:, :, c], acc[:, c % 4, D:R], 1.0 / WSCALE, None, ALU.mult))
                        dve.scalar_tensor_tensor(out=rl[:, c, 0:D], in0=acc[:, c % 4, 0:D], scalar=1.0 / WSCALE,
                                                 in1=rh[:, c, 0:D], op0=ALU.mult, op1=ALU.subtract).then_inc(wh_lo, 1)

                    for q, (kind, a) in enumerate(PASSES):
                        if kind == "att" and a < 5:
                            src = x_in if a == 1 else x_cur
                            if a == 1:
                                for k, m in enumerate((mask, maskT)):
                                    dve.tensor_copy(diag_keep[:, k, :, :], diag(m))
                                link(dve.memset(junk[:, 0, 0:2], 0.0))
                                for m in (mask, maskT):
                                    last = dve.tensor_tensor(diag(m), diag(m), diag_neg[:, :].unsqueeze(1).broadcast_to([P, NC, P]), ALU.max)
                                last.then_inc(diag_set, 1)
                                dve.wait_ge(diag_set, 1)
                            if a == 4:
                                for k, m in enumerate((mask, maskT)):
                                    last = dve.tensor_copy(diag(m), diag_keep[:, k, :, :])
                                last.then_inc(diag_set, 1)
                                dve.wait_ge(diag_set, 2)
                            split_scores(a)
                            dve.wait_ge(bc_made, 2 * a + 2)
                            for c in range(HC):
                                row_maximum(a, c)
                            catch_up()
                            make_row_term(0)
                            if a in (0, 4):
                                dve.wait_ge(mean_hi, 1 if a == 0 else 2)
                                dve.tensor_tensor(mnl[:, :], acc[0:4, 0, 0:R], mnh[:, :], ALU.subtract).then_inc(mean_lo, 1)
                            name = {0: "g0", 4: "g2"}.get(a, f"a{a - 1}")
                            for n in range(TILES):
                                score_tile(a, n)
                                if n < HC:
                                    row_maximum(a, HC + n)
                                    if n == HC - 1:
                                        catch_up()
                                if n == HC:
                                    make_row_term(1)
                                if n == 9:
                                    take_attention(a, q, 0, src)
                                if n == 10 and a in (1, 2, 3):
                                    norm_stats(h, 0)
                                if n == 12:
                                    if a in (1, 2, 3):
                                        norm_apply_affine(name, 0, h, h, a - 1, 0)
                                    else:
                                        add_elu(a, 0)
                                        norm_stats(h, 0)
                            dst = x_in if a == 0 else x_cur
                            if a in (0, 4):
                                norm_apply(name, 0, h, dst)
                                if a == 0:
                                    dve.wait_ge(ln_made, ln_count("g0", 0))
                                    score_columns(1, 0, x_in)
                                take_attention(a, q, 1, src)
                                add_elu(a, 1)
                                norm_stats(h, 1)
                                norm_apply(name, 1, h, dst)
                                if a == 0:
                                    dve.wait_ge(ln_made, ln_count("g0", 1))
                                    score_columns(1, 1, x_in)
                            else:
                                copy_transposed_low(4 * a)
                                take_attention(a, q, 1, src)
                                norm_stats(h, 1)
                                norm_apply_affine(name, 1, h, h, a - 1, 0)
                        elif kind == "ffn":
                            copy_transposed_low(4 * (a + 1) + 2)
                            for half in range(2):
                                dve.wait_ge(tile_done, TILES * q + 8 * (half + 1))
                                dve.wait_ge(hb_made, 2 * a + half + 1)
                                for c in range(HC):
                                    k = half * HC + c
                                    last = dve.scalar_tensor_tensor(out=h[:, k, :], in0=acc[:, c, 0:D], scalar=1.0 / WSCALE,
                                                                    in1=x_cur[:, k, :], op0=ALU.mult, op1=ALU.add)
                                last.then_inc(acc_free, 1)
                                dve.wait_ge(acc_free, 2 * q + half + 1)
                                norm_stats(h, half)
                                norm_apply_affine(f"f{a}", half, h, x_cur, a, 3)
                                dve.wait_ge(ln_made, ln_count(f"f{a}", half))
                                if a == 2:
                                    link(dve.tensor_tensor(flat(h, half), flat(x_cur, half), flat(x_in, half), ALU.add))
                                    norm_stats(h, half)
                                    norm_apply("g1", half, h, x_cur)
                                    dve.wait_ge(ln_made, ln_count("g1", half))
                                score_columns(a + 2, half, x_cur)
                        else:
                            copy_transposed_low(16)
                            copy_transposed_low(18)
                            for c in range(NC):
                                dve.wait_ge(wh_hi, NC + c + 1)
                                last = dve.tensor_scalar(st[:, :, c], acc[:, c % 4, D:R], 1.0 / WSCALE, None, ALU.mult)
                                last.then_inc(wh_lo, 1)
                            dve.wait_ge(wh_lo, 2 * NC)
                            split_scores(5)
                            dve.memset(spr[:, :, 0], 0.0)
                            link(dve.tensor_scalar(col[:, TERM, :], st[:, 0, :], SLOPE, None, ALU.mult))
                            split_row_term(slice(0, NC), col[:, TERM, :]).then_inc(spr_made, 2)
                            dve.wait_ge(bc_made, 2 * 5 + 1)
                            for j in range(NC):
                                lag(dve.tensor_tensor_reduce(junk[:, j % 2, :], maskT_n[:, j, :], s8_row[:, :], 1.0, -3e38,
                                                             ALU.add, ALU.max, col[:, MAX, j:j + 1]))
                            catch_up()
                            link(dve.tensor_scalar(col[:, KEEP, :], col[:, MAX, :], -BIG / 2, None, ALU.is_gt))
                            link(dve.scalar_tensor_tensor(out=col[:, MAX, :], in0=col[:, MAX, :], scalar=1 / (1 - SLOPE),
                                                          in1=col[:, KEEP, :], op0=ALU.mult, op1=ALU.mult))
                            link(dve.tensor_tensor(col[:, MAX, :], st[:, 1, :], col[:, MAX, :], ALU.add))
                            link(dve.scalar_tensor_tensor(out=col[:, LEAKY, :], in0=col[:, MAX, :], scalar=SLOPE,
                                                          in1=col[:, MAX, :], op0=ALU.mult, op1=ALU.max))
                            link(dve.tensor_tensor(col[:, 5, :], st[:, 1, :], col[:, LEAKY, :], ALU.subtract))
                            link(dve.tensor_tensor(col[:, 6, :], col[:, 5, :], col[:, KEEP, :], ALU.mult))

                            def scale_columns(j):
                                dve.wait_ge(p_made, 2 * (TILES * q + 2 * j + 2))
                                link(dve.tensor_tensor(rinv[:, j:j + 1], csum[:, j, 0:1], csum[:, j, 1:2], ALU.add))
                                link(dve.reciprocal(rinv[:, j:j + 1], rinv[:, j:j + 1]))
                                link(dve.tensor_scalar(rh[:, j, 0:D], h[:, j, :], rinv[:, j:j + 1], None, ALU.mult))
                                dve.scalar_tensor_tensor(out=rl[:, j, 0:D], in0=h[:, j, :], scalar=rinv[:, j:j + 1],
                                                         in1=rh[:, j, 0:D], op0=ALU.mult, op1=ALU.subtract).then_inc(r3_made, 1)

                            for n in range(TILES):
                                score_tile(5, n)
                                if n % 2 == 1 and n >= 3:
                                    scale_columns(n // 2 - 1)
                            scale_columns(NC - 1)
                            for half in range(2):
                                dve.wait_ge(l3_copy, 2 * (half + 1))
                                link(dve.scalar_tensor_tensor(out=flat(x_in, half), in0=flat(x_in, half), scalar=SLOPE,
                                                              in1=flat(x_in, half), op0=ALU.mult, op1=ALU.max))
                                link(dve.tensor_tensor(flat(x_cur, half), flat(x_in, half), flat(x_cur, half), ALU.add))
                                norm_stats(x_cur, half)
                            for half in range(2):
                                norm_apply("g3", half, x_cur, h)

            nc.sync.sem_clear(range(first.num, last_sem.num + 1))
            nc.all_engine_barrier()


_INS = ["x", "adj", "L0_gnn_W", "L0_gnn_a", "L1_gnn_attn_w", "L1_gnn_attn_b", "L1_gnn_W1", "L1_gnn_b1", "L1_gnn_W2",
        "L1_gnn_b2", "L1_gnn_g1", "L1_gnn_beta1", "L1_gnn_g2", "L1_gnn_beta2", "L2_gnn_W_fc", "L2_gnn_W_attn",
        "L3_gnn_W", "L3_gnn_a"]


def kernel(**inputs):
    import numpy as _np
    import concourse.bacc as _bacc
    from concourse import mybir as _mybir
    from concourse.bass_utils import run_bass_kernel_spmd as _run

    nc = _bacc.Bacc("TRN2", target_bir_lowering=False, num_devices=1)
    arrays, args = {}, []
    for name in _INS:
        a = _np.ascontiguousarray(inputs[name])
        arrays[f"in_{name}_dram"] = a
        args.append(nc.dram_tensor(f"in_{name}_dram", a.shape, _mybir.dt.from_np(a.dtype), kind="ExternalInput").ap())
    shape = inputs["x"].shape
    o = nc.dram_tensor("out_0_dram", shape, _mybir.dt.float32, kind="ExternalOutput").ap()
    build(nc, *args, o)
    r = _run(nc, [arrays], core_ids=[0])
    return r.results[0]["out_0_dram"]
```

```python
from contextlib import ExitStack

import concourse.bass as bass
from concourse import mybir

ALU = mybir.AluOpType
ACT = mybir.ActivationFunctionType
F32 = mybir.dt.float32
F16 = mybir.dt.float16
BF16 = mybir.dt.bfloat16
FP8 = mybir.dt.float8e4
I32 = mybir.dt.int32
U8 = mybir.dt.uint8

P = 128
BIG = float(2.0 ** 100)
ONE8 = 56.0
TINY = float(2.0 ** -60)
WSCALE = 64.0
EPS = 1e-5
SLOPE = 0.2
TILES = 16
RING = 4
LAYERS = 3

ROUNDS = [[("att", 0)]] + [[("att", l + 1), ("ffn", l)] for l in range(LAYERS)] + [[("att", 4)], [("att", 5)]]
SLOTS = [(g, passes) for passes in ROUNDS for g in range(2)]
PASSES = [(g, kind, i) for g, passes in SLOTS for kind, i in passes]
ALL_TILES = TILES * len(PASSES)
NEXT = 2

SIGNALS = {
    "mask_made": ("D", {"mask": 1}), "maskT_ps": ("P", {"maskT": 2}), "maskT_made": ("A", {"maskT": 2}),
    "diag_made": ("D", {"diag": 1}),
    "tr_ps": ("P", {"tr": 2}), "tr_hi": ("A", {"tr": 2}), "tr_lo": ("D", {"tr": 2}),
    "wh_ps": ("P", {"proj": 1}), "wh_hi": ("A", {"proj": 1}), "wh_lo": ("D", {"proj": 1}),
    "mean_ps": ("P", {"mean": 1}), "mean_hi": ("A", {"mean": 1}), "mean_lo": ("D", {"mean": 1}),
    "r_hi": ("A", {"right": 1}), "r_lo": ("G", {"right": 1}),
    "sp_made": ("D", {"split": 1}), "rows_ps": ("P", {"rows": 1}), "rows_made": ("A", {"rows": 1}),
    "t_ps": ("P", {"t": 1}), "t_made": ("A", {"t": 1}), "s8_ps": ("P", {"s8": 1}), "s8_made": ("A", {"s8": 1}),
    "spr_made": ("D", {"row_term": 1}), "rr_ps": ("P", {"rr": 2}), "rr_made": ("A", {"rr": 2}),
    "acc_free": ("D", {"take": 4}), "elu_min": ("D", {"clip": 1}), "r3_made": ("D", {"scale": 1}),
    "elu_exp": ("A", {"elu": 1}), "hb_made": ("G", {"b2": 1}),
    "l3_copy": ("A", {"l3": 4}), "var_made": ("D", {"stats": 1}), "rstd_made": ("G", {"norm": 1}), "ln_made": ("D", {"norm": 1}),
}


PLAN = {
    "fg_short": [
        ("take", ("att", "{a}", 0), "D10"),
        ("clip", ("{a}", 0), "D10"),
        ("elu", ("{a}", 0), "D12 A11"),
        ("stats", ("att{a}", 0), "D12"),
        ("norm", ("att{a}", 0), "D15 G12"),
    ],
    "fg_long": [
        ("take", ("att", "{a}", 0), "D10"),
        ("stats", ("att{a}", 0), "D10"),
        ("norm", ("att{a}", 0), "D12 G10"),
        ("take", ("att", "{a}", 1), "D18"),
        ("stats", ("att{a}", 1), "D18"),
        ("norm", ("att{a}", 1), "D20 G18"),
        ("tr", ("ffn{l}", 0), "D15 A15 P12"),
        ("tr", ("ffn{l}", 1), "D21 A21 P18"),
        ("b2", ("{l}", 0), "G18"),
        ("b2", ("{l}", 1), "G22"),
        ("take", ("ffn", "{l}", 0), "D24"),
        ("stats", ("ffn{l}", 0), "D25"),
        ("norm", ("ffn{l}", 0), "D26 G25"),
    ],
    "fg_long_last": [
        ("take", ("att", "{a}", 0), "D8"),
        ("stats", ("att{a}", 0), "D10"),
        ("norm", ("att{a}", 0), "D12 G10"),
        ("take", ("att", "{a}", 1), "D18"),
        ("stats", ("att{a}", 1), "D18"),
        ("norm", ("att{a}", 1), "D20 G18"),
        ("tr", ("ffn{l}", 0), "D15 A15 P12"),
        ("tr", ("ffn{l}", 1), "D21 A21 P18"),
        ("b2", ("{l}", 0), "G18"),
        ("b2", ("{l}", 1), "G22"),
        ("take", ("ffn", "{l}", 0), "D27"),
        ("stats", ("ffn{l}", 0), "D28"),
        ("norm", ("ffn{l}", 0), "D29 G28"),
        ("outer", (0,), "D30"),
        ("stats", ("outer", 0), "D30"),
        ("norm", ("outer", 0), "D32 G30"),
    ],
    "fg_columns": [
        ("scale", (0,), "D2"),
        ("scale", (1,), "D4"),
        ("scale", (2,), "D6"),
        ("scale", (3,), "D8"),
        ("scale", (4,), "D10"),
        ("scale", (5,), "D12"),
        ("scale", (6,), "D14"),
        ("scale", (7,), "D15"),
    ],
    "bg0": [
        ("mask", (0,), "D0"),
        ("mask", (1,), "D1"),
        ("mask", (2,), "D2"),
        ("mask", (3,), "D3"),
        ("mask", (4,), "D4"),
        ("mask", (5,), "D5"),
        ("mask", (6,), "D6"),
        ("mask", (7,), "D7"),
        ("maskT", (0,), "A1 P0"),
        ("maskT", (1,), "A5 P2"),
        ("maskT", (2,), "A6 P3"),
        ("maskT", (3,), "A7 P4"),
        ("maskT", (4,), "A8 P5"),
        ("maskT", (5,), "A9 P6"),
        ("maskT", (6,), "A10 P7"),
        ("maskT", (7,), "A11 P8"),
        ("tr", (0, 0), "D4 A4 P1"),
        ("tr", (0, 1), "D4 A4 P1"),
        ("proj", (0, 0), "D7 A7 P4"),
        ("proj", (0, 1), "D7 A7 P4"),
        ("proj", (0, 2), "D8 A8 P5"),
        ("proj", (0, 3), "D8 A8 P5"),
        ("proj", (0, 4), "D10 A10 P7"),
        ("proj", (0, 5), "D10 A10 P7"),
        ("proj", (0, 6), "D11 A11 P8"),
        ("proj", (0, 7), "D11 A11 P8"),
        ("split", (0, 0), "D8.5"),
        ("rows", (0, 0), "A10 P7"),
        ("t", (0, 0), "A11 P8"),
        ("s8", (0, 0), "A11 P8"),
        ("max", (0, 0, (0, 1)), "D11"),
        ("max", (0, 0, (2, 3)), "D11"),
        ("max", (0, 0, (4, 5)), "D12"),
        ("max", (0, 0, (6, 7)), "D12"),
        ("split", (0, 1), "D11"),
        ("rows", (0, 1), "A12 P10"),
        ("t", (0, 1), "A13 P11"),
        ("s8", (0, 1), "A13 P11"),
        ("max", (0, 1, (0, 1)), "D13"),
        ("max", (0, 1, (2, 3)), "D13"),
        ("max", (0, 1, (4, 5)), "D14"),
        ("max", (0, 1, (6, 7)), "D14"),
        ("row_term", (0,), "D14"),
        ("mean", (0,), "D15 A15 P12"),
        ("rr", (0,), "A15 P13"),
    ],
    "bg1": [
        ("take", ("att", 0, 1), "D2"),
        ("clip", (0, 1), "D2"),
        ("elu", (0, 1), "D4 A3"),
        ("stats", ("att0", 1), "D4"),
        ("norm", ("att0", 1), "D6 G4"),
        ("cols", (1, (0, 1)), "D0"),
        ("cols", (1, (2, 3)), "D0"),
        ("right", (1, 0), "A1 G4"),
        ("cols", (1, (4, 5)), "D6"),
        ("cols", (1, (6, 7)), "D6"),
        ("right", (1, 1), "A8 G9"),
        ("diag", (), "D1"),
        ("split", (1, 0), "D2"),
        ("rows", (1, 0), "A5 P2"),
        ("t", (1, 0), "A7 P4"),
        ("s8", (1, 0), "A7 P4"),
        ("max", (1, 0, (0, 1)), "D8"),
        ("max", (1, 0, (2, 3)), "D8"),
        ("max", (1, 0, (4, 5)), "D9"),
        ("max", (1, 0, (6, 7)), "D9"),
        ("split", (1, 1), "D7"),
        ("rows", (1, 1), "A10 P7"),
        ("t", (1, 1), "A11.5 P8.5"),
        ("s8", (1, 1), "A12 P9"),
        ("max", (1, 1, (0, 1)), "D12"),
        ("max", (1, 1, (2,)), "D12"),
        ("max", (1, 1, (3, 4)), "D12"),
        ("max", (1, 1, (5,)), "D12"),
        ("max", (1, 1, (6, 7)), "D13"),
        ("row_term", (1,), "D13"),
        ("rr", (1,), "A14 P12"),
    ],
    "bg2": [
        ("take", ("att", 0, 1), "D2"),
        ("clip", (0, 1), "D2.5"),
        ("elu", (0, 1), "D4 A3"),
        ("stats", ("att0", 1), "D4"),
        ("norm", ("att0", 1), "D6 G4"),
        ("cols", (1, (0, 1)), "D14"),
        ("cols", (1, (2, 3)), "D14"),
        ("right", (1, 0), "A17 G20"),
        ("cols", (1, (4, 5)), "D16"),
        ("cols", (1, (6, 7)), "D16"),
        ("right", (1, 1), "A18 G21"),
        ("diag", (), "D17"),
        ("split", (1, 0), "D15"),
        ("rows", (1, 0), "A19 P17"),
        ("t", (1, 0), "A22 P20"),
        ("s8", (1, 0), "A22 P20"),
        ("max", (1, 0, (0, 1)), "D22"),
        ("max", (1, 0, (2, 3)), "D22"),
        ("max", (1, 0, (4, 5)), "D22"),
        ("max", (1, 0, (6, 7)), "D22"),
        ("split", (1, 1), "D16"),
        ("rows", (1, 1), "A19 P17"),
        ("t", (1, 1), "A23 P21"),
        ("s8", (1, 1), "A23 P21"),
        ("max", (1, 1, (0, 1)), "D21"),
        ("max", (1, 1, (2, 3)), "D24"),
        ("max", (1, 1, (4, 5)), "D24"),
        ("max", (1, 1, (6, 7)), "D24"),
        ("row_term", (1,), "D25.5"),
        ("rr", (1,), "A29 P27"),
    ],
    "bg3": [
        ("take", ("ffn", "{l}", 1), "D2"),
        ("stats", ("ffn{l}", 1), "D2"),
        ("norm", ("ffn{l}", 1), "D4 G2"),
        ("cols", ("{a}", (0, 1)), "D14"),
        ("cols", ("{a}", (2, 3)), "D14"),
        ("right", ("{a}", 0), "A17 G20"),
        ("cols", ("{a}", (4, 5)), "D16"),
        ("cols", ("{a}", (6, 7)), "D16"),
        ("right", ("{a}", 1), "A18 G21"),
        ("split", ("{a}", 0), "D15"),
        ("rows", ("{a}", 0), "A19 P17"),
        ("t", ("{a}", 0), "A22 P20"),
        ("s8", ("{a}", 0), "A22 P20"),
        ("max", ("{a}", 0, (0, 1)), "D22"),
        ("max", ("{a}", 0, (2, 3)), "D22"),
        ("max", ("{a}", 0, (4, 5)), "D22"),
        ("max", ("{a}", 0, (6, 7)), "D21"),
        ("split", ("{a}", 1), "D16"),
        ("rows", ("{a}", 1), "A19 P17"),
        ("t", ("{a}", 1), "A24 P22"),
        ("s8", ("{a}", 1), "A24 P22"),
        ("max", ("{a}", 1, (0, 1)), "D25"),
        ("max", ("{a}", 1, (2, 3)), "D25"),
        ("max", ("{a}", 1, (4, 5)), "D25"),
        ("max", ("{a}", 1, (6, 7)), "D25"),
        ("row_term", ("{a}",), "D25"),
        ("rr", ("{a}",), "A28 P26"),
    ],
    "bg7": [
        ("take", ("ffn", 2, 1), "D2"),
        ("stats", ("ffn2", 1), "D2"),
        ("norm", ("ffn2", 1), "D4 G2"),
        ("outer", (1,), "D4"),
        ("stats", ("outer", 1), "D4"),
        ("norm", ("outer", 1), "D6 G4"),
        ("cols", (4, (0, 1)), "D14"),
        ("cols", (4, (2, 3)), "D14.5"),
        ("right", (4, 0), "A17 G20"),
        ("cols", (4, (4, 5)), "D16"),
        ("cols", (4, (6, 7)), "D16"),
        ("right", (4, 1), "A18 G21"),
        ("split", (4, 0), "D15"),
        ("rows", (4, 0), "A19 P17"),
        ("t", (4, 0), "A22 P20"),
        ("s8", (4, 0), "A22 P20"),
        ("max", (4, 0, (0, 1)), "D22"),
        ("max", (4, 0, (2, 3)), "D22"),
        ("max", (4, 0, (4, 5)), "D22"),
        ("max", (4, 0, (6, 7)), "D22"),
        ("split", (4, 1), "D16"),
        ("rows", (4, 1), "A19 P17"),
        ("t", (4, 1), "A23 P21"),
        ("s8", (4, 1), "A23 P21"),
        ("max", (4, 1, (0, 1)), "D24"),
        ("max", (4, 1, (2, 3)), "D24"),
        ("max", (4, 1, (4, 5)), "D24"),
        ("max", (4, 1, (6, 7)), "D24"),
        ("row_term", (4,), "D24"),
        ("mean", (4,), "D25 A25 P22"),
        ("rr", (4,), "A28 P26"),
        ("mask>", (0,), "D26"),
        ("mask>", (1,), "D26"),
        ("mask>", (2,), "D27"),
        ("mask>", (3,), "D27"),
        ("mask>", (4,), "D28"),
        ("mask>", (5,), "D29"),
        ("mask>", (6,), "D30"),
        ("mask>", (7,), "D31"),
    ],
    "bg8": [
        ("take", ("ffn", 2, 1), "D2"),
        ("stats", ("ffn2", 1), "D2"),
        ("norm", ("ffn2", 1), "D4 G2"),
        ("outer", (1,), "D4"),
        ("stats", ("outer", 1), "D4"),
        ("norm", ("outer", 1), "D6 G4"),
        ("cols", (4, (0, 1)), "D0"),
        ("cols", (4, (2, 3)), "D0"),
        ("right", (4, 0), "A1 G4"),
        ("cols", (4, (4, 5)), "D7"),
        ("cols", (4, (6, 7)), "D7"),
        ("right", (4, 1), "A9 G10"),
        ("split", (4, 0), "D1"),
        ("rows", (4, 0), "A5 P2"),
        ("t", (4, 0), "A7 P4"),
        ("s8", (4, 0), "A7 P4"),
        ("max", (4, 0, (0, 1)), "D8"),
        ("max", (4, 0, (2, 3)), "D8"),
        ("max", (4, 0, (4, 5)), "D9"),
        ("max", (4, 0, (6, 7)), "D8"),
        ("split", (4, 1), "D8"),
        ("rows", (4, 1), "A10 P7"),
        ("t", (4, 1), "A12 P9"),
        ("s8", (4, 1), "A12 P9"),
        ("max", (4, 1, (0, 1)), "D12"),
        ("max", (4, 1, (2,)), "D12"),
        ("max", (4, 1, (3, 4)), "D13"),
        ("max", (4, 1, (5,)), "D13"),
        ("max", (4, 1, (6, 7)), "D14"),
        ("row_term", (4,), "D14"),
        ("mean", (4,), "D13 A13 P10"),
        ("rr", (4,), "A15 P13"),
    ],
    "bg9": [
        ("take", ("att", 4, 1), "D2"),
        ("clip", (4, 1), "D2"),
        ("elu", (4, 1), "D4 A3"),
        ("stats", ("att4", 1), "D4"),
        ("norm", ("att4", 1), "D6 G4"),
        ("tr", (5, 0), "D4 A4 P1"),
        ("tr", (5, 1), "D9 A9 P6"),
        ("proj", (5, 0), "A6 P3"),
        ("proj", (5, 1), "A6 P3"),
        ("proj", (5, 2), "A7 P4"),
        ("proj", (5, 3), "A7 P4"),
        ("proj", (5, 4), "A10 P7"),
        ("proj", (5, 5), "A10 P7"),
        ("proj", (5, 6), "A11 P8"),
        ("proj", (5, 7), "A11 P8"),
        ("split", (5, 0), "D8"),
        ("rows", (5, 0), "A10 P7"),
        ("s8", (5, 0), "A11 P8"),
        ("max", (5, 0, (0, 1)), "D11"),
        ("max", (5, 0, (2, 3)), "D11"),
        ("max", (5, 0, (4, 5)), "D13"),
        ("max", (5, 0, (6, 7)), "D13"),
        ("split", (5, 1), "D11"),
        ("rows", (5, 1), "A12 P10"),
        ("s8", (5, 1), "A13 P11"),
        ("max", (5, 1, (0, 1)), "D13"),
        ("max", (5, 1, (2, 3)), "D13"),
        ("max", (5, 1, (4, 5)), "D14"),
        ("max", (5, 1, (6, 7)), "D14"),
        ("row_term", (5,), "D14"),
        ("rr", (5,), "A14 P12"),
    ],
    "bg10": [
        ("take", ("att", 4, 1), "D3"),
        ("clip", (4, 1), "D3"),
        ("elu", (4, 1), "D5 A4"),
        ("stats", ("att4", 1), "D5"),
        ("norm", ("att4", 1), "D7 G5"),
        ("tr", (5, 0), "D5 A5 P2"),
        ("tr", (5, 1), "D9 A9 P6"),
        ("proj", (5, 0), "A7 P4"),
        ("proj", (5, 1), "A6 P3"),
        ("proj", (5, 2), "A7 P4"),
        ("proj", (5, 3), "A7 P4"),
        ("proj", (5, 4), "A10 P7"),
        ("proj", (5, 5), "A10 P7"),
        ("proj", (5, 6), "A11 P8"),
        ("proj", (5, 7), "A11 P8"),
        ("split", (5, 0), "D7"),
        ("rows", (5, 0), "A10 P7"),
        ("s8", (5, 0), "A11 P8"),
        ("max", (5, 0, (0, 1)), "D11"),
        ("max", (5, 0, (2, 3)), "D11"),
        ("max", (5, 0, (4, 5)), "D12"),
        ("max", (5, 0, (6, 7)), "D12"),
        ("split", (5, 1), "D11"),
        ("rows", (5, 1), "A11 P9"),
        ("s8", (5, 1), "A13 P11"),
        ("max", (5, 1, (0, 1)), "D13"),
        ("max", (5, 1, (2, 3)), "D13"),
        ("max", (5, 1, (4, 5)), "D14"),
        ("max", (5, 1, (6, 7)), "D14"),
        ("row_term", (5,), "D14"),
        ("rr", (5,), "A15 P13"),
    ],
    "bg11": [
        ("l3", (), "D3 A2"),
        ("l3_sum", (0,), "D4"),
        ("stats", ("att5", 0), "D4"),
        ("norm", ("att5", 0), "D6 G4"),
        ("l3_sum", (1,), "D5"),
        ("stats", ("att5", 1), "D5"),
        ("norm", ("att5", 1), "D7 G5"),
        ("maskT", (0,), "A4 P1"),
        ("maskT", (1,), "A5 P2"),
        ("maskT", (2,), "A6 P3"),
        ("maskT", (3,), "A6 P3"),
        ("maskT", (4,), "A7 P4"),
        ("maskT", (5,), "A8 P5"),
        ("maskT", (6,), "A9 P6"),
        ("maskT", (7,), "A10 P7"),
        ("tr", (0, 0), "D3 A3 P0"),
        ("tr", (0, 1), "D5 A5 P2"),
        ("proj", (0, 0), "D6.5 A6.5 P3.5"),
        ("proj", (0, 1), "D6.5 A6.5 P3.5"),
        ("proj", (0, 2), "D7.5 A7.5 P4.5"),
        ("proj", (0, 3), "D7.5 A7.5 P4.5"),
        ("proj", (0, 4), "D10 A10 P7"),
        ("proj", (0, 5), "D10 A10 P7"),
        ("proj", (0, 6), "D11 A11 P8"),
        ("proj", (0, 7), "D11 A11 P8"),
        ("split", (0, 0), "D8"),
        ("rows", (0, 0), "A10 P7"),
        ("t", (0, 0), "A11 P8"),
        ("s8", (0, 0), "A11 P8"),
        ("max", (0, 0, (0, 1)), "D11"),
        ("max", (0, 0, (2, 3)), "D14"),
        ("max", (0, 0, (4, 5)), "D12"),
        ("max", (0, 0, (6, 7)), "D12"),
        ("split", (0, 1), "D11"),
        ("rows", (0, 1), "A12 P10"),
        ("t", (0, 1), "A13 P11"),
        ("s8", (0, 1), "A13 P11"),
        ("max", (0, 1, (0, 1)), "D13"),
        ("max", (0, 1, (2, 3)), "D13"),
        ("max", (0, 1, (4, 5)), "D14"),
        ("max", (0, 1, (6, 7)), "D14"),
        ("row_term", (0,), "D14"),
        ("mean", (0,), "D15 A15 P12"),
        ("rr", (0,), "A15 P13"),
    ],
    "tail": [
        ("l3", (), "D3 A3"),
        ("l3_sum", (0,), "D4"),
        ("stats", ("att5", 0), "D4"),
        ("norm", ("att5", 0), "D6 G4"),
        ("l3_sum", (1,), "D5"),
        ("stats", ("att5", 1), "D5"),
        ("norm", ("att5", 1), "D7 G5"),
    ],
}


def planned(name, g, **which):
    def fill(x):
        if not isinstance(x, str):
            return x
        x = x.format(**which)
        return int(x) if x.isdigit() else x

    steps = []
    for step, rest, places in PLAN[name]:
        ahead = step.endswith(">")
        steps.append(((step.rstrip(">"), NEXT if ahead else g, *(fill(x) for x in rest)),
                      {p[0]: float(p[1:]) for p in places.split()}))
    return steps


def foreground(k):
    g, passes = SLOTS[k]
    a = passes[0][1]
    if len(passes) == 2:
        return planned("fg_long_last" if a == LAYERS else "fg_long", g, a=a, l=a - 1)
    return planned("fg_columns" if a == 5 else "fg_short", g, a=a)


def background(k):
    g = 1 - SLOTS[k][0]
    if 3 <= k <= 6:
        return planned("bg3", g, a=(k - 1) // 2 + 1, l=(k - 3) // 2)
    if k == len(SLOTS) - 1:
        return [((s[0], NEXT if s[0] in AHEAD else g, *s[2:]), at_) for s, at_ in planned("bg11", g)]
    return planned(f"bg{k}", g)


AHEAD = ("maskT", "tr", "proj", "split", "rows", "t", "s8", "max", "row_term", "mean", "rr")


def timetable(engine, in_loop):
    if not in_loop:
        steps = []
        for c in range(8):
            steps += [("mask", NEXT, c), ("maskT", NEXT, c)]
            if c in (3, 5, 7):
                steps.append(("weight", NEXT, (c - 3) // 2))
        for half in range(2):
            steps += [("tr", NEXT, 0, half)] + [("proj", NEXT, 0, c) for c in range(4 * half, 4 * half + 4)]
            steps.append(("weight", NEXT, 3 + half))
        steps += [x for half in range(2) for x in (("split", NEXT, 0, half), ("rows", NEXT, 0, half), ("t", NEXT, 0, half),
                                                   ("s8", NEXT, 0, half), ("max", NEXT, 0, half, tuple(range(8))))]
        steps += [("row_term", NEXT, 0), ("mean", NEXT, 0), ("rr", NEXT, 0), ("weight", NEXT, 2 * LAYERS - 1)]
        parts = {"weight": "AD", "mask": "D", "maskT": "PA", "tr": "PAD", "proj": "PAD", "split": "D", "rows": "PA", "t": "PA", "s8": "PA",
                 "max": "D", "row_term": "D", "mean": "PAD", "rr": "PA"}
        return [(0, s) for s in steps if engine in parts[s[0]]]
    table, start = [], 0
    for k, (g, passes) in enumerate(SLOTS):
        table += [(start + at_[engine], s) for s, at_ in foreground(k) + background(k) if engine in at_]
        start += TILES * len(passes)
    table += [(start + at_[engine], s) for s, at_ in planned("tail", 1) if engine in at_]
    return sorted(table, key=lambda entry: entry[0])


def pass_index(g, kind, i):
    return PASSES.index((g, kind, i))


def begin_place(T):
    _, kind, i = PASSES[T // TILES]
    n = T % TILES
    if T < 3:
        return 0
    if kind == "ffn":
        return T - (FFN_AHEAD[n] if n < len(FFN_AHEAD) else 3)
    if i == 5:
        return T - (COLUMNS_AHEAD[n] if n < len(COLUMNS_AHEAD) else 4)
    short = len(SLOTS[slot_of(T - n - 1)][1]) == 1
    ahead = SHORT_AHEAD if short else LONG_AHEAD
    return T - (ahead[n] if n < len(ahead) else 3)


FFN_AHEAD = (1, 2, 2, 2)
COLUMNS_AHEAD = (2, 3)
LONG_AHEAD = (3,)
SHORT_AHEAD = (2, 3)


def slot_of(T):
    start = 0
    for k, (_, passes) in enumerate(SLOTS):
        start += TILES * len(passes)
        if T < start:
            return k
    raise ValueError(T)



def build(nc, x, adj, W0, a0, attn_w, attn_b, W1, b1, W2, b2, g1, beta1, g2, beta2, W_fc, W_attn, W3, a3, out):
    B, N, D = x.shape
    NC, DC, HALF = N // P, D // P, N // 2
    HC = NC // 2
    L, H = b1.shape
    KC = H // P
    OUT = W_fc.shape[0]
    R = D + 2
    assert (NC, HC * P, KC, L, B % 2) == (8, HALF, 8, LAYERS, 0)

    ctx = ExitStack()
    with ctx:
        def sb(name, shape, dt):
            return ctx.enter_context(nc.sbuf_tensor(name, shape, dt))

        ident_f = sb("ident_f", [P, P], F32)
        ident_b = sb("ident_b", [P, P], BF16)
        ident_big = sb("ident_big", [P, P], BF16)
        ident_pos = sb("ident_pos", [P, P], BF16)
        ident_u8 = sb("ident_u8", [P, P], U8)
        pick_s = sb("pick_s", [6, P], BF16)
        pick_t = sb("pick_t", [6, P], BF16)
        pick_r = sb("pick_r", [4, P], BF16)
        mean_w = sb("mean_w", [P, 4], F16)
        neg_half = sb("neg_half", [P, NC], F32)
        wbuf = sb("wbuf", [P, 4, DC * H], F16)
        w1h, w1l = (wbuf[:, k, :].rearrange("p (c d) -> p c d", c=DC) for k in range(2))
        w2h, w2l = (wbuf[:, k, :].rearrange("p (c d) -> p c d", c=KC) for k in range(2, 4))
        wgh, wgl = sb("wgh", [P, 2, DC, R], F16), sb("wgl", [P, 2, DC, R], F16)
        b1c = sb("b1c", [P, L, KC], F32)
        score_v = sb("score_v", [P, L + 1, 2, D], F32)
        ab = sb("attn_bias", [P, L], F32)
        lnc = sb("ln_const", [P, L, 5, D], F32)
        w_split = nc.dram_tensor("w_split", [L, 4, P, DC * H], F16, kind="Internal").ap()

        def pair(name, shape, dt):
            return [sb(f"{name}{g}", shape, dt) for g in range(2)]

        x_cur, x_in = pair("x_cur", [P, NC, D], F32), pair("x_in", [P, NC, D], F32)
        rh, rl = pair("rh", [P, NC, R], F16), pair("rl", [P, NC, R], F16)
        mask = pair("mask", [P, NC * N], FP8)
        maskT = pair("maskT", [P, NC * N], FP8)
        maskD = pair("maskD", [P, NC, P], FP8)
        s8_row = pair("s8_row", [P, N], F32)
        rowr = pair("rowr", [4, N], BF16)
        st = pair("st", [P, 2, NC], F32)
        n8t = pair("n8t", [P, NC], F32)
        keep = pair("keep", [P, NC], F32)
        cbias = pair("cbias", [P, NC], F32)
        csum = pair("csum", [P, NC, 2], F32)
        mnh, mnl = pair("mnh", [4, R], F16), pair("mnl", [4, R], F16)

        yTh, yTl = sb("yTh", [P, DC, N], F16), sb("yTl", [P, DC, N], F16)
        adj_sb = sb("adj_sb", [P, 2, N], I32)
        t_row = sb("t_row", [P, N], F32)
        junk = sb("junk", [P, 2, HALF], BF16)
        e1, e2 = sb("e1", [P, HC, D], F32), sb("e2", [P, HC, D], F32)
        xt = sb("xt", [P, RING, HALF], F32)
        p32 = sb("p32", [P, RING, HALF], F32)
        ph, pl = sb("ph", [P, RING, HALF], F16), sb("pl", [P, RING, HALF], F16)
        c2 = sb("c2", [P, 2, NC], F32)
        res = sb("res", [P, 2, NC], F32)
        sp = sb("sp", [P, NC, 6], BF16)
        spr = sb("spr", [P, NC, 4], BF16)
        rows = sb("rows", [6, N], BF16)
        hmax = sb("hmax", [P, 2, NC], F32)
        cmax, clk, cterm, resr = (sb(n, [P, NC], F32) for n in ("cmax", "clk", "cterm", "resr"))
        rinv = sb("rinv", [P, NC], F32)
        bst = sb("bst", [P, HC, 6], F32)
        mv = sb("mv", [P, NC, 2], F32)
        vare = sb("vare", [P, NC], F32)
        rstd = sb("rstd", [P, NC], F32)
        a_col = sb("a_col", [OUT, 2], F32)
        wa = sb("wa", [P, 4, DC], F32)

        acc = ctx.enter_context(nc.psum_tensor("acc", [P, 4, 512], F32))
        vu = ctx.enter_context(nc.psum_tensor("vu", [P, 2, 512], F32))
        misc = ctx.enter_context(nc.psum_tensor("misc", [P, 2, 512], F32))
        misc_flat = misc[:, :, :].rearrange("p a b -> p (a b)")

        def u8(m):
            return m[:, :].bitcast(U8)

        def diag_parts(m):
            n = (NC - 1) * (N + P)
            return [(m[:, 0:n].rearrange("p (c k) -> p c k", k=N + P)[:, :, 0:P], slice(0, NC - 1)),
                    (m[:, n:n + P].rearrange("p (c k) -> p c k", c=1), slice(NC - 1, NC))]

        def nodes(m, half):
            return m[:, half * HC:(half + 1) * HC, :]

        def flat(m):
            return m.rearrange("p c d -> p (c d)")

        s_load, s_dve, s_pool, s_pe, s_wload, s_wdone = (
            ctx.enter_context(nc.semaphore(f"setup_{n}")) for n in ("load", "dve", "pool", "pe", "wload", "wdone"))
        stage = flat(x_in[0][:, :, :])
        with nc.Block() as block:
            @block.sync
            def _(sp_):
                for l in range(L):
                    for k, a in enumerate((g1, beta1, b2, g2, beta2)):
                        sp_.dma_start(lnc[:, l, k, :], a[l].partition_broadcast(P)).then_inc(s_load, 16)
                    sp_.dma_start(score_v[:, l, :, :], attn_w[l].rearrange("(a d) -> a d", a=2).partition_broadcast(P)).then_inc(s_load, 16)
                    with nc.allow_non_contiguous_dma(reason="bias as columns"):
                        sp_.dma_start(b1c[:, l, :], b1[l].rearrange("(c p) -> p c", p=P)).then_inc(s_load, 16)
                sp_.dma_start(ab[:, :], attn_b.partition_broadcast(P)).then_inc(s_load, 16)
                with nc.allow_non_contiguous_dma(reason="attention vector as columns"):
                    sp_.dma_start(a_col[:, :], W_attn[0].rearrange("(a o) -> o a", a=2)).then_inc(s_load, 16)
                sp_.dma_start(e2[0:OUT, 0, :], W_fc).then_inc(s_load, 16)
                sp_.dma_start(s8_row[0][:, 0:2 * D], a0.rearrange("d o -> (d o)").partition_broadcast(P)).then_inc(s_load, 16)
                sp_.dma_start(s8_row[0][:, 2 * D:4 * D], a3.rearrange("d o -> (d o)").partition_broadcast(P)).then_inc(s_load, 16)
                for w, weight in enumerate((W0, W3)):
                    if w >= 1:
                        sp_.wait_ge(s_wdone, w)
                    sp_.dma_start(stage[:, 0:DC * D].rearrange("p (c d) -> p c d", c=DC),
                                  weight.rearrange("(c p) d -> p c d", p=P)).then_inc(s_wload, 16)

            @block.gpsimd
            def _(pool):
                pool.memset(ident_f[:, :], 0.0).then_inc(s_pool, 1)
                pool.wait_ge(s_pool, 1)
                pool.affine_select(out=ident_f[:, :], in_=ident_f[:, :], compare_op=ALU.not_equal, fill=1.0,
                                   base=0, pattern=[[-1, P]], channel_multiplier=1).then_inc(s_pool, 1)

            @block.vector
            def _(dve):
                n = [0]

                def link(ins):
                    n[0] += 1
                    ins.then_inc(s_dve, 1)
                    dve.wait_ge(s_dve, n[0])

                dve.memset(pick_s[:, :], 0.0)
                dve.memset(pick_t[:, :], 1.0)
                dve.memset(pick_r[:, :], 1.0)
                dve.memset(mean_w[:, :], 0.0)
                dve.memset(neg_half[:, :], -0.5)
                for g in range(2):
                    dve.memset(rh[g][:, :, :], 0.0)
                    dve.memset(rl[g][:, :, :], 0.0)
                dve.memset(e1[0:OUT, 0, :], 1.0)
                link(dve.memset(spr[:, :, :], 0.0))
                dve.memset(pick_s[0:3, :], 1.0)
                dve.memset(pick_t[0:3, :], 0.0)
                dve.memset(pick_r[0:1, :], 0.0)
                dve.memset(mean_w[:, 0:1], 1.0 / N)
                for g in range(2):
                    last = dve.memset(rh[g][:, :, D:D + 1], 1.0)
                link(last)
                dve.wait_ge(s_pool, 2)
                dve.tensor_copy(ident_b[:, :], ident_f[:, :])
                dve.tensor_scalar(ident_big[:, :], ident_f[:, :], -BIG, None, ALU.mult)
                dve.tensor_scalar(ident_pos[:, :], ident_f[:, :], BIG, None, ALU.mult)
                dve.tensor_copy(ident_u8[:, :], ident_f[:, :])
                dve.wait_ge(s_load, 16 * (7 * L + 5))
                for k in range(2):
                    last = dve.tensor_scalar(e1[0:OUT, 1 + k, 0:P], e1[0:OUT, 0, 0:P], a_col[:, k:k + 1], None, ALU.mult)
                link(last)
                for w in range(2):
                    dve.wait_ge(s_wload, 16 * (w + 1))
                    src = stage[:, 0:DC * D].rearrange("p (c d) -> p c d", c=DC)
                    for c in range(DC):
                        for k in range(2):
                            a_row = s8_row[0][:, (2 * w + k) * D:(2 * w + k + 1) * D]
                            i = 4 * w + 2 * c + k
                            last = dve.tensor_tensor_reduce(x_cur[0][:, i, :], src[:, c, :], a_row, 1.0, 0.0,
                                                            ALU.mult, ALU.add, wa[:, 2 * w + k, c:c + 1])
                    link(last)
                    link(dve.tensor_scalar(wgh[:, w, :, 0:D], src, WSCALE, None, ALU.mult))
                    for k in range(2):
                        link(dve.tensor_scalar(wgh[:, w, :, D + k], wa[:, 2 * w + k, :], WSCALE, None, ALU.mult))
                        dve.scalar_tensor_tensor(out=wgl[:, w, :, D + k], in0=wa[:, 2 * w + k, :], scalar=WSCALE,
                                                 in1=wgh[:, w, :, D + k], op0=ALU.mult, op1=ALU.subtract)
                    dve.scalar_tensor_tensor(out=wgl[:, w, :, 0:D], in0=src, scalar=WSCALE,
                                             in1=wgh[:, w, :, 0:D], op0=ALU.mult, op1=ALU.subtract).then_inc(s_wdone, 1)
                dve.wait_ge(s_pe, 1)
                dve.tensor_copy(score_v[:, L, :, :], acc[:, 0:2, 0:D])

            @block.tensor
            def _(pe):
                pe.wait_ge(s_dve, 3)
                for k in range(2):
                    last = pe.matmul(acc[:, k, 0:D], e1[0:OUT, 1 + k, 0:P], e2[0:OUT, 0, :], start=True, stop=True)
                last.then_inc(s_pe, 1)

        names = ("x_loaded adj_loaded_0 adj_loaded_1 w_loaded mask_made maskT_ps maskT_made diag_made tr_ps tr_hi tr_lo "
                 "wh_ps wh_hi wh_lo mean_ps mean_hi mean_lo r_hi r_lo sp_made rows_ps rows_made t_ps t_made s8_ps s8_made "
                 "spr_made rr_ps rr_made v_ps x_made p_made pl_made tile_done acc_free elu_min elu_exp var_made rstd_made "
                 "ln_made hb_made r3_made l3_copy w_in_0 w_in_1 w_hi w_lo w_out_0 w_out_1 dve_step stored").split()
        sems = [ctx.enter_context(nc.semaphore(n)) for n in names]
        (x_loaded, adj_loaded_0, adj_loaded_1, w_loaded, mask_made, maskT_ps, maskT_made, diag_made, tr_ps, tr_hi, tr_lo,
         wh_ps, wh_hi, wh_lo, mean_ps, mean_hi, mean_lo, r_hi, r_lo, sp_made, rows_ps, rows_made, t_ps, t_made, s8_ps, s8_made,
         spr_made, rr_ps, rr_made, v_ps, x_made, p_made, pl_made, tile_done, acc_free, elu_min, elu_exp, var_made, rstd_made,
         ln_made, hb_made, r3_made, l3_copy, w_in_0, w_in_1, w_hi, w_lo, w_out_0, w_out_1, dve_step, stored) = sems
        w_in, w_out = (w_in_0, w_in_1), (w_out_0, w_out_1)
        adj_loaded = (adj_loaded_0, adj_loaded_1)

        def clear_semaphores():
            nc.sync.sem_clear(range(sems[0].num, sems[-1].num + 1))
            nc.all_engine_barrier()

        def emit(in_loop, pair_no, next_pair):
            tables = {e: timetable(e, in_loop) for e in "DAPG"}

            def at(sem, *step):
                engine, signals = SIGNALS[sem.name]
                value = 0
                for _, s in tables[engine]:
                    value += signals.get(s[0], 0)
                    if s == step:
                        return value
                raise KeyError(step)

            def chunk_free(q, c):
                g, kind, i = PASSES[q]
                if (kind, i) == ("att", 5):
                    return l3_copy, at(l3_copy, "l3", g) - 3 + c
                return acc_free, at(acc_free, "take", g, kind, i, 1) - 3 + c

            score_tiles = [T for T in range(ALL_TILES) if PASSES[T // TILES][1] == "att"]

            def run(engine, tile, step):
                table = list(tables[engine])
                for T in range(ALL_TILES if in_loop else 0):
                    tile(T, *PASSES[T // TILES], T % TILES)
                    while table and table[0][0] <= T:
                        step(*table.pop(0)[1])
                for _, s in table:
                    step(*s)

            def ffn_stage(w):
                return flat(x_cur[w % 2][:, :, :])

            def where(a, n):
                return (n // 2, n % 2) if a == 5 else (n % NC, n // NC)

            def prepared(g, a):
                return g == 0 and a == 0

            with nc.Block() as block:
                @block.sync
                def _(sp_):
                    def load_adj(g, b, chunks=range(NC)):
                        for c in chunks:
                            e = at(mask_made, "mask", g, c)
                            if e > 2:
                                sp_.wait_ge(mask_made, e - 2)
                            sp_.dma_start(adj_sb[:, c % 2, :], adj[b, c * P:(c + 1) * P, :]).then_inc(adj_loaded[c % 2], 16)

                    def load_x(g, b):
                        sp_.dma_start(x_in[g % 2][:, :, :], x[b].rearrange("(c p) d -> p c d", p=P)).then_inc(x_loaded, 16)

                    def store_graph(g, b):
                        for half in range(2):
                            sp_.wait_ge(ln_made, at(ln_made, "norm", g, "att5", half))
                            sp_.dma_start(out[b, half * HALF:(half + 1) * HALF, :].rearrange("(c p) d -> p c d", p=P),
                                          nodes(x_cur[g], half)).then_inc(stored, 16)

                    if not in_loop:
                        load_x(NEXT, 0)
                        load_adj(NEXT, 0, range(2))
                        for w in range(2 * L + 2):
                            if w >= 2:
                                sp_.wait_ge(w_lo, w - 1)
                                sp_.dma_start(w_split[(w - 2) % L, 2 * ((w - 2) // L):2 * ((w - 2) // L) + 2].rearrange("k p n -> p k n"),
                                              wbuf[:, 2 * (w % 2):2 * (w % 2) + 2, :]).then_inc(w_out[w % 2], 16)
                            if w < 2 * L:
                                src, chunks = (W1[w], DC) if w < L else (W2[w - L], KC)
                                sp_.dma_start(ffn_stage(w).rearrange("p (c d) -> p c d", c=chunks),
                                              src.rearrange("(c p) d -> p c d", p=P)).then_inc(w_in[w % 2], 16)
                            if w in (1, 2, 3):
                                load_adj(NEXT, 0, (2 * w, 2 * w + 1))
                        for k in range(2):
                            sp_.wait_ge(w_out[k], 16 * L)
                        return
                    load_x(1, 2 * pair_no + 1)
                    load_adj(1, 2 * pair_no + 1)
                    for l in range(L):
                        if l >= 1:
                            sp_.wait_ge(tile_done, TILES * (pass_index(1, "ffn", l - 1) + 1))
                        for k in range(4):
                            sp_.dma_start(wbuf[:, k, :], w_split[l, k]).then_inc(w_loaded, 16)
                    load_adj(NEXT, 2 * next_pair)
                    sp_.wait_ge(r3_made, at(r3_made, "scale", 0, NC - 1))
                    sp_.wait_ge(x_loaded, 16)
                    load_x(NEXT, 2 * next_pair)
                    store_graph(0, 2 * pair_no)
                    store_graph(1, 2 * pair_no + 1)
                    sp_.wait_ge(stored, 64)

                @block.tensor
                def _(pe):
                    held = {0: None, 1: None}

                    def take_misc(bank, sem, value):
                        if held[bank]:
                            pe.wait_ge(*held[bank])
                        held[bank] = (sem, value)

                    def transpose_mask(g, c):
                        pe.wait_ge(mask_made, at(mask_made, "mask", g, c))
                        for b in range(2):
                            take_misc(b, maskT_made, at(maskT_made, "maskT", g, c) - 1 + b)
                            for j in range(HC):
                                col = c * N + (b * HC + j) * P
                                last = pe.matmul(misc[:, b, j * P:(j + 1) * P], mask[g % 2][:, col:col + P], ident_b[:, :],
                                                 start=True, stop=True)
                            last.then_inc(maskT_ps, 1)

                    def transpose_half(g, what, half):
                        if what == 0:
                            pe.wait_ge(x_loaded, 32 if in_loop and g == NEXT else 16)
                        elif what == 5:
                            pe.wait_ge(ln_made, at(ln_made, "norm", g, "att4", half))
                        else:
                            pe.wait_ge(ln_made, at(ln_made, "norm", g, f"att{int(what[3]) + 1}", half))
                        src = (x_in if what == 0 else x_cur)[g % 2]
                        for fc in range(DC):
                            take_misc(fc, tr_lo, at(tr_lo, "tr", g, what, half) - 1 + fc)
                            for c in range(HC):
                                last = pe.transpose(misc[:, fc, c * P:(c + 1) * P],
                                                    src[:, half * HC + c, fc * P:(fc + 1) * P], ident_f[:, :])
                            last.then_inc(tr_ps, 1)

                    def project(g, a, c):
                        pe.wait_ge(tr_lo, at(tr_lo, "tr", g, a, c // HC))
                        if a == 0:
                            take_misc(c % 2, wh_lo, at(wh_lo, "proj", g, a, c))
                        else:
                            take_misc(c % 2, wh_hi, at(wh_hi, "proj", g, a, c))
                        w = 0 if a == 0 else 1
                        for fc in range(DC):
                            for i, (y, wt) in enumerate([(yTh, wgh), (yTh, wgl), (yTl, wgh)]):
                                last = pe.matmul(misc[:, c % 2, 0:R], y[:, fc, c * P:(c + 1) * P], wt[:, w, fc, :],
                                                 start=(fc == 0 and i == 0), stop=(fc == DC - 1 and i == 2))
                        last.then_inc(wh_ps, 1)

                    def mean_of_r(g, a):
                        if a == 0:
                            pe.wait_ge(wh_lo, at(wh_lo, "proj", g, a, NC - 1))
                        else:
                            pe.wait_ge(r_hi, at(r_hi, "right", g, a, 1))
                            pe.wait_ge(r_lo, at(r_lo, "right", g, a, 1))
                        take_misc(0, mean_lo, at(mean_lo, "mean", g, a))
                        for c in range(NC):
                            for m in (rh, rl):
                                last = pe.matmul(misc[0:4, 0, 0:R], mean_w[:, :], m[g % 2][:, c, :],
                                                 start=(c == 0 and m is rh), stop=(c == NC - 1 and m is rl))
                        last.then_inc(mean_ps, 1)

                    def rows_of(g, a, half):
                        pe.wait_ge(sp_made, at(sp_made, "split", g, a, half))
                        take_misc(half, rows_made, at(rows_made, "rows", g, a, half))
                        for c in range(HC):
                            last = pe.matmul(misc[0:6, half, c * P:(c + 1) * P], sp[:, half * HC + c, :], ident_b[:, :],
                                             start=True, stop=True)
                        last.then_inc(rows_ps, 1)

                    def spread(name, g, a, half, pick, bank, done, made):
                        pe.wait_ge(rows_made, at(rows_made, "rows", g, a, half))
                        take_misc(bank, made, at(made, name, g, a, half))
                        pe.matmul(misc[:, bank, :], pick[:, :], rows[:, half * HALF:(half + 1) * HALF],
                                  start=True, stop=True).then_inc(done, 1)

                    def row_term(g, a):
                        pe.wait_ge(spr_made, at(spr_made, "row_term", g, a))
                        for b in range(2):
                            take_misc(b, rr_made, at(rr_made, "rr", g, a) - 1 + b)
                            for c in range(HC):
                                last = pe.matmul(misc[0:4, b, c * P:(c + 1) * P], spr[:, b * HC + c, :], ident_b[:, :],
                                                 start=True, stop=True)
                            last.then_inc(rr_ps, 1)

                    def step(name, g, *rest):
                        if name == "maskT":
                            transpose_mask(g, *rest)
                        if name == "tr":
                            transpose_half(g, *rest)
                        if name == "proj":
                            project(g, *rest)
                        if name == "mean":
                            mean_of_r(g, *rest)
                        if name == "rows":
                            rows_of(g, *rest)
                        if name == "t":
                            spread(name, g, *rest, pick_t, rest[1], t_ps, t_made)
                        if name == "s8":
                            spread(name, g, *rest, pick_s, 1 - rest[1], s8_ps, s8_made)
                        if name == "rr":
                            row_term(g, *rest)

                    def wait_bank(T):
                        if T >= 2:
                            if T - 2 in score_tiles:
                                pe.wait_ge(x_made, score_tiles.index(T - 2) + 1)
                            else:
                                pe.wait_ge(p_made, 2 * (T - 1))

                    def score_base(T, g, a, n):
                        j, half = where(a, n)
                        if not prepared(g, a):
                            if n == 0:
                                pe.wait_ge(rr_made, at(rr_made, "rr", g, a) - 1)
                                if a == 0:
                                    pe.wait_ge(maskT_made, at(maskT_made, "maskT", g, NC - 1))
                                if a == 1:
                                    pe.wait_ge(diag_made, at(diag_made, "diag", g))
                            if half == 1 and j == 0:
                                pe.wait_ge(rr_made, at(rr_made, "rr", g, a))
                        wait_bank(T)
                        pe.matmul(vu[:, T % 2, :], ident_big[:, :], maskT[g][:, j * N + half * HALF:j * N + (half + 1) * HALF],
                                  start=True, stop=False)
                        if a in (1, 2, 3) and j // HC == half:
                            k = j % HC
                            pe.matmul(vu[:, T % 2, k * P:(k + 1) * P], ident_pos[:, :], maskD[g][:, j, :], start=False, stop=False)
                        pe.matmul(vu[:, T % 2, :], pick_r[:, :], rowr[g][:, half * HALF:(half + 1) * HALF],
                                  start=False, stop=True).then_inc(v_ps, 1)

                    def wait_accumulator(T, half, c):
                        q = T // TILES
                        if half == 1:
                            pe.wait_ge(acc_free, at(acc_free, "take", *PASSES[q], 0) - 3 + c)
                        elif q > 0:
                            pe.wait_ge(*chunk_free(q - 1, c))

                    def aggregate(T, g, a, n):
                        j, half = where(a, n)
                        s = T % RING
                        if n == 0 and not prepared(g, a):
                            if a == 0:
                                pe.wait_ge(wh_lo, at(wh_lo, "proj", g, a, NC - 1))
                            else:
                                pe.wait_ge(r_hi, at(r_hi, "right", g, a, 1))
                                pe.wait_ge(r_lo, at(r_lo, "right", g, a, 1))
                        pe.wait_ge(p_made, 2 * (T + 1))
                        for c in range(HC):
                            if j == 0:
                                wait_accumulator(T, half, c)
                            for i, r in enumerate((rh, rl)):
                                pe.matmul(acc[:, c, 0:R], ph[:, s, c * P:(c + 1) * P], r[g][:, j, :],
                                          start=(j == 0 and i == 0), stop=False)
                        pe.wait_ge(pl_made, T + 1)
                        for c in range(HC):
                            last = pe.matmul(acc[:, c, 0:R], pl[:, s, c * P:(c + 1) * P], rh[g][:, j, :], start=False,
                                             stop=(j == NC - 1 and a not in (0, 4)))
                        if j == NC - 1 and a in (0, 4):
                            if half == 0 and not prepared(g, a):
                                pe.wait_ge(mean_lo, at(mean_lo, "mean", g, a))
                            for c in range(HC):
                                e_row = rowr[g][:, half * HALF + c * P:half * HALF + (c + 1) * P]
                                pe.matmul(acc[:, c, 0:R], e_row, mnh[g][:, :], start=False, stop=False)
                                last = pe.matmul(acc[:, c, 0:R], e_row, mnl[g][:, :], start=False, stop=True)
                        last.then_inc(tile_done, 1)

                    def aggregate_columns(T, g, n):
                        j, half = where(5, n)
                        s = T % RING
                        if half == 0:
                            pe.wait_ge(r3_made, at(r3_made, "scale", g, j))
                        pe.wait_ge(pl_made, T + 1)
                        for c in range(HC):
                            ic = half * HC + c
                            if j == 0 and ic % 2 == 0:
                                pe.wait_ge(*chunk_free(T // TILES - 1, ic // 2))
                            dst = acc[:, ic // 2, (ic % 2) * D:(ic % 2 + 1) * D]
                            for i, (p, r) in enumerate([(ph, rh), (ph, rl), (pl, rh)]):
                                last = pe.matmul(dst, p[:, s, c * P:(c + 1) * P], r[g][:, j, 0:D],
                                                 start=(j == 0 and i == 0 and ic % 2 == 0),
                                                 stop=(j == NC - 1 and i == 2), skip_group_check=True)
                        last.then_inc(tile_done, 1)

                    def hidden(T, g, l, n):
                        k, half = n % KC, n // KC
                        if n == 0:
                            pe.wait_ge(w_loaded, 64 * (l + 1))
                        if k == 0:
                            pe.wait_ge(tr_lo, at(tr_lo, "tr", g, f"ffn{l}", half))
                        wait_bank(T)
                        for fc in range(DC):
                            for i, (wt, y) in enumerate([(w1h, yTh), (w1h, yTl), (w1l, yTh)]):
                                last = pe.matmul(vu[:, T % 2, :], wt[:, fc, k * P:(k + 1) * P],
                                                 y[:, fc, half * HALF:(half + 1) * HALF],
                                                 start=(fc == 0 and i == 0), stop=(fc == DC - 1 and i == 2))
                        last.then_inc(v_ps, 1)

                    def contract(T, n):
                        k, half = n % KC, n // KC
                        s = T % RING
                        pe.wait_ge(p_made, 2 * (T + 1))
                        for c in range(HC):
                            if k == 0:
                                wait_accumulator(T, half, c)
                            for i, wt in enumerate((w2h, w2l)):
                                pe.matmul(acc[:, c, 0:D], ph[:, s, c * P:(c + 1) * P], wt[:, k, :],
                                          start=(k == 0 and i == 0), stop=False)
                        pe.wait_ge(pl_made, T + 1)
                        for c in range(HC):
                            last = pe.matmul(acc[:, c, 0:D], pl[:, s, c * P:(c + 1) * P], w2h[:, k, :],
                                             start=False, stop=(k == KC - 1))
                        last.then_inc(tile_done, 1)

                    begun = [0]

                    def tile(T, g, kind, i, n):
                        while begun[0] < ALL_TILES and begin_place(begun[0]) <= T:
                            B_ = begun[0]
                            bg, bkind, bi = PASSES[B_ // TILES]
                            (score_base if bkind == "att" else hidden)(B_, bg, bi, B_ % TILES)
                            begun[0] += 1
                        if kind == "ffn":
                            contract(T, n)
                        elif i == 5:
                            aggregate_columns(T, g, n)
                        else:
                            aggregate(T, g, i, n)

                    run("P", tile, step)

                @block.scalar
                def _(act):
                    def step(name, g, *rest):
                        G = g % 2
                        if name == "maskT":
                            c, = rest
                            for b in range(2):
                                act.wait_ge(maskT_ps, at(maskT_ps, "maskT", g, c) - 1 + b)
                                act.activation(u8(maskT[G]).rearrange("p (j n) -> p j n", j=NC)[:, b * HC:(b + 1) * HC, c * P:(c + 1) * P],
                                               misc[:, b, :].rearrange("p (j n) -> p j n", j=HC),
                                               ACT.Copy, scale=ONE8).then_inc(maskT_made, 1)
                        if name == "weight":
                            w, = rest
                            act.wait_ge(w_in[w % 2], 16 * (w // 2 + 1))
                            if w >= 2:
                                act.wait_ge(w_out[w % 2], 16 * (w // 2))
                            act.activation(wbuf[:, 2 * (w % 2), :], ffn_stage(w), ACT.Copy, scale=WSCALE).then_inc(w_hi, 1)
                        if name == "tr":
                            what, half = rest
                            for fc in range(DC):
                                act.wait_ge(tr_ps, at(tr_ps, "tr", g, what, half) - 1 + fc)
                                act.activation(yTh[:, fc, half * HALF:(half + 1) * HALF], misc[:, fc, :], ACT.Copy).then_inc(tr_hi, 1)
                        if name == "proj":
                            a, c = rest
                            act.wait_ge(wh_ps, at(wh_ps, "proj", g, a, c))
                            dst = rh[G][:, c, 0:D] if a == 0 else x_in[G][:, c, :]
                            act.activation(st[G][:, :, c], misc[:, c % 2, D:R], ACT.Copy, scale=1.0 / WSCALE)
                            act.activation(dst, misc[:, c % 2, 0:D], ACT.Copy, scale=1.0 / WSCALE).then_inc(wh_hi, 1)
                        if name == "right":
                            a, half = rest
                            src, norm = {1: (x_in, "att0"), 2: (x_cur, "ffn0"), 3: (x_cur, "ffn1"), 4: (x_cur, "outer")}[a]
                            act.wait_ge(ln_made, at(ln_made, "norm", g, norm, half))
                            act.activation(rh[G][:, half * HC:(half + 1) * HC, 0:D], nodes(src[G], half), ACT.Copy).then_inc(r_hi, 1)
                        if name == "rows":
                            a, half = rest
                            act.wait_ge(rows_ps, at(rows_ps, "rows", g, a, half))
                            act.activation(rows[:, half * HALF:(half + 1) * HALF], misc[0:6, half, :], ACT.Copy).then_inc(rows_made, 1)
                        if name == "t":
                            a, half = rest
                            act.wait_ge(t_ps, at(t_ps, "t", g, a, half))
                            act.activation(t_row[:, half * HALF:(half + 1) * HALF], misc[:, half, :], ACT.Copy, scale=TINY).then_inc(t_made, 1)
                        if name == "s8":
                            a, half = rest
                            hs = slice(half * HALF, (half + 1) * HALF)
                            act.wait_ge(s8_ps, at(s8_ps, "s8", g, a, half))
                            if a == 5:
                                act.activation(t_row[:, hs], misc[:, 1 - half, :], ACT.Copy, scale=TINY)
                            act.activation(s8_row[G][:, hs], misc[:, 1 - half, :], ACT.Copy).then_inc(s8_made, 1)
                        if name == "mean":
                            act.wait_ge(mean_ps, at(mean_ps, "mean", g, *rest))
                            act.activation(mnh[G][:, :], misc[0:4, 0, 0:R], ACT.Copy).then_inc(mean_hi, 1)
                        if name == "rr":
                            for b in range(2):
                                act.wait_ge(rr_ps, at(rr_ps, "rr", g, *rest) - 1 + b)
                                act.activation(rowr[G][:, b * HALF:(b + 1) * HALF], misc[0:4, b, :], ACT.Copy).then_inc(rr_made, 1)
                        if name == "elu":
                            act.wait_ge(elu_min, at(elu_min, "clip", g, *rest))
                            act.activation(e2[:, :, :], e2[:, :, :], ACT.Exp).then_inc(elu_exp, 1)
                        if name == "l3":
                            act.wait_ge(tile_done, TILES * (pass_index(g, "att", 5) + 1))
                            for b in range(4):
                                e = (e1, e2)[b // 2]
                                act.activation(flat(e[:, 2 * (b % 2):2 * (b % 2) + 2, :]), acc[:, b, :], ACT.Copy).then_inc(l3_copy, 1)

                    def tile(T, g, kind, a, n):
                        s = T % RING
                        if T >= RING:
                            act.wait_ge(tile_done, T - RING + 1)
                        if kind == "att":
                            A = score_tiles.index(T)
                            act.wait_ge(x_made, A + 1)
                            if a < 5:
                                t_j = st[g][:, 1, n % NC:n % NC + 1]
                                act.activation(p32[:, s, :], xt[:, A % RING, :], ACT.Exp, bias=t_j).then_inc(p_made, 1)
                                act.activation(ph[:, s, :], xt[:, A % RING, :], ACT.Exp, bias=t_j).then_inc(p_made, 1)
                            else:
                                j, half = n // 2, n % 2
                                bias, scale = cbias[g][:, j:j + 1], keep[g][:, j:j + 1]
                                act.activation(p32[:, s, :], xt[:, A % RING, :], ACT.Exp, bias=bias, scale=scale,
                                               accum_out=csum[g][:, j, half:half + 1]).then_inc(p_made, 1)
                                act.activation(ph[:, s, :], xt[:, A % RING, :], ACT.Exp, bias=bias, scale=scale).then_inc(p_made, 1)
                        else:
                            act.wait_ge(v_ps, T + 1)
                            bias = b1c[:, a, n % KC:n % KC + 1]
                            act.activation(p32[:, s, :], vu[:, T % 2, :], ACT.Gelu, bias=bias, scale=1.0 / WSCALE).then_inc(p_made, 1)
                            act.activation(ph[:, s, :], vu[:, T % 2, :], ACT.Gelu, bias=bias, scale=1.0 / WSCALE).then_inc(p_made, 1)

                    run("A", tile, step)

                @block.gpsimd
                def _(pool):
                    def step(name, g, *rest):
                        half = rest[-1]
                        cs = slice(half * HC, (half + 1) * HC)
                        if name == "norm":
                            pool.wait_ge(var_made, at(var_made, "stats", g, *rest))
                            pool.tensor_tensor(rstd[:, cs], vare[:, cs], neg_half[:, cs], ALU.pow).then_inc(rstd_made, 1)
                        if name == "right":
                            a = rest[0]
                            pool.wait_ge(r_hi, at(r_hi, "right", g, a, half))
                            pool.tensor_tensor(rl[g][:, cs, 0:D], nodes((x_in if a == 1 else x_cur)[g], half),
                                               rh[g][:, cs, 0:D], ALU.subtract).then_inc(r_lo, 1)
                        if name == "b2":
                            l = rest[0]
                            pool.wait_ge(tr_ps, at(tr_ps, "tr", g, f"ffn{l}", half))
                            pool.tensor_tensor(nodes(x_cur[g], half), nodes(x_cur[g], half),
                                               lnc[:, l, 2:3, :].broadcast_to([P, HC, D]), ALU.add).then_inc(hb_made, 1)

                    def tile(T, g, kind, a, n):
                        s = T % RING
                        pool.wait_ge(p_made, 2 * (T + 1))
                        pool.tensor_tensor(pl[:, s, :], p32[:, s, :], ph[:, s, :], ALU.subtract).then_inc(pl_made, 1)

                    run("G", tile, step)

                @block.vector
                def _(dve):
                    steps = [0]

                    def link(ins):
                        steps[0] += 1
                        ins.then_inc(dve_step, 1)
                        dve.wait_ge(dve_step, steps[0])

                    def lag(ins):
                        steps[0] += 1
                        ins.then_inc(dve_step, 1)
                        if steps[0] > 1:
                            dve.wait_ge(dve_step, steps[0] - 1)

                    def catch_up():
                        dve.wait_ge(dve_step, steps[0])

                    def make_mask(g, c):
                        e = at(mask_made, "mask", g, c)
                        dve.wait_ge(adj_loaded[c % 2], 16 * ((e - 1) // 2 + 1))
                        dve.tensor_scalar(u8(mask[g % 2])[:, c * N:(c + 1) * N], adj_sb[:, c % 2, :], 0, ONE8,
                                          ALU.is_le, ALU.mult).then_inc(mask_made, 1)

                    def take_diagonal(g):
                        if g == 1:
                            dve.wait_ge(maskT_made, at(maskT_made, "maskT", g, NC - 1))
                        for part, cs in diag_parts(u8(maskT[g])):
                            last = dve.tensor_tensor(maskD[g][:, cs, :].bitcast(U8), part,
                                                     ident_u8[:, :].unsqueeze(1).broadcast_to([P, cs.stop - cs.start, P]), ALU.mult)
                        last.then_inc(diag_made, 1)

                    def copy_transposed_low(g, what, half):
                        cs = slice(half * HALF, (half + 1) * HALF)
                        for fc in range(DC):
                            dve.wait_ge(tr_hi, at(tr_hi, "tr", g, what, half) - 1 + fc)
                            dve.tensor_tensor(yTl[:, fc, cs], misc[:, fc, :], yTh[:, fc, cs], ALU.subtract).then_inc(tr_lo, 1)

                    def take_projection(g, a, c):
                        G = g % 2
                        dve.wait_ge(wh_hi, at(wh_hi, "proj", g, a, c))
                        dve.scalar_tensor_tensor(out=rl[G][:, c, 0:D], in0=misc[:, c % 2, 0:D], scalar=1.0 / WSCALE,
                                                 in1=rh[G][:, c, 0:D], op0=ALU.mult, op1=ALU.subtract).then_inc(wh_lo, 1)

                    def score_columns(g, a, chunks):
                        src = x_in if a == 1 else x_cur
                        for c in chunks:
                            for k in range(2):
                                lag(dve.tensor_tensor_reduce(junk[:, k, 0:D], src[g][:, c, :], score_v[:, a - 1, k, :], 1.0, 0.0,
                                                             ALU.mult, ALU.add, st[g][:, k, c:c + 1]))
                        catch_up()

                    def split_scores(g, a, half):
                        G = g % 2
                        cs = slice(half * HC, (half + 1) * HC)
                        if a in (0, 5):
                            dve.wait_ge(wh_hi, at(wh_hi, "proj", g, a, (half + 1) * HC - 1))
                        if a in (1, 2, 3):
                            link(dve.tensor_scalar(st[G][:, 0, cs], st[G][:, 0, cs], ab[:, a - 1:a], None, ALU.add))
                        dve.tensor_scalar(c2[:, 0, cs], st[G][:, 0, cs], 1 - SLOPE, None, ALU.mult)
                        dve.tensor_scalar(n8t[G][:, cs], st[G][:, 1, cs], SLOPE - 1, None, ALU.mult)
                        link(dve.tensor_copy(c2[:, 1, cs], st[G][:, 1, cs]))
                        parts = sp[:, cs, :].rearrange("p c (v k) -> p v c k", v=2)
                        link(dve.tensor_copy(parts[:, :, :, 0], c2[:, :, cs]))
                        link(dve.tensor_tensor(res[:, :, cs], c2[:, :, cs], parts[:, :, :, 0], ALU.subtract))
                        link(dve.tensor_copy(parts[:, :, :, 1], res[:, :, cs]))
                        dve.tensor_tensor(parts[:, :, :, 2], res[:, :, cs], parts[:, :, :, 1], ALU.subtract).then_inc(sp_made, 1)

                    def maximum(g, a, half, chunks):
                        if a == 5:
                            dve.wait_ge(s8_made, at(s8_made, "s8", g, a, half))
                        else:
                            dve.wait_ge(t_made, at(t_made, "t", g, a, half))
                        m = u8((mask if a < 5 else maskT)[g % 2])
                        for c in chunks:
                            col = c * N + half * HALF
                            lag(dve.tensor_tensor_reduce(junk[:, c % 2, :], t_row[:, half * HALF:(half + 1) * HALF], m[:, col:col + HALF],
                                                         1.0, -3e38, ALU.subtract, ALU.max, hmax[:, half, c:c + 1]))

                    def split_row_term():
                        link(dve.tensor_copy(spr[:, :, 1], cterm[:, :]))
                        link(dve.tensor_tensor(resr[:, :], cterm[:, :], spr[:, :, 1], ALU.subtract))
                        link(dve.tensor_copy(spr[:, :, 2], resr[:, :]))
                        dve.tensor_tensor(spr[:, :, 3], resr[:, :], spr[:, :, 2], ALU.subtract).then_inc(spr_made, 1)

                    def leaky_maximum(G, a, other, scale):
                        catch_up()
                        link(dve.tensor_tensor(cmax[:, :], hmax[:, 0, :], hmax[:, 1, :], ALU.max))
                        if a in (1, 2, 3):
                            link(dve.scalar_tensor_tensor(out=cmax[:, :], in0=st[G][:, 1, :], scalar=TINY, in1=cmax[:, :],
                                                          op0=ALU.mult, op1=ALU.max))
                        link(dve.tensor_scalar(keep[G][:, :], cmax[:, :], -0.5, None, ALU.is_gt))
                        link(dve.scalar_tensor_tensor(out=cmax[:, :], in0=cmax[:, :], scalar=scale, in1=keep[G][:, :],
                                                      op0=ALU.mult, op1=ALU.mult))
                        link(dve.tensor_tensor(cmax[:, :], other, cmax[:, :], ALU.add))
                        link(dve.scalar_tensor_tensor(out=clk[:, :], in0=cmax[:, :], scalar=SLOPE, in1=cmax[:, :],
                                                      op0=ALU.mult, op1=ALU.max))

                    def make_row_term(g, a):
                        G = g % 2
                        s = st[G][:, 0, :]
                        if a == 5:
                            dve.memset(spr[:, :, 0], 0.0)
                            link(dve.tensor_scalar(cterm[:, :], s, SLOPE, None, ALU.mult))
                            split_row_term()
                            leaky_maximum(G, a, st[G][:, 1, :], 1 / TINY / (1 - SLOPE))
                            link(dve.tensor_tensor(clk[:, :], st[G][:, 1, :], clk[:, :], ALU.subtract))
                            link(dve.tensor_tensor(cbias[G][:, :], clk[:, :], keep[G][:, :], ALU.mult))
                            return
                        leaky_maximum(G, a, s, 1 / TINY)
                        dve.tensor_scalar(spr[:, :, 0], keep[G][:, :], 0.0, None, ALU.is_equal)
                        link(dve.scalar_tensor_tensor(out=cterm[:, :], in0=s, scalar=SLOPE, in1=clk[:, :],
                                                      op0=ALU.mult, op1=ALU.subtract))
                        split_row_term()

                    def norm_stats(g, name, half):
                        srcs = e1 if name in ("att0", "att4") else nodes(x_cur[g], half)
                        for c in range(HC):
                            last = dve.bn_stats(bst[:, c, :], srcs[:, c, :])
                        link(last)
                        for c in range(HC):
                            last = dve.bn_aggr(mv[:, half * HC + c, :], bst[:, c, :])
                        link(last)
                        cs = slice(half * HC, (half + 1) * HC)
                        dve.tensor_scalar(vare[:, cs], mv[:, cs, 1], EPS, None, ALU.add).then_inc(var_made, 1)

                    def norm_apply(g, name, half):
                        dve.wait_ge(rstd_made, at(rstd_made, "norm", g, name, half))
                        xs = nodes(x_cur[g], half)
                        if name in ("att0", "att4", "outer", "att5"):
                            src = e1 if name in ("att0", "att4") else xs
                            dst = nodes(x_in[g], half) if name == "att0" else xs
                            for c in range(HC):
                                k = half * HC + c
                                last = dve.tensor_scalar(dst[:, c, :], src[:, c, :], mv[:, k, 0:1], rstd[:, k:k + 1],
                                                         ALU.subtract, ALU.mult)
                        else:
                            l, k0 = (int(name[3]) - 1, 0) if name[:3] == "att" else (int(name[3]), 3)
                            for c in range(HC):
                                last = dve.scalar_tensor_tensor(out=xs[:, c, :], in0=xs[:, c, :], scalar=mv[:, half * HC + c, 0:1],
                                                                in1=lnc[:, l, k0, :], op0=ALU.subtract, op1=ALU.mult)
                            link(last)
                            for c in range(HC):
                                k = half * HC + c
                                last = dve.scalar_tensor_tensor(out=xs[:, c, :], in0=xs[:, c, :], scalar=rstd[:, k:k + 1],
                                                                in1=lnc[:, l, k0 + 1, :], op0=ALU.mult, op1=ALU.add)
                        last.then_inc(ln_made, 1)
                        dve.wait_ge(ln_made, at(ln_made, "norm", g, name, half))

                    def take(g, kind, i, half):
                        dve.wait_ge(tile_done, TILES * pass_index(g, kind, i) + 8 * (half + 1))
                        if kind == "att":
                            cs = slice(half * HC, (half + 1) * HC)
                            link(dve.reciprocal(rinv[:, cs], acc[:, :, D]))
                        else:
                            dve.wait_ge(hb_made, at(hb_made, "b2", g, i, half))
                        for c in range(HC):
                            k = half * HC + c
                            if kind == "ffn":
                                last = dve.scalar_tensor_tensor(out=x_cur[g][:, k, :], in0=acc[:, c, 0:D], scalar=1.0 / WSCALE,
                                                                in1=x_cur[g][:, k, :], op0=ALU.mult, op1=ALU.add)
                            elif i in (1, 2, 3):
                                last = dve.scalar_tensor_tensor(out=x_cur[g][:, k, :], in0=acc[:, c, 0:D], scalar=rinv[:, k:k + 1],
                                                                in1=(x_in if i == 1 else x_cur)[g][:, k, :],
                                                                op0=ALU.mult, op1=ALU.add)
                            else:
                                last = dve.tensor_scalar(e1[:, c, :], acc[:, c, 0:D], rinv[:, k:k + 1], None, ALU.mult)
                            last.then_inc(acc_free, 1)
                        dve.wait_ge(acc_free, at(acc_free, "take", g, kind, i, half))

                    def add_elu(g, a, half):
                        link(dve.scalar_tensor_tensor(out=flat(e1[:, :, :]), in0=flat(e1[:, :, :]), scalar=0.0,
                                                      in1=flat(nodes((x_in if a == 0 else x_cur)[g], half)), op0=ALU.max, op1=ALU.add))
                        dve.wait_ge(elu_exp, at(elu_exp, "elu", g, a, half))
                        link(dve.scalar_tensor_tensor(out=flat(e1[:, :, :]), in0=flat(e2[:, :, :]), scalar=-1.0,
                                                      in1=flat(e1[:, :, :]), op0=ALU.add, op1=ALU.add))

                    def scale_columns(g, j):
                        q = pass_index(g, "att", 5)
                        dve.wait_ge(p_made, 2 * (TILES * q + 2 * j + 2))
                        link(dve.tensor_tensor(rinv[:, j:j + 1], csum[g][:, j, 0:1], csum[g][:, j, 1:2], ALU.add))
                        link(dve.reciprocal(rinv[:, j:j + 1], rinv[:, j:j + 1]))
                        link(dve.tensor_scalar(rh[g][:, j, 0:D], x_in[g][:, j, :], rinv[:, j:j + 1], None, ALU.mult))
                        dve.scalar_tensor_tensor(out=rl[g][:, j, 0:D], in0=x_in[g][:, j, :], scalar=rinv[:, j:j + 1],
                                                 in1=rh[g][:, j, 0:D], op0=ALU.mult, op1=ALU.subtract).then_inc(r3_made, 1)

                    def step(name, g, *rest):
                        if name == "mask":
                            make_mask(g, *rest)
                        if name == "weight":
                            w, = rest
                            dve.wait_ge(w_hi, w + 1)
                            dve.scalar_tensor_tensor(out=wbuf[:, 2 * (w % 2) + 1, :], in0=ffn_stage(w), scalar=WSCALE,
                                                     in1=wbuf[:, 2 * (w % 2), :], op0=ALU.mult, op1=ALU.subtract).then_inc(w_lo, 1)
                        if name == "diag":
                            take_diagonal(g)
                        if name == "tr":
                            copy_transposed_low(g, *rest)
                        if name == "proj":
                            take_projection(g, *rest)
                        if name == "mean":
                            dve.wait_ge(mean_hi, at(mean_hi, "mean", g, *rest))
                            dve.tensor_tensor(mnl[g % 2][:, :], misc[0:4, 0, 0:R], mnh[g % 2][:, :], ALU.subtract).then_inc(mean_lo, 1)
                        if name == "cols":
                            score_columns(g, *rest)
                        if name == "split":
                            split_scores(g, *rest)
                        if name == "max":
                            maximum(g, *rest)
                        if name == "row_term":
                            make_row_term(g, *rest)
                        if name == "take":
                            take(g, *rest)
                        if name == "clip":
                            dve.tensor_scalar(flat(e2[:, :, :]), flat(e1[:, :, :]), 0.0, None, ALU.min).then_inc(elu_min, 1)
                        if name == "elu":
                            add_elu(g, *rest)
                        if name == "stats":
                            norm_stats(g, *rest)
                        if name == "norm":
                            norm_apply(g, *rest)
                        if name == "outer":
                            xs = flat(nodes(x_cur[g], rest[0]))
                            link(dve.tensor_tensor(xs, xs, flat(nodes(x_in[g], rest[0])), ALU.add))
                        if name == "scale":
                            scale_columns(g, *rest)
                        if name == "l3":
                            for half, e in enumerate((e1, e2)):
                                dve.wait_ge(l3_copy, at(l3_copy, "l3", g) - 2 + 2 * half)
                                link(dve.scalar_tensor_tensor(out=flat(e[:, :, :]), in0=flat(e[:, :, :]), scalar=SLOPE,
                                                              in1=flat(e[:, :, :]), op0=ALU.mult, op1=ALU.max))
                        if name == "l3_sum":
                            xs = flat(nodes(x_cur[g], rest[0]))
                            link(dve.tensor_tensor(xs, flat((e1, e2)[rest[0]][:, :, :]), xs, ALU.add))

                    def tile(T, g, kind, a, n):
                        if kind == "ffn":
                            return
                        A = score_tiles.index(T)
                        j, half = where(a, n)
                        dve.wait_ge(v_ps, T + 1)
                        if j == 0 and not prepared(g, a):
                            dve.wait_ge(s8_made, at(s8_made, "s8", g, a, half))
                        if A >= RING:
                            dve.wait_ge(p_made, 2 * (score_tiles[A - RING] + 1))
                        dve.scalar_tensor_tensor(out=xt[:, A % RING, :], in0=s8_row[g][:, half * HALF:(half + 1) * HALF],
                                                 scalar=n8t[g][:, j:j + 1], in1=vu[:, T % 2, :],
                                                 op0=ALU.max, op1=ALU.add).then_inc(x_made, 1)

                    run("D", tile, step)

            clear_semaphores()

        emit(False, 0, 0)
        with nc.Fori(0, B // 2) as pair_no:
            emit(True, pair_no, (pair_no + 1) % (B // 2) if B > 2 else 0)


_INS = ["x", "adj", "L0_gnn_W", "L0_gnn_a", "L1_gnn_attn_w", "L1_gnn_attn_b", "L1_gnn_W1", "L1_gnn_b1", "L1_gnn_W2",
        "L1_gnn_b2", "L1_gnn_g1", "L1_gnn_beta1", "L1_gnn_g2", "L1_gnn_beta2", "L2_gnn_W_fc", "L2_gnn_W_attn",
        "L3_gnn_W", "L3_gnn_a"]


def kernel(**inputs):
    import numpy as _np
    import concourse.bacc as _bacc
    from concourse import mybir as _mybir
    from concourse.bass_utils import run_bass_kernel_spmd as _run

    nc = _bacc.Bacc("TRN2", target_bir_lowering=False, num_devices=1)
    arrays, args = {}, []
    for name in _INS:
        a = _np.ascontiguousarray(inputs[name])
        arrays[f"in_{name}_dram"] = a
        args.append(nc.dram_tensor(f"in_{name}_dram", a.shape, _mybir.dt.from_np(a.dtype), kind="ExternalInput").ap())
    shape = inputs["x"].shape
    o = nc.dram_tensor("out_0_dram", shape, _mybir.dt.float32, kind="ExternalOutput").ap()
    build(nc, *args, o)
    r = _run(nc, [arrays], core_ids=[0])
    return r.results[0]["out_0_dram"]
```

```python
from contextlib import ExitStack

import concourse.bass as bass
from concourse import mybir

ALU = mybir.AluOpType
ACT = mybir.ActivationFunctionType
F32 = mybir.dt.float32
F16 = mybir.dt.float16
BF16 = mybir.dt.bfloat16
FP8 = mybir.dt.float8e4
I32 = mybir.dt.int32
U8 = mybir.dt.uint8

P = 128
BIG = float(2.0 ** 100)
ONE8 = 56.0
TINY = float(2.0 ** -60)
WSCALE = 64.0
EPS = 1e-5
SLOPE = 0.2
TILES = 16
RING = 4
LAYERS = 3

ROUNDS = [[("att", 0)]] + [[("att", l + 1), ("ffn", l)] for l in range(LAYERS)] + [[("att", 4)], [("att", 5)]]
SLOTS = [(g, passes) for passes in ROUNDS for g in range(2)]
PASSES = [(g, kind, i) for g, passes in SLOTS for kind, i in passes]
ALL_TILES = TILES * len(PASSES)
NEXT = 2

SIGNALS = {
    "mask_made": ("D", {"mask": 1}), "maskT_ps": ("P", {"maskT": 2}), "maskT_made": ("A", {"maskT": 2}),
    "diag_made": ("D", {"diag": 1}),
    "tr_ps": ("P", {"tr": 2}), "tr_hi": ("A", {"tr": 2}), "tr_lo": ("D", {"tr": 2}),
    "wh_ps": ("P", {"proj": 1}), "wh_hi": ("A", {"proj": 1}), "wh_lo": ("G", {"proj": 1}),
    "mean_ps": ("P", {"mean": 1}), "mean_hi": ("A", {"mean": 1}), "mean_lo": ("D", {"mean": 1}),
    "r_hi": ("A", {"right": 1}), "r_lo": ("G", {"right": 1}),
    "sp_made": ("D", {"split": 1}), "rows_ps": ("P", {"rows": 1}), "rows_made": ("A", {"rows": 1}),
    "t_ps": ("P", {"t": 1}), "t_made": ("A", {"t": 1}), "s8_ps": ("P", {"s8": 1}), "s8_made": ("A", {"s8": 1}),
    "spr_made": ("D", {"row_term": 1}), "rr_ps": ("P", {"rr": 2}), "rr_made": ("A", {"rr": 2}),
    "acc_free": ("D", {"take": 4}), "elu_min": ("D", {"clip": 1}), "r3_made": ("D", {"scale": 1}),
    "elu_exp": ("A", {"elu": 1}), "hb_made": ("G", {"b2": 1}),
    "l3_copy": ("A", {"l3": 4}), "var_made": ("D", {"stats": 1}), "rstd_made": ("G", {"norm": 1}), "ln_made": ("D", {"norm": 1}),
}


PLAN = {
    "own_gat": [
        ("take", ("att", "{a}", 0), "D10"),
        ("clip", ("{a}", 0), "D10"),
        ("elu", ("{a}", 0), "D11.5 A10.5"),
        ("stats", ("att{a}", 0), "D12"),
        ("norm", ("att{a}", 0), "D14.5 G11.5"),
    ],
    "own_layer": [
        ("take", ("att", "{a}", 0), "D10"),
        ("stats", ("att{a}", 0), "D10"),
        ("norm", ("att{a}", 0), "D12 G10"),
        ("take", ("att", "{a}", 1), "D17"),
        ("stats", ("att{a}", 1), "D18"),
        ("norm", ("att{a}", 1), "D20 G18"),
        ("tr", ("ffn{l}", 0), "D15 A15 P12"),
        ("tr", ("ffn{l}", 1), "D21 A21 P18"),
        ("b2", ("{l}", 0), "G18"),
        ("b2", ("{l}", 1), "G22"),
        ("take", ("ffn", "{l}", 0), "D24"),
        ("stats", ("ffn{l}", 0), "D25"),
        ("norm", ("ffn{l}", 0), "D26 G25"),
    ],
    "own_last_layer": [
        ("take", ("att", "{a}", 0), "D7.5"),
        ("stats", ("att{a}", 0), "D10"),
        ("norm", ("att{a}", 0), "D12 G10"),
        ("take", ("att", "{a}", 1), "D18"),
        ("stats", ("att{a}", 1), "D18.5"),
        ("norm", ("att{a}", 1), "D19 G17"),
        ("tr", ("ffn{l}", 0), "D14 A12 P11"),
        ("tr", ("ffn{l}", 1), "D21 A21 P18"),
        ("b2", ("{l}", 0), "G17"),
        ("b2", ("{l}", 1), "G21.5"),
        ("take", ("ffn", "{l}", 0), "D25"),
        ("stats", ("ffn{l}", 0), "D27"),
        ("norm", ("ffn{l}", 0), "D28 G27"),
        ("outer", (0,), "D30"),
        ("stats", ("outer", 0), "D30"),
        ("norm", ("outer", 0), "D32 G30"),
    ],
    "own_columns": [
        ("scale", (0,), "D2"),
        ("scale", (1,), "D4"),
        ("scale", (2,), "D6"),
        ("scale", (3,), "D8"),
        ("scale", (4,), "D10"),
        ("scale", (5,), "D12"),
        ("scale", (6,), "D14"),
        ("scale", (7,), "D15"),
    ],
    "slot_0": [
        ("mask", (0,), "D0"),
        ("mask", (1,), "D1"),
        ("mask", (2,), "D2"),
        ("mask", (3,), "D3.5"),
        ("mask", (4,), "D4"),
        ("mask", (5,), "D5"),
        ("mask", (6,), "D6"),
        ("mask", (7,), "D7"),
        ("maskT", (0,), "A1 P0"),
        ("maskT", (1,), "A5 P2"),
        ("maskT", (2,), "A6 P3"),
        ("maskT", (3,), "A7 P4"),
        ("maskT", (4,), "A8 P5"),
        ("maskT", (5,), "A9 P6"),
        ("maskT", (6,), "A10 P7"),
        ("maskT", (7,), "A11 P8"),
        ("tr", (0, 0), "D4 A4 P1"),
        ("tr", (0, 1), "D4 A4 P1"),
        ("proj", (0, 0), "G7 A7 P4"),
        ("proj", (0, 1), "G7 A7 P4"),
        ("proj", (0, 2), "G8 A8 P5"),
        ("proj", (0, 3), "G8 A8 P5"),
        ("proj", (0, 4), "G10 A10 P7"),
        ("proj", (0, 5), "G10 A10 P7"),
        ("proj", (0, 6), "G11 A11 P8"),
        ("proj", (0, 7), "G11 A11 P8"),
        ("split", (0, 0), "D8.5"),
        ("rows", (0, 0), "A10 P7"),
        ("t", (0, 0), "A12 P9"),
        ("s8", (0, 0), "A12 P9"),
        ("max", (0, 0, (0, 1)), "D12"),
        ("max", (0, 0, (2, 3)), "D12"),
        ("max", (0, 0, (4, 5)), "D12"),
        ("max", (0, 0, (6, 7)), "D12.5"),
        ("split", (0, 1), "D11"),
        ("rows", (0, 1), "A12 P10"),
        ("t", (0, 1), "A13 P11"),
        ("s8", (0, 1), "A13 P11"),
        ("max", (0, 1, (0, 1)), "D13"),
        ("max", (0, 1, (2, 3)), "D13"),
        ("max", (0, 1, (4, 5)), "D14"),
        ("max", (0, 1, (6, 7)), "D14"),
        ("row_term", (0,), "D15"),
        ("mean", (0,), "D15 A15 P12"),
        ("rr", (0,), "A15 P13"),
    ],
    "slot_1": [
        ("take", ("att", 0, 1), "D2"),
        ("clip", (0, 1), "D2"),
        ("elu", (0, 1), "D4 A3"),
        ("stats", ("att0", 1), "D4.5"),
        ("norm", ("att0", 1), "D6 G4"),
        ("cols", (1, (0, 1)), "D0"),
        ("cols", (1, (2, 3)), "D0"),
        ("right", (1, 0), "A1 G4"),
        ("cols", (1, (4, 5)), "D6"),
        ("cols", (1, (6, 7)), "D6"),
        ("right", (1, 1), "A8 G9"),
        ("diag", (), "D0"),
        ("split", (1, 0), "D2"),
        ("rows", (1, 0), "A5 P2"),
        ("t", (1, 0), "A7 P4"),
        ("s8", (1, 0), "A7 P4"),
        ("max", (1, 0, (0, 1)), "D9"),
        ("max", (1, 0, (2, 3)), "D9"),
        ("max", (1, 0, (4, 5)), "D9"),
        ("max", (1, 0, (6, 7)), "D12.5"),
        ("split", (1, 1), "D7"),
        ("rows", (1, 1), "A10 P7"),
        ("t", (1, 1), "A11.5 P8.5"),
        ("s8", (1, 1), "A12 P9"),
        ("max", (1, 1, (0, 1)), "D12"),
        ("max", (1, 1, (2,)), "D12"),
        ("max", (1, 1, (3, 4)), "D12"),
        ("max", (1, 1, (5,)), "D12"),
        ("max", (1, 1, (6, 7)), "D13"),
        ("row_term", (1,), "D13"),
        ("rr", (1,), "A14 P12"),
    ],
    "slot_2": [
        ("take", ("att", 0, 1), "D2"),
        ("clip", (0, 1), "D2.5"),
        ("elu", (0, 1), "D4 A3"),
        ("stats", ("att0", 1), "D4.5"),
        ("norm", ("att0", 1), "D6 G4"),
        ("cols", (1, (0, 1)), "D14"),
        ("cols", (1, (2, 3)), "D14"),
        ("right", (1, 0), "A16 G19"),
        ("cols", (1, (4, 5)), "D16"),
        ("cols", (1, (6, 7)), "D16"),
        ("right", (1, 1), "A18 G21"),
        ("diag", (), "D17"),
        ("split", (1, 0), "D15"),
        ("rows", (1, 0), "A19 P17"),
        ("t", (1, 0), "A22 P20"),
        ("s8", (1, 0), "A22 P20"),
        ("max", (1, 0, (0, 1)), "D24"),
        ("max", (1, 0, (2, 3)), "D22"),
        ("max", (1, 0, (4, 5)), "D22"),
        ("max", (1, 0, (6, 7)), "D22"),
        ("split", (1, 1), "D16"),
        ("rows", (1, 1), "A19 P17"),
        ("t", (1, 1), "A23 P21"),
        ("s8", (1, 1), "A26 P24"),
        ("max", (1, 1, (0, 1)), "D22"),
        ("max", (1, 1, (2, 3)), "D27"),
        ("max", (1, 1, (4, 5)), "D27"),
        ("max", (1, 1, (6, 7)), "D24"),
        ("row_term", (1,), "D27.5"),
        ("rr", (1,), "A30 P28"),
    ],
    "slots_3_to_6": [
        ("take", ("ffn", "{l}", 1), "D2"),
        ("stats", ("ffn{l}", 1), "D2"),
        ("norm", ("ffn{l}", 1), "D5 G2"),
        ("cols", ("{a}", (0, 1)), "D14"),
        ("cols", ("{a}", (2, 3)), "D14"),
        ("right", ("{a}", 0), "A17 G22"),
        ("cols", ("{a}", (4, 5)), "D16"),
        ("cols", ("{a}", (6, 7)), "D16"),
        ("right", ("{a}", 1), "A18 G21"),
        ("split", ("{a}", 0), "D14.5"),
        ("rows", ("{a}", 0), "A21 P18.5"),
        ("t", ("{a}", 0), "A22 P19.5"),
        ("s8", ("{a}", 0), "A24 P20"),
        ("max", ("{a}", 0, (0, 1)), "D22"),
        ("max", ("{a}", 0, (2, 3)), "D23"),
        ("max", ("{a}", 0, (4, 5)), "D22"),
        ("max", ("{a}", 0, (6, 7)), "D21"),
        ("split", ("{a}", 1), "D16"),
        ("rows", ("{a}", 1), "A19 P17"),
        ("t", ("{a}", 1), "A24 P22"),
        ("s8", ("{a}", 1), "A24 P22"),
        ("max", ("{a}", 1, (0, 1)), "D23.5"),
        ("max", ("{a}", 1, (2, 3)), "D25.5"),
        ("max", ("{a}", 1, (4, 5)), "D25.5"),
        ("max", ("{a}", 1, (6, 7)), "D25.5"),
        ("row_term", ("{a}",), "D25.5"),
        ("rr", ("{a}",), "A29 P26.5"),
    ],
    "slot_7": [
        ("take", ("ffn", 2, 1), "D2"),
        ("stats", ("ffn2", 1), "D2"),
        ("norm", ("ffn2", 1), "D4 G2"),
        ("outer", (1,), "D4"),
        ("stats", ("outer", 1), "D4"),
        ("norm", ("outer", 1), "D6 G4"),
        ("cols", (4, (0, 1)), "D14"),
        ("cols", (4, (2, 3)), "D14.5"),
        ("right", (4, 0), "A17 G20"),
        ("cols", (4, (4, 5)), "D16"),
        ("cols", (4, (6, 7)), "D16"),
        ("right", (4, 1), "A18 G21"),
        ("split", (4, 0), "D15"),
        ("rows", (4, 0), "A19 P16"),
        ("t", (4, 0), "A21 P19"),
        ("s8", (4, 0), "A21 P19"),
        ("max", (4, 0, (0, 1)), "D21"),
        ("max", (4, 0, (2, 3)), "D21"),
        ("max", (4, 0, (4, 5)), "D21"),
        ("max", (4, 0, (6, 7)), "D21"),
        ("split", (4, 1), "D16"),
        ("rows", (4, 1), "A19 P17"),
        ("t", (4, 1), "A22 P20"),
        ("s8", (4, 1), "A23 P21"),
        ("max", (4, 1, (0, 1)), "D24"),
        ("max", (4, 1, (2, 3)), "D24"),
        ("max", (4, 1, (4, 5)), "D23"),
        ("max", (4, 1, (6, 7)), "D24"),
        ("row_term", (4,), "D24"),
        ("mean", (4,), "D24 A25 P22"),
        ("rr", (4,), "A25 P23"),
        ("mask>", (0,), "D24"),
        ("mask>", (1,), "D26"),
        ("mask>", (2,), "D27"),
        ("mask>", (3,), "D27"),
        ("mask>", (4,), "D28"),
        ("mask>", (5,), "D29"),
        ("mask>", (6,), "D30"),
        ("mask>", (7,), "D31"),
    ],
    "slot_8": [
        ("take", ("ffn", 2, 1), "D2"),
        ("stats", ("ffn2", 1), "D2"),
        ("norm", ("ffn2", 1), "D4 G2"),
        ("outer", (1,), "D4"),
        ("stats", ("outer", 1), "D4"),
        ("norm", ("outer", 1), "D6 G4"),
        ("cols", (4, (0, 1)), "D0"),
        ("cols", (4, (2, 3)), "D0"),
        ("right", (4, 0), "A1 G2"),
        ("cols", (4, (4, 5)), "D6"),
        ("cols", (4, (6, 7)), "D7"),
        ("right", (4, 1), "A6 G10"),
        ("split", (4, 0), "D1"),
        ("rows", (4, 0), "A5 P2"),
        ("t", (4, 0), "A7 P4"),
        ("s8", (4, 0), "A7.5 P4.5"),
        ("max", (4, 0, (0, 1)), "D8"),
        ("max", (4, 0, (2, 3)), "D8"),
        ("max", (4, 0, (4, 5)), "D9"),
        ("max", (4, 0, (6, 7)), "D8"),
        ("split", (4, 1), "D8"),
        ("rows", (4, 1), "A10 P7"),
        ("t", (4, 1), "A12 P9"),
        ("s8", (4, 1), "A12 P9"),
        ("max", (4, 1, (0, 1)), "D12"),
        ("max", (4, 1, (2,)), "D12"),
        ("max", (4, 1, (3, 4)), "D13"),
        ("max", (4, 1, (5,)), "D13"),
        ("max", (4, 1, (6, 7)), "D14"),
        ("row_term", (4,), "D14"),
        ("mean", (4,), "D13 A13 P10"),
        ("rr", (4,), "A15 P13"),
    ],
    "slot_9": [
        ("take", ("att", 4, 1), "D2"),
        ("clip", (4, 1), "D3"),
        ("elu", (4, 1), "D4 A3"),
        ("stats", ("att4", 1), "D4"),
        ("norm", ("att4", 1), "D6 G4"),
        ("tr", (5, 0), "D4 A4 P1"),
        ("tr", (5, 1), "D9 A9 P6"),
        ("proj", (5, 0), "A5.5 P2.5"),
        ("proj", (5, 1), "A6 P3"),
        ("proj", (5, 2), "A7 P4"),
        ("proj", (5, 3), "A7 P4"),
        ("proj", (5, 4), "A10.5 P7.5"),
        ("proj", (5, 5), "A10 P7"),
        ("proj", (5, 6), "A11 P8"),
        ("proj", (5, 7), "A11 P8"),
        ("split", (5, 0), "D8"),
        ("rows", (5, 0), "A10 P7"),
        ("s8", (5, 0), "A10 P7"),
        ("max", (5, 0, (0, 1)), "D11"),
        ("max", (5, 0, (2, 3)), "D11"),
        ("max", (5, 0, (4, 5)), "D13"),
        ("max", (5, 0, (6, 7)), "D14"),
        ("split", (5, 1), "D11"),
        ("rows", (5, 1), "A12 P10"),
        ("s8", (5, 1), "A13 P11"),
        ("max", (5, 1, (0, 1)), "D13"),
        ("max", (5, 1, (2, 3)), "D13"),
        ("max", (5, 1, (4, 5)), "D14"),
        ("max", (5, 1, (6, 7)), "D13.5"),
        ("row_term", (5,), "D14"),
        ("rr", (5,), "A14 P13"),
    ],
    "slot_10": [
        ("take", ("att", 4, 1), "D3"),
        ("clip", (4, 1), "D3"),
        ("elu", (4, 1), "D4 A3"),
        ("stats", ("att4", 1), "D5"),
        ("norm", ("att4", 1), "D7 G5"),
        ("tr", (5, 0), "D5 A5 P2"),
        ("tr", (5, 1), "D9 A9 P6"),
        ("proj", (5, 0), "A7 P4"),
        ("proj", (5, 1), "A6 P3"),
        ("proj", (5, 2), "A6 P3"),
        ("proj", (5, 3), "A7 P4"),
        ("proj", (5, 4), "A9 P7"),
        ("proj", (5, 5), "A10 P7"),
        ("proj", (5, 6), "A10 P7"),
        ("proj", (5, 7), "A11 P8"),
        ("split", (5, 0), "D7"),
        ("rows", (5, 0), "A10 P7"),
        ("s8", (5, 0), "A11 P8"),
        ("max", (5, 0, (0, 1)), "D11"),
        ("max", (5, 0, (2, 3)), "D11"),
        ("max", (5, 0, (4, 5)), "D14"),
        ("max", (5, 0, (6, 7)), "D12"),
        ("split", (5, 1), "D11"),
        ("rows", (5, 1), "A11 P9"),
        ("s8", (5, 1), "A12 P10"),
        ("max", (5, 1, (0, 1)), "D13"),
        ("max", (5, 1, (2, 3)), "D13"),
        ("max", (5, 1, (4, 5)), "D14"),
        ("max", (5, 1, (6, 7)), "D14"),
        ("row_term", (5,), "D14"),
        ("rr", (5,), "A15 P13"),
    ],
    "slot_11": [
        ("l3", (), "D3 A2"),
        ("l3_sum", (0,), "D4"),
        ("stats", ("att5", 0), "D4"),
        ("norm", ("att5", 0), "D6 G4"),
        ("l3_sum", (1,), "D5"),
        ("stats", ("att5", 1), "D5"),
        ("norm", ("att5", 1), "D7 G4"),
        ("maskT", (0,), "A4 P1"),
        ("maskT", (1,), "A5 P2"),
        ("maskT", (2,), "A6 P3"),
        ("maskT", (3,), "A6 P3"),
        ("maskT", (4,), "A7 P4"),
        ("maskT", (5,), "A8 P5"),
        ("maskT", (6,), "A9 P6"),
        ("maskT", (7,), "A10 P7"),
        ("tr", (0, 0), "D3 A3 P0"),
        ("tr", (0, 1), "D5 A5 P2"),
        ("proj", (0, 0), "G6.5 A6.5 P3.5"),
        ("proj", (0, 1), "G6.5 A6.5 P3.5"),
        ("proj", (0, 2), "G7.5 A7.5 P4.5"),
        ("proj", (0, 3), "G7.5 A7.5 P4.5"),
        ("proj", (0, 4), "G10 A10 P7"),
        ("proj", (0, 5), "G10 A10 P7"),
        ("proj", (0, 6), "A11 P8 G10"),
        ("proj", (0, 7), "G11 A11 P8"),
        ("split", (0, 0), "D8"),
        ("rows", (0, 0), "A10 P7"),
        ("t", (0, 0), "A11 P8"),
        ("s8", (0, 0), "A11 P8"),
        ("max", (0, 0, (0, 1)), "D11"),
        ("max", (0, 0, (2, 3)), "D13"),
        ("max", (0, 0, (4, 5)), "D12"),
        ("max", (0, 0, (6, 7)), "D12"),
        ("split", (0, 1), "D11"),
        ("rows", (0, 1), "A12 P10"),
        ("t", (0, 1), "A12 P11"),
        ("s8", (0, 1), "A13 P11"),
        ("max", (0, 1, (0, 1)), "D13"),
        ("max", (0, 1, (2, 3)), "D13"),
        ("max", (0, 1, (4, 5)), "D14"),
        ("max", (0, 1, (6, 7)), "D13.5"),
        ("row_term", (0,), "D14"),
        ("mean", (0,), "D14.5 A15 P12"),
        ("rr", (0,), "A15 P13"),
    ],
    "tail": [
        ("l3", (), "D3 A3"),
        ("l3_sum", (0,), "D4"),
        ("stats", ("att5", 0), "D4"),
        ("norm", ("att5", 0), "D6 G4"),
        ("l3_sum", (1,), "D5"),
        ("stats", ("att5", 1), "D5.5"),
        ("norm", ("att5", 1), "D7 G5"),
    ],
}


def planned(name, g, **which):
    def fill(x):
        if not isinstance(x, str):
            return x
        x = x.format(**which)
        return int(x) if x.isdigit() else x

    steps = []
    for step, rest, places in PLAN[name]:
        ahead = step.endswith(">")
        steps.append(((step.rstrip(">"), NEXT if ahead else g, *(fill(x) for x in rest)),
                      {p[0]: float(p[1:]) for p in places.split()}))
    return steps


def foreground(k):
    g, passes = SLOTS[k]
    a = passes[0][1]
    if len(passes) == 2:
        return planned("own_last_layer" if a == LAYERS else "own_layer", g, a=a, l=a - 1)
    return planned("own_columns" if a == 5 else "own_gat", g, a=a)


def background(k):
    g = 1 - SLOTS[k][0]
    if 3 <= k <= 6:
        return planned("slots_3_to_6", g, a=(k - 1) // 2 + 1, l=(k - 3) // 2)
    if k == len(SLOTS) - 1:
        return [((s[0], NEXT if s[0] in AHEAD else g, *s[2:]), at_) for s, at_ in planned("slot_11", g)]
    return planned(f"slot_{k}", g)


AHEAD = ("maskT", "tr", "proj", "split", "rows", "t", "s8", "max", "row_term", "mean", "rr")


def timetable(engine, in_loop):
    if not in_loop:
        steps = []
        for c in range(8):
            steps += [("mask", NEXT, c), ("maskT", NEXT, c)]
            if c in (3, 5, 7):
                steps.append(("weight", NEXT, (c - 3) // 2))
        for half in range(2):
            steps += [("tr", NEXT, 0, half)] + [("proj", NEXT, 0, c) for c in range(4 * half, 4 * half + 4)]
            steps.append(("weight", NEXT, 3 + half))
        steps += [x for half in range(2) for x in (("split", NEXT, 0, half), ("rows", NEXT, 0, half), ("t", NEXT, 0, half),
                                                   ("s8", NEXT, 0, half), ("max", NEXT, 0, half, tuple(range(8))))]
        steps += [("row_term", NEXT, 0), ("mean", NEXT, 0), ("rr", NEXT, 0), ("weight", NEXT, 2 * LAYERS - 1)]
        parts = {"weight": "AD", "mask": "D", "maskT": "PA", "tr": "PAD", "proj": "PAG", "split": "D", "rows": "PA",
                 "t": "PA", "s8": "PA", "max": "D", "row_term": "D", "mean": "PAD", "rr": "PA"}
        return [(0, s) for s in steps if engine in parts[s[0]]]
    table, start = [], 0
    for k, (g, passes) in enumerate(SLOTS):
        table += [(start + at_[engine], s) for s, at_ in foreground(k) + background(k) if engine in at_]
        start += TILES * len(passes)
    table += [(start + at_[engine], s) for s, at_ in planned("tail", 1) if engine in at_]
    return sorted(table, key=lambda entry: entry[0])


def pass_index(g, kind, i):
    return PASSES.index((g, kind, i))


def begin_place(T):
    _, kind, i = PASSES[T // TILES]
    n = T % TILES
    if T < 3:
        return 0
    if kind == "ffn":
        return T - (FFN_AHEAD[n] if n < len(FFN_AHEAD) else 3)
    if i == 5:
        return T - (COLUMNS_AHEAD[n] if n < len(COLUMNS_AHEAD) else 3)
    short = len(SLOTS[slot_of(T - n - 1)][1]) == 1
    ahead = SHORT_AHEAD if short else LONG_AHEAD
    return T - (ahead[n] if n < len(ahead) else 3)


FFN_AHEAD = (1, 1, 2, 2)
COLUMNS_AHEAD = (2,)
LONG_AHEAD = (3,)
SHORT_AHEAD = (1, 2)


def slot_of(T):
    start = 0
    for k, (_, passes) in enumerate(SLOTS):
        start += TILES * len(passes)
        if T < start:
            return k
    raise ValueError(T)



def build(nc, x, adj, W0, a0, attn_w, attn_b, W1, b1, W2, b2, g1, beta1, g2, beta2, W_fc, W_attn, W3, a3, out):
    B, N, D = x.shape
    NC, DC, HALF = N // P, D // P, N // 2
    HC = NC // 2
    L, H = b1.shape
    KC = H // P
    OUT = W_fc.shape[0]
    R = D + 2
    assert (NC, HC * P, KC, L, B % 2) == (8, HALF, 8, LAYERS, 0)

    ctx = ExitStack()
    with ctx:
        def sb(name, shape, dt):
            return ctx.enter_context(nc.sbuf_tensor(name, shape, dt))

        ident_f = sb("ident_f", [P, P], F32)
        ident_b = sb("ident_b", [P, P], BF16)
        ident_big = sb("ident_big", [P, P], BF16)
        ident_pos = sb("ident_pos", [P, P], BF16)
        ident_u8 = sb("ident_u8", [P, P], U8)
        pick_s = sb("pick_s", [6, P], BF16)
        pick_t = sb("pick_t", [6, P], BF16)
        pick_r = sb("pick_r", [4, P], BF16)
        mean_w = sb("mean_w", [P, 4], F16)
        neg_half = sb("neg_half", [P, NC], F32)
        wbuf = sb("wbuf", [P, 4, DC * H], F16)
        w1h, w1l = (wbuf[:, k, :].rearrange("p (c d) -> p c d", c=DC) for k in range(2))
        w2h, w2l = (wbuf[:, k, :].rearrange("p (c d) -> p c d", c=KC) for k in range(2, 4))
        wgh, wgl = sb("wgh", [P, 2, DC, R], F16), sb("wgl", [P, 2, DC, R], F16)
        b1c = sb("b1c", [P, L, KC], F32)
        score_v = sb("score_v", [P, L + 1, 2, D], F32)
        ab = sb("attn_bias", [P, L], F32)
        lnc = sb("ln_const", [P, L, 5, D], F32)
        w_split = nc.dram_tensor("w_split", [L, 4, P, DC * H], F16, kind="Internal").ap()

        def pair(name, shape, dt):
            return [sb(f"{name}{g}", shape, dt) for g in range(2)]

        x_cur, x_in = pair("x_cur", [P, NC, D], F32), pair("x_in", [P, NC, D], F32)
        rh, rl = pair("rh", [P, NC, R], F16), pair("rl", [P, NC, R], F16)
        mask = pair("mask", [P, NC * N], FP8)
        maskT = pair("maskT", [P, NC * N], FP8)
        maskD = pair("maskD", [P, NC, P], FP8)
        s8_row = pair("s8_row", [P, N], F32)
        rowr = pair("rowr", [4, N], BF16)
        st = pair("st", [P, 2, NC], F32)
        n8t = pair("n8t", [P, NC], F32)
        keep = pair("keep", [P, NC], F32)
        cbias = pair("cbias", [P, NC], F32)
        csum = pair("csum", [P, NC, 2], F32)
        mnh, mnl = pair("mnh", [4, R], F16), pair("mnl", [4, R], F16)

        yTh, yTl = sb("yTh", [P, DC, N], F16), sb("yTl", [P, DC, N], F16)
        adj_sb = sb("adj_sb", [P, 2, N], I32)
        t_row = sb("t_row", [P, N], F32)
        junk = sb("junk", [P, 2, HALF], BF16)
        xw = sb("xw", [P, NC, D], F32)
        e1, e2 = sb("e1", [P, HC, D], F32), sb("e2", [P, HC, D], F32)
        xt = sb("xt", [P, RING, HALF], F32)
        p32 = sb("p32", [P, RING, HALF], F32)
        ph, pl = sb("ph", [P, RING, HALF], F16), sb("pl", [P, RING, HALF], F16)
        c2 = sb("c2", [P, 2, NC], F32)
        res = sb("res", [P, 2, NC], F32)
        sp = sb("sp", [P, NC, 6], BF16)
        spr = sb("spr", [P, NC, 4], BF16)
        rows = sb("rows", [6, N], BF16)
        hmax = sb("hmax", [P, 2, NC], F32)
        cmax, clk, cterm, resr = (sb(n, [P, NC], F32) for n in ("cmax", "clk", "cterm", "resr"))
        rinv = sb("rinv", [P, NC], F32)
        bst = sb("bst", [P, HC, 6], F32)
        mv = sb("mv", [P, NC, 2], F32)
        vare = sb("vare", [P, NC], F32)
        rstd = sb("rstd", [P, NC], F32)
        a_col = sb("a_col", [OUT, 2], F32)
        wa = sb("wa", [P, 4, DC], F32)

        acc = ctx.enter_context(nc.psum_tensor("acc", [P, 4, 512], F32))
        vu = ctx.enter_context(nc.psum_tensor("vu", [P, 2, 512], F32))
        misc = ctx.enter_context(nc.psum_tensor("misc", [P, 2, 512], F32))
        misc_flat = misc[:, :, :].rearrange("p a b -> p (a b)")

        def u8(m):
            return m[:, :].bitcast(U8)

        def diag_parts(m):
            n = (NC - 1) * (N + P)
            return [(m[:, 0:n].rearrange("p (c k) -> p c k", k=N + P)[:, :, 0:P], slice(0, NC - 1)),
                    (m[:, n:n + P].rearrange("p (c k) -> p c k", c=1), slice(NC - 1, NC))]

        def nodes(m, half):
            return m[:, half * HC:(half + 1) * HC, :]

        def flat(m):
            return m.rearrange("p c d -> p (c d)")

        s_load, s_dve, s_pool, s_pe, s_wload, s_wdone = (
            ctx.enter_context(nc.semaphore(f"setup_{n}")) for n in ("load", "dve", "pool", "pe", "wload", "wdone"))
        stage = flat(x_in[0][:, :, :])
        with nc.Block() as block:
            @block.sync
            def _(sp_):
                for l in range(L):
                    for k, a in enumerate((g1, beta1, b2, g2, beta2)):
                        sp_.dma_start(lnc[:, l, k, :], a[l].partition_broadcast(P)).then_inc(s_load, 16)
                    sp_.dma_start(score_v[:, l, :, :], attn_w[l].rearrange("(a d) -> a d", a=2).partition_broadcast(P)).then_inc(s_load, 16)
                    with nc.allow_non_contiguous_dma(reason="bias as columns"):
                        sp_.dma_start(b1c[:, l, :], b1[l].rearrange("(c p) -> p c", p=P)).then_inc(s_load, 16)
                sp_.dma_start(ab[:, :], attn_b.partition_broadcast(P)).then_inc(s_load, 16)
                with nc.allow_non_contiguous_dma(reason="attention vector as columns"):
                    sp_.dma_start(a_col[:, :], W_attn[0].rearrange("(a o) -> o a", a=2)).then_inc(s_load, 16)
                sp_.dma_start(e2[0:OUT, 0, :], W_fc).then_inc(s_load, 16)
                sp_.dma_start(s8_row[0][:, 0:2 * D], a0.rearrange("d o -> (d o)").partition_broadcast(P)).then_inc(s_load, 16)
                sp_.dma_start(s8_row[0][:, 2 * D:4 * D], a3.rearrange("d o -> (d o)").partition_broadcast(P)).then_inc(s_load, 16)
                for w, weight in enumerate((W0, W3)):
                    if w >= 1:
                        sp_.wait_ge(s_wdone, w)
                    sp_.dma_start(stage[:, 0:DC * D].rearrange("p (c d) -> p c d", c=DC),
                                  weight.rearrange("(c p) d -> p c d", p=P)).then_inc(s_wload, 16)

            @block.gpsimd
            def _(pool):
                pool.memset(ident_f[:, :], 0.0).then_inc(s_pool, 1)
                pool.wait_ge(s_pool, 1)
                pool.affine_select(out=ident_f[:, :], in_=ident_f[:, :], compare_op=ALU.not_equal, fill=1.0,
                                   base=0, pattern=[[-1, P]], channel_multiplier=1).then_inc(s_pool, 1)

            @block.vector
            def _(dve):
                n = [0]

                def link(ins):
                    n[0] += 1
                    ins.then_inc(s_dve, 1)
                    dve.wait_ge(s_dve, n[0])

                dve.memset(pick_s[:, :], 0.0)
                dve.memset(pick_t[:, :], 1.0)
                dve.memset(pick_r[:, :], 1.0)
                dve.memset(mean_w[:, :], 0.0)
                dve.memset(neg_half[:, :], -0.5)
                for g in range(2):
                    dve.memset(rh[g][:, :, :], 0.0)
                    dve.memset(rl[g][:, :, :], 0.0)
                dve.memset(e1[0:OUT, 0, :], 1.0)
                link(dve.memset(spr[:, :, :], 0.0))
                dve.memset(pick_s[0:3, :], 1.0)
                dve.memset(pick_t[0:3, :], 0.0)
                dve.memset(pick_r[0:1, :], 0.0)
                dve.memset(mean_w[:, 0:1], 1.0 / N)
                for g in range(2):
                    last = dve.memset(rh[g][:, :, D:D + 1], 1.0)
                link(last)
                dve.wait_ge(s_pool, 2)
                dve.tensor_copy(ident_b[:, :], ident_f[:, :])
                dve.tensor_scalar(ident_big[:, :], ident_f[:, :], -BIG, None, ALU.mult)
                dve.tensor_scalar(ident_pos[:, :], ident_f[:, :], BIG, None, ALU.mult)
                dve.tensor_copy(ident_u8[:, :], ident_f[:, :])
                dve.wait_ge(s_load, 16 * (7 * L + 5))
                for k in range(2):
                    last = dve.tensor_scalar(e1[0:OUT, 1 + k, 0:P], e1[0:OUT, 0, 0:P], a_col[:, k:k + 1], None, ALU.mult)
                link(last)
                for w in range(2):
                    dve.wait_ge(s_wload, 16 * (w + 1))
                    src = stage[:, 0:DC * D].rearrange("p (c d) -> p c d", c=DC)
                    for c in range(DC):
                        for k in range(2):
                            a_row = s8_row[0][:, (2 * w + k) * D:(2 * w + k + 1) * D]
                            i = 4 * w + 2 * c + k
                            last = dve.tensor_tensor_reduce(x_cur[0][:, i, :], src[:, c, :], a_row, 1.0, 0.0,
                                                            ALU.mult, ALU.add, wa[:, 2 * w + k, c:c + 1])
                    link(last)
                    link(dve.tensor_scalar(wgh[:, w, :, 0:D], src, WSCALE, None, ALU.mult))
                    for k in range(2):
                        link(dve.tensor_scalar(wgh[:, w, :, D + k], wa[:, 2 * w + k, :], WSCALE, None, ALU.mult))
                        dve.scalar_tensor_tensor(out=wgl[:, w, :, D + k], in0=wa[:, 2 * w + k, :], scalar=WSCALE,
                                                 in1=wgh[:, w, :, D + k], op0=ALU.mult, op1=ALU.subtract)
                    dve.scalar_tensor_tensor(out=wgl[:, w, :, 0:D], in0=src, scalar=WSCALE,
                                             in1=wgh[:, w, :, 0:D], op0=ALU.mult, op1=ALU.subtract).then_inc(s_wdone, 1)
                dve.wait_ge(s_pe, 1)
                dve.tensor_copy(score_v[:, L, :, :], acc[:, 0:2, 0:D])

            @block.tensor
            def _(pe):
                pe.wait_ge(s_dve, 3)
                for k in range(2):
                    last = pe.matmul(acc[:, k, 0:D], e1[0:OUT, 1 + k, 0:P], e2[0:OUT, 0, :], start=True, stop=True)
                last.then_inc(s_pe, 1)

        names = ("x_loaded adj_loaded_0 adj_loaded_1 w_loaded mask_made maskT_ps maskT_made diag_made tr_ps tr_hi tr_lo "
                 "wh_ps wh_hi wh_lo mean_ps mean_hi mean_lo r_hi r_lo sp_made rows_ps rows_made t_ps t_made s8_ps s8_made "
                 "spr_made rr_ps rr_made v_ps x_made p_made pl_made tile_done acc_free elu_min elu_exp var_made rstd_made "
                 "ln_made hb_made r3_made l3_copy w_in_0 w_in_1 w_hi w_lo w_out_0 w_out_1 dve_step stored").split()
        sems = [ctx.enter_context(nc.semaphore(n)) for n in names]
        (x_loaded, adj_loaded_0, adj_loaded_1, w_loaded, mask_made, maskT_ps, maskT_made, diag_made, tr_ps, tr_hi, tr_lo,
         wh_ps, wh_hi, wh_lo, mean_ps, mean_hi, mean_lo, r_hi, r_lo, sp_made, rows_ps, rows_made, t_ps, t_made, s8_ps, s8_made,
         spr_made, rr_ps, rr_made, v_ps, x_made, p_made, pl_made, tile_done, acc_free, elu_min, elu_exp, var_made, rstd_made,
         ln_made, hb_made, r3_made, l3_copy, w_in_0, w_in_1, w_hi, w_lo, w_out_0, w_out_1, dve_step, stored) = sems
        w_in, w_out = (w_in_0, w_in_1), (w_out_0, w_out_1)
        adj_loaded = (adj_loaded_0, adj_loaded_1)

        def clear_semaphores():
            nc.sync.sem_clear(range(sems[0].num, sems[-1].num + 1))
            nc.all_engine_barrier()

        def emit(in_loop, pair_no, next_pair):
            tables = {e: timetable(e, in_loop) for e in "DAPG"}

            def at(sem, *step):
                engine, signals = SIGNALS[sem.name]
                value = 0
                for _, s in tables[engine]:
                    value += signals.get(s[0], 0)
                    if s == step:
                        return value
                raise KeyError(step)

            def chunk_free(q, c):
                g, kind, i = PASSES[q]
                if (kind, i) == ("att", 5):
                    return l3_copy, at(l3_copy, "l3", g) - 3 + c
                return acc_free, at(acc_free, "take", g, kind, i, 1) - 3 + c

            score_tiles = [T for T in range(ALL_TILES) if PASSES[T // TILES][1] == "att"]

            def run(engine, tile, step):
                if in_loop:
                    for T in range(ALL_TILES):
                        tile(T, *PASSES[T // TILES], T % TILES)
                        for place, s in tables[engine]:
                            if T - 1 < place <= T:
                                step(*s)
                for place, s in tables[engine]:
                    if place > ALL_TILES - 1 or not in_loop:
                        step(*s)

            def ffn_stage(w):
                return flat(x_cur[w % 2][:, :, :])

            def where(a, n):
                return (n // 2, n % 2) if a == 5 else (n % NC, n // NC)

            def prepared(g, a):
                return g == 0 and a == 0

            with nc.Block() as block:
                @block.sync
                def _(sp_):
                    def load_adj(g, b, chunks=range(NC)):
                        for c in chunks:
                            e = at(mask_made, "mask", g, c)
                            if e > 2:
                                sp_.wait_ge(mask_made, e - 2)
                            sp_.dma_start(adj_sb[:, c % 2, :], adj[b, c * P:(c + 1) * P, :]).then_inc(adj_loaded[c % 2], 16)

                    def load_x(g, b):
                        sp_.dma_start(x_in[g % 2][:, :, :], x[b].rearrange("(c p) d -> p c d", p=P)).then_inc(x_loaded, 16)

                    def store_graph(g, b):
                        for half in range(2):
                            sp_.wait_ge(ln_made, at(ln_made, "norm", g, "att5", half))
                            sp_.dma_start(out[b, half * HALF:(half + 1) * HALF, :].rearrange("(c p) d -> p c d", p=P),
                                          nodes(x_cur[g], half)).then_inc(stored, 16)

                    if not in_loop:
                        load_x(NEXT, 0)
                        load_adj(NEXT, 0, range(2))
                        for w in range(2 * L + 2):
                            if w >= 2:
                                sp_.wait_ge(w_lo, w - 1)
                                sp_.dma_start(w_split[(w - 2) % L, 2 * ((w - 2) // L):2 * ((w - 2) // L) + 2].rearrange("k p n -> p k n"),
                                              wbuf[:, 2 * (w % 2):2 * (w % 2) + 2, :]).then_inc(w_out[w % 2], 16)
                            if w < 2 * L:
                                src, chunks = (W1[w], DC) if w < L else (W2[w - L], KC)
                                sp_.dma_start(ffn_stage(w).rearrange("p (c d) -> p c d", c=chunks),
                                              src.rearrange("(c p) d -> p c d", p=P)).then_inc(w_in[w % 2], 16)
                            if w in (1, 2, 3):
                                load_adj(NEXT, 0, (2 * w, 2 * w + 1))
                        for k in range(2):
                            sp_.wait_ge(w_out[k], 16 * L)
                        return
                    load_x(1, 2 * pair_no + 1)
                    load_adj(1, 2 * pair_no + 1)
                    for l in range(L):
                        if l >= 1:
                            sp_.wait_ge(tile_done, TILES * (pass_index(1, "ffn", l - 1) + 1))
                        for k in range(4):
                            sp_.dma_start(wbuf[:, k, :], w_split[l, k]).then_inc(w_loaded, 16)
                    load_adj(NEXT, 2 * next_pair)
                    sp_.wait_ge(r3_made, at(r3_made, "scale", 0, NC - 1))
                    sp_.wait_ge(x_loaded, 16)
                    load_x(NEXT, 2 * next_pair)
                    store_graph(0, 2 * pair_no)
                    store_graph(1, 2 * pair_no + 1)
                    sp_.wait_ge(stored, 64)

                @block.tensor
                def _(pe):
                    held = {0: None, 1: None}

                    def take_misc(bank, sem, value):
                        if held[bank]:
                            pe.wait_ge(*held[bank])
                        held[bank] = (sem, value)

                    def transpose_mask(g, c):
                        pe.wait_ge(mask_made, at(mask_made, "mask", g, c))
                        for b in range(2):
                            take_misc(b, maskT_made, at(maskT_made, "maskT", g, c) - 1 + b)
                            for j in range(HC):
                                col = c * N + (b * HC + j) * P
                                last = pe.matmul(misc[:, b, j * P:(j + 1) * P], mask[g % 2][:, col:col + P], ident_b[:, :],
                                                 start=True, stop=True)
                            last.then_inc(maskT_ps, 1)

                    def transpose_half(g, what, half):
                        if what == 0:
                            pe.wait_ge(x_loaded, 32 if in_loop and g == NEXT else 16)
                        elif what == 5:
                            pe.wait_ge(ln_made, at(ln_made, "norm", g, "att4", half))
                        else:
                            pe.wait_ge(ln_made, at(ln_made, "norm", g, f"att{int(what[3]) + 1}", half))
                        src = (x_in if what == 0 else x_cur)[g % 2]
                        for fc in range(DC):
                            take_misc(fc, tr_lo, at(tr_lo, "tr", g, what, half) - 1 + fc)
                            for c in range(HC):
                                last = pe.transpose(misc[:, fc, c * P:(c + 1) * P],
                                                    src[:, half * HC + c, fc * P:(fc + 1) * P], ident_f[:, :])
                            last.then_inc(tr_ps, 1)

                    def project(g, a, c):
                        pe.wait_ge(tr_lo, at(tr_lo, "tr", g, a, c // HC))
                        take_misc(c % 2, wh_hi, at(wh_hi, "proj", g, a, c))
                        w = 0 if a == 0 else 1
                        for fc in range(DC):
                            for i, (y, wt) in enumerate([(yTh, wgh), (yTh, wgl), (yTl, wgh)]):
                                last = pe.matmul(misc[:, c % 2, 0:R], y[:, fc, c * P:(c + 1) * P], wt[:, w, fc, :],
                                                 start=(fc == 0 and i == 0), stop=(fc == DC - 1 and i == 2))
                        last.then_inc(wh_ps, 1)

                    def mean_of_r(g, a):
                        if a == 0:
                            pe.wait_ge(wh_lo, at(wh_lo, "proj", g, a, NC - 1))
                        else:
                            pe.wait_ge(r_hi, at(r_hi, "right", g, a, 1))
                            pe.wait_ge(r_lo, at(r_lo, "right", g, a, 1))
                        take_misc(0, mean_lo, at(mean_lo, "mean", g, a))
                        for c in range(NC):
                            for m in (rh, rl):
                                last = pe.matmul(misc[0:4, 0, 0:R], mean_w[:, :], m[g % 2][:, c, :],
                                                 start=(c == 0 and m is rh), stop=(c == NC - 1 and m is rl))
                        last.then_inc(mean_ps, 1)

                    def rows_of(g, a, half):
                        pe.wait_ge(sp_made, at(sp_made, "split", g, a, half))
                        take_misc(half, rows_made, at(rows_made, "rows", g, a, half))
                        for c in range(HC):
                            last = pe.matmul(misc[0:6, half, c * P:(c + 1) * P], sp[:, half * HC + c, :], ident_b[:, :],
                                             start=True, stop=True)
                        last.then_inc(rows_ps, 1)

                    def spread(name, g, a, half, pick, bank, done, made):
                        pe.wait_ge(rows_made, at(rows_made, "rows", g, a, half))
                        take_misc(bank, made, at(made, name, g, a, half))
                        pe.matmul(misc[:, bank, :], pick[:, :], rows[:, half * HALF:(half + 1) * HALF],
                                  start=True, stop=True).then_inc(done, 1)

                    def row_term(g, a):
                        pe.wait_ge(spr_made, at(spr_made, "row_term", g, a))
                        for b in range(2):
                            take_misc(b, rr_made, at(rr_made, "rr", g, a) - 1 + b)
                            for c in range(HC):
                                last = pe.matmul(misc[0:4, b, c * P:(c + 1) * P], spr[:, b * HC + c, :], ident_b[:, :],
                                                 start=True, stop=True)
                            last.then_inc(rr_ps, 1)

                    def step(name, g, *rest):
                        if name == "maskT":
                            transpose_mask(g, *rest)
                        if name == "tr":
                            transpose_half(g, *rest)
                        if name == "proj":
                            project(g, *rest)
                        if name == "mean":
                            mean_of_r(g, *rest)
                        if name == "rows":
                            rows_of(g, *rest)
                        if name == "t":
                            spread(name, g, *rest, pick_t, rest[1], t_ps, t_made)
                        if name == "s8":
                            spread(name, g, *rest, pick_s, 1 - rest[1], s8_ps, s8_made)
                        if name == "rr":
                            row_term(g, *rest)

                    def wait_bank(T):
                        if T >= 2:
                            if T - 2 in score_tiles:
                                pe.wait_ge(x_made, score_tiles.index(T - 2) + 1)
                            else:
                                pe.wait_ge(p_made, 2 * (T - 1))

                    def score_base(T, g, a, n):
                        j, half = where(a, n)
                        if not prepared(g, a):
                            if n == 0:
                                pe.wait_ge(rr_made, at(rr_made, "rr", g, a) - 1)
                                if a == 0:
                                    pe.wait_ge(maskT_made, at(maskT_made, "maskT", g, NC - 1))
                                if a == 1:
                                    pe.wait_ge(diag_made, at(diag_made, "diag", g))
                            if half == 1 and j == 0:
                                pe.wait_ge(rr_made, at(rr_made, "rr", g, a))
                        wait_bank(T)
                        pe.matmul(vu[:, T % 2, :], ident_big[:, :], maskT[g][:, j * N + half * HALF:j * N + (half + 1) * HALF],
                                  start=True, stop=False)
                        if a in (1, 2, 3) and j // HC == half:
                            k = j % HC
                            pe.matmul(vu[:, T % 2, k * P:(k + 1) * P], ident_pos[:, :], maskD[g][:, j, :], start=False, stop=False)
                        pe.matmul(vu[:, T % 2, :], pick_r[:, :], rowr[g][:, half * HALF:(half + 1) * HALF],
                                  start=False, stop=True).then_inc(v_ps, 1)

                    def wait_accumulator(T, half, c):
                        q = T // TILES
                        if half == 1:
                            pe.wait_ge(acc_free, at(acc_free, "take", *PASSES[q], 0) - 3 + c)
                        elif q > 0:
                            pe.wait_ge(*chunk_free(q - 1, c))

                    def aggregate(T, g, a, n):
                        j, half = where(a, n)
                        s = T % RING
                        if n == 0 and not prepared(g, a):
                            if a == 0:
                                pe.wait_ge(wh_lo, at(wh_lo, "proj", g, a, NC - 1))
                            else:
                                pe.wait_ge(r_hi, at(r_hi, "right", g, a, 1))
                                pe.wait_ge(r_lo, at(r_lo, "right", g, a, 1))
                        pe.wait_ge(p_made, 2 * (T + 1))
                        for c in range(HC):
                            if j == 0:
                                wait_accumulator(T, half, c)
                            for i, r in enumerate((rh, rl)):
                                pe.matmul(acc[:, c, 0:R], ph[:, s, c * P:(c + 1) * P], r[g][:, j, :],
                                          start=(j == 0 and i == 0), stop=False)
                        pe.wait_ge(pl_made, T + 1)
                        for c in range(HC):
                            last = pe.matmul(acc[:, c, 0:R], pl[:, s, c * P:(c + 1) * P], rh[g][:, j, :], start=False,
                                             stop=(j == NC - 1 and a not in (0, 4)))
                        if j == NC - 1 and a in (0, 4):
                            if half == 0 and not prepared(g, a):
                                pe.wait_ge(mean_lo, at(mean_lo, "mean", g, a))
                            for c in range(HC):
                                e_row = rowr[g][:, half * HALF + c * P:half * HALF + (c + 1) * P]
                                pe.matmul(acc[:, c, 0:R], e_row, mnh[g][:, :], start=False, stop=False)
                                last = pe.matmul(acc[:, c, 0:R], e_row, mnl[g][:, :], start=False, stop=True)
                        last.then_inc(tile_done, 1)

                    def aggregate_columns(T, g, n):
                        j, half = where(5, n)
                        s = T % RING
                        if half == 0:
                            pe.wait_ge(r3_made, at(r3_made, "scale", g, j))
                        pe.wait_ge(pl_made, T + 1)
                        for c in range(HC):
                            ic = half * HC + c
                            if j == 0 and ic % 2 == 0:
                                pe.wait_ge(*chunk_free(T // TILES - 1, ic // 2))
                            dst = acc[:, ic // 2, (ic % 2) * D:(ic % 2 + 1) * D]
                            for i, (p, r) in enumerate([(ph, rh), (ph, rl), (pl, rh)]):
                                last = pe.matmul(dst, p[:, s, c * P:(c + 1) * P], r[g][:, j, 0:D],
                                                 start=(j == 0 and i == 0 and ic % 2 == 0),
                                                 stop=(j == NC - 1 and i == 2), skip_group_check=True)
                        last.then_inc(tile_done, 1)

                    def hidden(T, g, l, n):
                        k, half = n % KC, n // KC
                        if n == 0:
                            pe.wait_ge(w_loaded, 64 * (l + 1))
                        if k == 0:
                            pe.wait_ge(tr_lo, at(tr_lo, "tr", g, f"ffn{l}", half))
                        wait_bank(T)
                        for fc in range(DC):
                            for i, (wt, y) in enumerate([(w1h, yTh), (w1h, yTl), (w1l, yTh)]):
                                last = pe.matmul(vu[:, T % 2, :], wt[:, fc, k * P:(k + 1) * P],
                                                 y[:, fc, half * HALF:(half + 1) * HALF],
                                                 start=(fc == 0 and i == 0), stop=(fc == DC - 1 and i == 2))
                        last.then_inc(v_ps, 1)

                    def contract(T, n):
                        k, half = n % KC, n // KC
                        s = T % RING
                        pe.wait_ge(p_made, 2 * (T + 1))
                        for c in range(HC):
                            if k == 0:
                                wait_accumulator(T, half, c)
                            for i, wt in enumerate((w2h, w2l)):
                                pe.matmul(acc[:, c, 0:D], ph[:, s, c * P:(c + 1) * P], wt[:, k, :],
                                          start=(k == 0 and i == 0), stop=False)
                        pe.wait_ge(pl_made, T + 1)
                        for c in range(HC):
                            last = pe.matmul(acc[:, c, 0:D], pl[:, s, c * P:(c + 1) * P], w2h[:, k, :],
                                             start=False, stop=(k == KC - 1))
                        last.then_inc(tile_done, 1)

                    begun = [0]

                    def tile(T, g, kind, i, n):
                        while begun[0] < ALL_TILES and begin_place(begun[0]) <= T:
                            B_ = begun[0]
                            bg, bkind, bi = PASSES[B_ // TILES]
                            (score_base if bkind == "att" else hidden)(B_, bg, bi, B_ % TILES)
                            begun[0] += 1
                        if kind == "ffn":
                            contract(T, n)
                        elif i == 5:
                            aggregate_columns(T, g, n)
                        else:
                            aggregate(T, g, i, n)

                    run("P", tile, step)

                @block.scalar
                def _(act):
                    def step(name, g, *rest):
                        G = g % 2
                        if name == "maskT":
                            c, = rest
                            for b in range(2):
                                act.wait_ge(maskT_ps, at(maskT_ps, "maskT", g, c) - 1 + b)
                                act.activation(u8(maskT[G]).rearrange("p (j n) -> p j n", j=NC)[:, b * HC:(b + 1) * HC, c * P:(c + 1) * P],
                                               misc[:, b, :].rearrange("p (j n) -> p j n", j=HC),
                                               ACT.Copy, scale=ONE8).then_inc(maskT_made, 1)
                        if name == "weight":
                            w, = rest
                            act.wait_ge(w_in[w % 2], 16 * (w // 2 + 1))
                            if w >= 2:
                                act.wait_ge(w_out[w % 2], 16 * (w // 2))
                            act.activation(wbuf[:, 2 * (w % 2), :], ffn_stage(w), ACT.Copy, scale=WSCALE).then_inc(w_hi, 1)
                        if name == "tr":
                            what, half = rest
                            for fc in range(DC):
                                act.wait_ge(tr_ps, at(tr_ps, "tr", g, what, half) - 1 + fc)
                                act.activation(yTh[:, fc, half * HALF:(half + 1) * HALF], misc[:, fc, :], ACT.Copy).then_inc(tr_hi, 1)
                        if name == "proj":
                            a, c = rest
                            act.wait_ge(wh_ps, at(wh_ps, "proj", g, a, c))
                            dst = xw[:, c, :] if a == 0 else x_in[G][:, c, :]
                            act.activation(st[G][:, :, c], misc[:, c % 2, D:R], ACT.Copy, scale=1.0 / WSCALE)
                            last = act.activation(dst, misc[:, c % 2, 0:D], ACT.Copy, scale=1.0 / WSCALE)
                            if a == 0:
                                last = act.activation(rh[G][:, c, 0:D], misc[:, c % 2, 0:D], ACT.Copy, scale=1.0 / WSCALE)
                            last.then_inc(wh_hi, 1)
                        if name == "right":
                            a, half = rest
                            src, norm = {1: (x_in, "att0"), 2: (x_cur, "ffn0"), 3: (x_cur, "ffn1"), 4: (x_cur, "outer")}[a]
                            act.wait_ge(ln_made, at(ln_made, "norm", g, norm, half))
                            act.activation(rh[G][:, half * HC:(half + 1) * HC, 0:D], nodes(src[G], half), ACT.Copy).then_inc(r_hi, 1)
                        if name == "rows":
                            a, half = rest
                            act.wait_ge(rows_ps, at(rows_ps, "rows", g, a, half))
                            act.activation(rows[:, half * HALF:(half + 1) * HALF], misc[0:6, half, :], ACT.Copy).then_inc(rows_made, 1)
                        if name == "t":
                            a, half = rest
                            act.wait_ge(t_ps, at(t_ps, "t", g, a, half))
                            act.activation(t_row[:, half * HALF:(half + 1) * HALF], misc[:, half, :], ACT.Copy, scale=TINY).then_inc(t_made, 1)
                        if name == "s8":
                            a, half = rest
                            hs = slice(half * HALF, (half + 1) * HALF)
                            act.wait_ge(s8_ps, at(s8_ps, "s8", g, a, half))
                            if a == 5:
                                act.activation(t_row[:, hs], misc[:, 1 - half, :], ACT.Copy, scale=TINY)
                            act.activation(s8_row[G][:, hs], misc[:, 1 - half, :], ACT.Copy).then_inc(s8_made, 1)
                        if name == "mean":
                            act.wait_ge(mean_ps, at(mean_ps, "mean", g, *rest))
                            act.activation(mnh[G][:, :], misc[0:4, 0, 0:R], ACT.Copy).then_inc(mean_hi, 1)
                        if name == "rr":
                            for b in range(2):
                                act.wait_ge(rr_ps, at(rr_ps, "rr", g, *rest) - 1 + b)
                                act.activation(rowr[G][:, b * HALF:(b + 1) * HALF], misc[0:4, b, :], ACT.Copy).then_inc(rr_made, 1)
                        if name == "elu":
                            act.wait_ge(elu_min, at(elu_min, "clip", g, *rest))
                            act.activation(e2[:, :, :], e2[:, :, :], ACT.Exp).then_inc(elu_exp, 1)
                        if name == "l3":
                            act.wait_ge(tile_done, TILES * (pass_index(g, "att", 5) + 1))
                            for b in range(4):
                                e = (e1, e2)[b // 2]
                                act.activation(flat(e[:, 2 * (b % 2):2 * (b % 2) + 2, :]), acc[:, b, :], ACT.Copy).then_inc(l3_copy, 1)

                    def tile(T, g, kind, a, n):
                        s = T % RING
                        if T >= RING:
                            act.wait_ge(tile_done, T - RING + 1)
                        if kind == "att":
                            A = score_tiles.index(T)
                            act.wait_ge(x_made, A + 1)
                            if a < 5:
                                t_j = st[g][:, 1, n % NC:n % NC + 1]
                                act.activation(p32[:, s, :], xt[:, A % RING, :], ACT.Exp, bias=t_j).then_inc(p_made, 1)
                                act.activation(ph[:, s, :], xt[:, A % RING, :], ACT.Exp, bias=t_j).then_inc(p_made, 1)
                            else:
                                j, half = n // 2, n % 2
                                bias, scale = cbias[g][:, j:j + 1], keep[g][:, j:j + 1]
                                act.activation(p32[:, s, :], xt[:, A % RING, :], ACT.Exp, bias=bias, scale=scale,
                                               accum_out=csum[g][:, j, half:half + 1]).then_inc(p_made, 1)
                                act.activation(ph[:, s, :], xt[:, A % RING, :], ACT.Exp, bias=bias, scale=scale).then_inc(p_made, 1)
                        else:
                            act.wait_ge(v_ps, T + 1)
                            bias = b1c[:, a, n % KC:n % KC + 1]
                            act.activation(p32[:, s, :], vu[:, T % 2, :], ACT.Gelu, bias=bias, scale=1.0 / WSCALE).then_inc(p_made, 1)
                            act.activation(ph[:, s, :], vu[:, T % 2, :], ACT.Gelu, bias=bias, scale=1.0 / WSCALE).then_inc(p_made, 1)

                    run("A", tile, step)

                @block.gpsimd
                def _(pool):
                    def step(name, g, *rest):
                        if name == "proj":
                            a, c = rest
                            pool.wait_ge(wh_hi, at(wh_hi, "proj", g, a, c))
                            pool.tensor_tensor(rl[g % 2][:, c, 0:D], xw[:, c, :], rh[g % 2][:, c, 0:D], ALU.subtract).then_inc(wh_lo, 1)
                            return
                        half = rest[-1]
                        cs = slice(half * HC, (half + 1) * HC)
                        if name == "norm":
                            pool.wait_ge(var_made, at(var_made, "stats", g, *rest))
                            pool.tensor_tensor(rstd[:, cs], vare[:, cs], neg_half[:, cs], ALU.pow).then_inc(rstd_made, 1)
                        if name == "right":
                            a = rest[0]
                            pool.wait_ge(r_hi, at(r_hi, "right", g, a, half))
                            pool.tensor_tensor(rl[g][:, cs, 0:D], nodes((x_in if a == 1 else x_cur)[g], half),
                                               rh[g][:, cs, 0:D], ALU.subtract).then_inc(r_lo, 1)
                        if name == "b2":
                            l = rest[0]
                            pool.wait_ge(tr_ps, at(tr_ps, "tr", g, f"ffn{l}", half))
                            pool.tensor_tensor(nodes(x_cur[g], half), nodes(x_cur[g], half),
                                               lnc[:, l, 2:3, :].broadcast_to([P, HC, D]), ALU.add).then_inc(hb_made, 1)

                    def tile(T, g, kind, a, n):
                        s = T % RING
                        pool.wait_ge(p_made, 2 * (T + 1))
                        pool.tensor_tensor(pl[:, s, :], p32[:, s, :], ph[:, s, :], ALU.subtract).then_inc(pl_made, 1)

                    run("G", tile, step)

                @block.vector
                def _(dve):
                    steps = [0]

                    def link(ins):
                        steps[0] += 1
                        ins.then_inc(dve_step, 1)
                        dve.wait_ge(dve_step, steps[0])

                    def lag(ins):
                        steps[0] += 1
                        ins.then_inc(dve_step, 1)
                        if steps[0] > 1:
                            dve.wait_ge(dve_step, steps[0] - 1)

                    def catch_up():
                        dve.wait_ge(dve_step, steps[0])

                    def make_mask(g, c):
                        e = at(mask_made, "mask", g, c)
                        dve.wait_ge(adj_loaded[c % 2], 16 * ((e - 1) // 2 + 1))
                        dve.tensor_scalar(u8(mask[g % 2])[:, c * N:(c + 1) * N], adj_sb[:, c % 2, :], 0, ONE8,
                                          ALU.is_le, ALU.mult).then_inc(mask_made, 1)

                    def take_diagonal(g):
                        if g == 1:
                            dve.wait_ge(maskT_made, at(maskT_made, "maskT", g, NC - 1))
                        for part, cs in diag_parts(u8(maskT[g])):
                            last = dve.tensor_tensor(maskD[g][:, cs, :].bitcast(U8), part,
                                                     ident_u8[:, :].unsqueeze(1).broadcast_to([P, cs.stop - cs.start, P]), ALU.mult)
                        last.then_inc(diag_made, 1)

                    def copy_transposed_low(g, what, half):
                        cs = slice(half * HALF, (half + 1) * HALF)
                        for fc in range(DC):
                            dve.wait_ge(tr_hi, at(tr_hi, "tr", g, what, half) - 1 + fc)
                            dve.tensor_tensor(yTl[:, fc, cs], misc[:, fc, :], yTh[:, fc, cs], ALU.subtract).then_inc(tr_lo, 1)

                    def score_columns(g, a, chunks):
                        src = x_in if a == 1 else x_cur
                        for c in chunks:
                            for k in range(2):
                                lag(dve.tensor_tensor_reduce(junk[:, k, 0:D], src[g][:, c, :], score_v[:, a - 1, k, :], 1.0, 0.0,
                                                             ALU.mult, ALU.add, st[g][:, k, c:c + 1]))
                        catch_up()

                    def split_scores(g, a, half):
                        G = g % 2
                        cs = slice(half * HC, (half + 1) * HC)
                        if a in (0, 5):
                            dve.wait_ge(wh_hi, at(wh_hi, "proj", g, a, (half + 1) * HC - 1))
                        if a in (1, 2, 3):
                            link(dve.tensor_scalar(st[G][:, 0, cs], st[G][:, 0, cs], ab[:, a - 1:a], None, ALU.add))
                        dve.tensor_scalar(c2[:, 0, cs], st[G][:, 0, cs], 1 - SLOPE, None, ALU.mult)
                        dve.tensor_scalar(n8t[G][:, cs], st[G][:, 1, cs], SLOPE - 1, None, ALU.mult)
                        link(dve.tensor_copy(c2[:, 1, cs], st[G][:, 1, cs]))
                        parts = sp[:, cs, :].rearrange("p c (v k) -> p v c k", v=2)
                        link(dve.tensor_copy(parts[:, :, :, 0], c2[:, :, cs]))
                        link(dve.tensor_tensor(res[:, :, cs], c2[:, :, cs], parts[:, :, :, 0], ALU.subtract))
                        link(dve.tensor_copy(parts[:, :, :, 1], res[:, :, cs]))
                        dve.tensor_tensor(parts[:, :, :, 2], res[:, :, cs], parts[:, :, :, 1], ALU.subtract).then_inc(sp_made, 1)

                    def maximum(g, a, half, chunks):
                        if a == 5:
                            dve.wait_ge(s8_made, at(s8_made, "s8", g, a, half))
                        else:
                            dve.wait_ge(t_made, at(t_made, "t", g, a, half))
                        m = u8((mask if a < 5 else maskT)[g % 2])
                        for c in chunks:
                            col = c * N + half * HALF
                            lag(dve.tensor_tensor_reduce(junk[:, c % 2, :], t_row[:, half * HALF:(half + 1) * HALF], m[:, col:col + HALF],
                                                         1.0, -3e38, ALU.subtract, ALU.max, hmax[:, half, c:c + 1]))

                    def split_row_term():
                        link(dve.tensor_copy(spr[:, :, 1], cterm[:, :]))
                        link(dve.tensor_tensor(resr[:, :], cterm[:, :], spr[:, :, 1], ALU.subtract))
                        link(dve.tensor_copy(spr[:, :, 2], resr[:, :]))
                        dve.tensor_tensor(spr[:, :, 3], resr[:, :], spr[:, :, 2], ALU.subtract).then_inc(spr_made, 1)

                    def leaky_maximum(G, a, other, scale):
                        catch_up()
                        link(dve.tensor_tensor(cmax[:, :], hmax[:, 0, :], hmax[:, 1, :], ALU.max))
                        if a in (1, 2, 3):
                            link(dve.scalar_tensor_tensor(out=cmax[:, :], in0=st[G][:, 1, :], scalar=TINY, in1=cmax[:, :],
                                                          op0=ALU.mult, op1=ALU.max))
                        link(dve.tensor_scalar(keep[G][:, :], cmax[:, :], -0.5, None, ALU.is_gt))
                        link(dve.scalar_tensor_tensor(out=cmax[:, :], in0=cmax[:, :], scalar=scale, in1=keep[G][:, :],
                                                      op0=ALU.mult, op1=ALU.mult))
                        link(dve.tensor_tensor(cmax[:, :], other, cmax[:, :], ALU.add))
                        link(dve.scalar_tensor_tensor(out=clk[:, :], in0=cmax[:, :], scalar=SLOPE, in1=cmax[:, :],
                                                      op0=ALU.mult, op1=ALU.max))

                    def make_row_term(g, a):
                        G = g % 2
                        s = st[G][:, 0, :]
                        if a == 5:
                            dve.memset(spr[:, :, 0], 0.0)
                            link(dve.tensor_scalar(cterm[:, :], s, SLOPE, None, ALU.mult))
                            split_row_term()
                            leaky_maximum(G, a, st[G][:, 1, :], 1 / TINY / (1 - SLOPE))
                            link(dve.tensor_tensor(clk[:, :], st[G][:, 1, :], clk[:, :], ALU.subtract))
                            link(dve.tensor_tensor(cbias[G][:, :], clk[:, :], keep[G][:, :], ALU.mult))
                            return
                        leaky_maximum(G, a, s, 1 / TINY)
                        dve.tensor_scalar(spr[:, :, 0], keep[G][:, :], 0.0, None, ALU.is_equal)
                        link(dve.scalar_tensor_tensor(out=cterm[:, :], in0=s, scalar=SLOPE, in1=clk[:, :],
                                                      op0=ALU.mult, op1=ALU.subtract))
                        split_row_term()

                    def norm_stats(g, name, half):
                        srcs = e1 if name in ("att0", "att4") else nodes(x_cur[g], half)
                        for c in range(HC):
                            last = dve.bn_stats(bst[:, c, :], srcs[:, c, :])
                        link(last)
                        for c in range(HC):
                            last = dve.bn_aggr(mv[:, half * HC + c, :], bst[:, c, :])
                        link(last)
                        cs = slice(half * HC, (half + 1) * HC)
                        dve.tensor_scalar(vare[:, cs], mv[:, cs, 1], EPS, None, ALU.add).then_inc(var_made, 1)

                    def norm_apply(g, name, half):
                        dve.wait_ge(rstd_made, at(rstd_made, "norm", g, name, half))
                        xs = nodes(x_cur[g], half)
                        if name in ("att0", "att4", "outer", "att5"):
                            src = e1 if name in ("att0", "att4") else xs
                            dst = nodes(x_in[g], half) if name == "att0" else xs
                            for c in range(HC):
                                k = half * HC + c
                                last = dve.tensor_scalar(dst[:, c, :], src[:, c, :], mv[:, k, 0:1], rstd[:, k:k + 1],
                                                         ALU.subtract, ALU.mult)
                        else:
                            l, k0 = (int(name[3]) - 1, 0) if name[:3] == "att" else (int(name[3]), 3)
                            for c in range(HC):
                                last = dve.scalar_tensor_tensor(out=xs[:, c, :], in0=xs[:, c, :], scalar=mv[:, half * HC + c, 0:1],
                                                                in1=lnc[:, l, k0, :], op0=ALU.subtract, op1=ALU.mult)
                            link(last)
                            for c in range(HC):
                                k = half * HC + c
                                last = dve.scalar_tensor_tensor(out=xs[:, c, :], in0=xs[:, c, :], scalar=rstd[:, k:k + 1],
                                                                in1=lnc[:, l, k0 + 1, :], op0=ALU.mult, op1=ALU.add)
                        last.then_inc(ln_made, 1)
                        dve.wait_ge(ln_made, at(ln_made, "norm", g, name, half))

                    def take(g, kind, i, half):
                        dve.wait_ge(tile_done, TILES * pass_index(g, kind, i) + 8 * (half + 1))
                        if kind == "att":
                            cs = slice(half * HC, (half + 1) * HC)
                            link(dve.reciprocal(rinv[:, cs], acc[:, :, D]))
                        else:
                            dve.wait_ge(hb_made, at(hb_made, "b2", g, i, half))
                        for c in range(HC):
                            k = half * HC + c
                            if kind == "ffn":
                                last = dve.scalar_tensor_tensor(out=x_cur[g][:, k, :], in0=acc[:, c, 0:D], scalar=1.0 / WSCALE,
                                                                in1=x_cur[g][:, k, :], op0=ALU.mult, op1=ALU.add)
                            elif i in (1, 2, 3):
                                last = dve.scalar_tensor_tensor(out=x_cur[g][:, k, :], in0=acc[:, c, 0:D], scalar=rinv[:, k:k + 1],
                                                                in1=(x_in if i == 1 else x_cur)[g][:, k, :],
                                                                op0=ALU.mult, op1=ALU.add)
                            else:
                                last = dve.tensor_scalar(e1[:, c, :], acc[:, c, 0:D], rinv[:, k:k + 1], None, ALU.mult)
                            last.then_inc(acc_free, 1)
                        dve.wait_ge(acc_free, at(acc_free, "take", g, kind, i, half))

                    def add_elu(g, a, half):
                        link(dve.scalar_tensor_tensor(out=flat(e1[:, :, :]), in0=flat(e1[:, :, :]), scalar=0.0,
                                                      in1=flat(nodes((x_in if a == 0 else x_cur)[g], half)), op0=ALU.max, op1=ALU.add))
                        dve.wait_ge(elu_exp, at(elu_exp, "elu", g, a, half))
                        link(dve.scalar_tensor_tensor(out=flat(e1[:, :, :]), in0=flat(e2[:, :, :]), scalar=-1.0,
                                                      in1=flat(e1[:, :, :]), op0=ALU.add, op1=ALU.add))

                    def scale_columns(g, j):
                        q = pass_index(g, "att", 5)
                        dve.wait_ge(p_made, 2 * (TILES * q + 2 * j + 2))
                        link(dve.tensor_tensor(rinv[:, j:j + 1], csum[g][:, j, 0:1], csum[g][:, j, 1:2], ALU.add))
                        link(dve.reciprocal(rinv[:, j:j + 1], rinv[:, j:j + 1]))
                        link(dve.tensor_scalar(rh[g][:, j, 0:D], x_in[g][:, j, :], rinv[:, j:j + 1], None, ALU.mult))
                        dve.scalar_tensor_tensor(out=rl[g][:, j, 0:D], in0=x_in[g][:, j, :], scalar=rinv[:, j:j + 1],
                                                 in1=rh[g][:, j, 0:D], op0=ALU.mult, op1=ALU.subtract).then_inc(r3_made, 1)

                    def step(name, g, *rest):
                        if name == "mask":
                            make_mask(g, *rest)
                        if name == "weight":
                            w, = rest
                            dve.wait_ge(w_hi, w + 1)
                            dve.scalar_tensor_tensor(out=wbuf[:, 2 * (w % 2) + 1, :], in0=ffn_stage(w), scalar=WSCALE,
                                                     in1=wbuf[:, 2 * (w % 2), :], op0=ALU.mult, op1=ALU.subtract).then_inc(w_lo, 1)
                        if name == "diag":
                            take_diagonal(g)
                        if name == "tr":
                            copy_transposed_low(g, *rest)
                        if name == "mean":
                            dve.wait_ge(mean_hi, at(mean_hi, "mean", g, *rest))
                            dve.tensor_tensor(mnl[g % 2][:, :], misc[0:4, 0, 0:R], mnh[g % 2][:, :], ALU.subtract).then_inc(mean_lo, 1)
                        if name == "cols":
                            score_columns(g, *rest)
                        if name == "split":
                            split_scores(g, *rest)
                        if name == "max":
                            maximum(g, *rest)
                        if name == "row_term":
                            make_row_term(g, *rest)
                        if name == "take":
                            take(g, *rest)
                        if name == "clip":
                            dve.tensor_scalar(flat(e2[:, :, :]), flat(e1[:, :, :]), 0.0, None, ALU.min).then_inc(elu_min, 1)
                        if name == "elu":
                            add_elu(g, *rest)
                        if name == "stats":
                            norm_stats(g, *rest)
                        if name == "norm":
                            norm_apply(g, *rest)
                        if name == "outer":
                            xs = flat(nodes(x_cur[g], rest[0]))
                            link(dve.tensor_tensor(xs, xs, flat(nodes(x_in[g], rest[0])), ALU.add))
                        if name == "scale":
                            scale_columns(g, *rest)
                        if name == "l3":
                            for half, e in enumerate((e1, e2)):
                                dve.wait_ge(l3_copy, at(l3_copy, "l3", g) - 2 + 2 * half)
                                link(dve.scalar_tensor_tensor(out=flat(e[:, :, :]), in0=flat(e[:, :, :]), scalar=SLOPE,
                                                              in1=flat(e[:, :, :]), op0=ALU.mult, op1=ALU.max))
                        if name == "l3_sum":
                            xs = flat(nodes(x_cur[g], rest[0]))
                            link(dve.tensor_tensor(xs, flat((e1, e2)[rest[0]][:, :, :]), xs, ALU.add))

                    def tile(T, g, kind, a, n):
                        if kind == "ffn":
                            return
                        A = score_tiles.index(T)
                        j, half = where(a, n)
                        dve.wait_ge(v_ps, T + 1)
                        if j == 0 and not prepared(g, a):
                            dve.wait_ge(s8_made, at(s8_made, "s8", g, a, half))
                        if A >= RING:
                            dve.wait_ge(p_made, 2 * (score_tiles[A - RING] + 1))
                        dve.scalar_tensor_tensor(out=xt[:, A % RING, :], in0=s8_row[g][:, half * HALF:(half + 1) * HALF],
                                                 scalar=n8t[g][:, j:j + 1], in1=vu[:, T % 2, :],
                                                 op0=ALU.max, op1=ALU.add).then_inc(x_made, 1)

                    run("D", tile, step)

            clear_semaphores()

        emit(False, 0, 0)
        with nc.Fori(0, B // 2) as pair_no:
            emit(True, pair_no, (pair_no + 1) % (B // 2) if B > 2 else 0)


_INS = ["x", "adj", "L0_gnn_W", "L0_gnn_a", "L1_gnn_attn_w", "L1_gnn_attn_b", "L1_gnn_W1", "L1_gnn_b1", "L1_gnn_W2",
        "L1_gnn_b2", "L1_gnn_g1", "L1_gnn_beta1", "L1_gnn_g2", "L1_gnn_beta2", "L2_gnn_W_fc", "L2_gnn_W_attn",
        "L3_gnn_W", "L3_gnn_a"]


def kernel(**inputs):
    import numpy as _np
    import concourse.bacc as _bacc
    from concourse import mybir as _mybir
    from concourse.bass_utils import run_bass_kernel_spmd as _run

    nc = _bacc.Bacc("TRN2", target_bir_lowering=False, num_devices=1)
    arrays, args = {}, []
    for name in _INS:
        a = _np.ascontiguousarray(inputs[name])
        arrays[f"in_{name}_dram"] = a
        args.append(nc.dram_tensor(f"in_{name}_dram", a.shape, _mybir.dt.from_np(a.dtype), kind="ExternalInput").ap())
    shape = inputs["x"].shape
    o = nc.dram_tensor("out_0_dram", shape, _mybir.dt.float32, kind="ExternalOutput").ap()
    build(nc, *args, o)
    r = _run(nc, [arrays], core_ids=[0])
    return r.results[0]["out_0_dram"]
```
